# Optimizing a Trainium2 kernel written in Bass

```python
import numpy as np
import jax
import jax.numpy as jnp

def _softmax(x, axis=-1):
    return jax.nn.softmax(x, axis=axis)

def _gelu(x):
    return jax.nn.gelu(x, approximate=True)

def _silu(x):
    return jax.nn.silu(x)

def _sigmoid(x):
    return jax.nn.sigmoid(x)

def _layernorm(x, axis=-1, eps=1e-05):
    m = jnp.mean(x, axis=axis, keepdims=True)
    v = jnp.var(x, axis=axis, keepdims=True)
    return (x - m) / jnp.sqrt(v + eps)

def _scatter_add(tgt, idx, src, axis=0):
    return tgt.at[idx].add(src)

def _segment_sum(src, seg, n):
    return jax.ops.segment_sum(src, seg, n)
kernel_name = 'mk_adaln_d2_jaxref_r8_0ff88a'

def setup_inputs(seed: int=0):
    np.random.seed(seed)
    _w = jnp.asarray

    def _L0_attn_setup():
        import jax, jax.numpy as jnp
        import numpy as np
        import math
        B, S, H = (1, 256, 512)
        NH, NKV, HD = (32, 8, 128)
        GS = 128
        WBITS = 4
        ZERO = float(2 ** (WBITS - 1))
        THETA = 10000.0

        def _dequant_matmul(x, qw, scales):
            w = (qw.astype(jnp.float32) - ZERO) * jnp.repeat(scales, GS, axis=0)
            return x @ w

        def _rope_tables(seq_len, dtype):
            inv_freq = 1.0 / THETA ** (jnp.arange(0, HD, 2, dtype=jnp.float32) / HD)
            freqs = jnp.arange(seq_len, dtype=jnp.float32)[:, None] * inv_freq
            emb = jnp.concatenate([freqs, freqs], axis=-1)
            return (jnp.cos(emb).astype(dtype), jnp.sin(emb).astype(dtype))

        def _rotate_half(x):
            x1, x2 = jnp.split(x, 2, axis=-1)
            return jnp.concatenate([-x2, x1], axis=-1)

        def _apply_rope(x, cos, sin):
            return x * cos[None, None] + _rotate_half(x) * sin[None, None]
        key = jax.random.key(seed)
        ks = jax.random.split(key, 9)
        small = lambda k, shp: jax.random.uniform(k, shp, jnp.float32) * 0.01 + 0.001
        return {'hidden_states': jax.random.normal(ks[0], (B, S, H), jnp.float32), 'scales_q': small(ks[1], (H // GS, NH * HD)), 'scales_k': small(ks[2], (H // GS, NKV * HD)), 'scales_v': small(ks[3], (H // GS, NKV * HD)), 'scales_o': small(ks[4], (NH * HD // GS, H)), 'qw_q': jax.random.randint(ks[5], (H, NH * HD), 0, 2 ** WBITS, jnp.int32), 'qw_k': jax.random.randint(ks[6], (H, NKV * HD), 0, 2 ** WBITS, jnp.int32), 'qw_v': jax.random.randint(ks[7], (H, NKV * HD), 0, 2 ** WBITS, jnp.int32), 'qw_o': jax.random.randint(ks[8], (NH * HD, H), 0, 2 ** WBITS, jnp.int32)}
    _L0_attn_in = _L0_attn_setup()

    def _L0_ffn_setup():
        import jax, jax.numpy as jnp
        import numpy as np
        D_MODEL = 512
        D_HIDDEN = 1376
        RANK = 16
        BATCH, SEQ = (2, 256)

        def _matmul_lora(x, w, a, b, scale=1.0):
            out = jnp.einsum('bsd,hd->bsh', x, w)
            out = out + jnp.einsum('bsr,hr->bsh', jnp.einsum('bsd,rd->bsr', x, a), b) * scale
            return out
        key = jax.random.key(seed)
        ks = jax.random.split(key, 10)
        s = 0.02
        return {'x': jax.random.normal(ks[0], (BATCH, SEQ, D_MODEL), jnp.float32), 'gate_w': jax.random.normal(ks[1], (D_HIDDEN, D_MODEL), jnp.float32) * s, 'up_w': jax.random.normal(ks[2], (D_HIDDEN, D_MODEL), jnp.float32) * s, 'down_w': jax.random.normal(ks[3], (D_MODEL, D_HIDDEN), jnp.float32) * s, 'gate_a': jax.random.normal(ks[4], (RANK, D_MODEL), jnp.float32) * s, 'gate_b': jax.random.normal(ks[5], (D_HIDDEN, RANK), jnp.float32) * s, 'up_a': jax.random.normal(ks[6], (RANK, D_MODEL), jnp.float32) * s, 'up_b': jax.random.normal(ks[7], (D_HIDDEN, RANK), jnp.float32) * s, 'down_a': jax.random.normal(ks[8], (RANK, D_HIDDEN), jnp.float32) * s, 'down_b': jax.random.normal(ks[9], (D_MODEL, RANK), jnp.float32) * s}
    _L0_ffn_in = _L0_ffn_setup()
    _L0_c = _w((lambda *s: np.random.randn(*s).astype(np.float32) * 0.05)(1, 512))
    _L0_wmod = _w((lambda *s: np.random.randn(*s).astype(np.float32) * 0.05)(512, 6 * 512) * 512 ** (-0.5))

    def _L1_attn_setup():
        import jax, jax.numpy as jnp
        import numpy as np
        import math
        D_MODEL = 512
        NUM_HEADS = 32
        NUM_KV_HEADS = 8
        HEAD_DIM = D_MODEL // NUM_HEADS
        GROUP = NUM_HEADS // NUM_KV_HEADS
        SEQ_LEN = 256
        BATCH = 2
        ROPE_THETA = 10000.0

        def apply_rope(x, start_pos=0):
            b, h, s, hd = x.shape
            inv_freq = 1.0 / ROPE_THETA ** (jnp.arange(0, hd, 2, dtype=jnp.float32) / hd)
            pos = jnp.arange(start_pos, start_pos + s, dtype=jnp.float32)
            ang = pos[:, None] * inv_freq[None, :]
            cos = jnp.cos(ang).astype(x.dtype)
            sin = jnp.sin(ang).astype(x.dtype)
            xr = x[..., 0::2]
            xi = x[..., 1::2]
            out_r = xr * cos - xi * sin
            out_i = xr * sin + xi * cos
            return jnp.stack([out_r, out_i], axis=-1).reshape(b, h, s, hd)
        key = jax.random.key(seed)
        ks = jax.random.split(key, 5)
        qkv_dim = HEAD_DIM * (NUM_HEADS + 2 * NUM_KV_HEADS)
        scale = 1.0 / math.sqrt(D_MODEL)
        return {'x': jax.random.normal(ks[0], (BATCH, SEQ_LEN, D_MODEL), jnp.float32), 'w_qkv': jax.random.normal(ks[1], (qkv_dim, D_MODEL), jnp.float32) * scale, 'b_qkv': jax.random.normal(ks[2], (qkv_dim,), jnp.float32) * 0.01, 'w_o': jax.random.normal(ks[3], (D_MODEL, D_MODEL), jnp.float32) * scale, 'b_o': jax.random.normal(ks[4], (D_MODEL,), jnp.float32) * 0.01}
    _L1_attn_in = _L1_attn_setup()

    def _L1_ffn_setup():
        import jax, jax.numpy as jnp
        import numpy as np
        N_EXPERTS = 28
        TOP_K = 2
        RANK = 8
        LORA_ALPHA = 16
        SCALING = LORA_ALPHA / RANK
        TEMP = 1.0
        key = jax.random.key(seed)
        ks = jax.random.split(key, 5)
        B, S, D_IN, D_OUT = (4, 256, 512, 512)
        x = jax.random.normal(ks[0], (B, S, D_IN), dtype=jnp.float32)
        base_W = jax.random.normal(ks[1], (D_OUT, D_IN), dtype=jnp.float32) * (1.0 / np.sqrt(D_IN))
        gate_W = jax.random.normal(ks[2], (N_EXPERTS, D_IN), dtype=jnp.float32) * (1.0 / np.sqrt(D_IN))
        lora_A = jax.random.normal(ks[3], (N_EXPERTS, RANK, D_IN), dtype=jnp.float32) * (1.0 / np.sqrt(D_IN))
        lora_B = jax.random.normal(ks[4], (N_EXPERTS, D_OUT, RANK), dtype=jnp.float32) * 0.01
        return {'x': x, 'base_W': base_W, 'gate_W': gate_W, 'lora_A': lora_A, 'lora_B': lora_B}
    _L1_ffn_in = _L1_ffn_setup()
    _L1_c = _w((lambda *s: np.random.randn(*s).astype(np.float32) * 0.05)(1, 512))
    _L1_wmod = _w((lambda *s: np.random.randn(*s).astype(np.float32) * 0.05)(512, 6 * 512) * 512 ** (-0.5))
    _d = {'L0_attn_hidden_states': _L0_attn_in['hidden_states'], 'L0_attn_scales_q': _L0_attn_in['scales_q'], 'L0_attn_scales_k': _L0_attn_in['scales_k'], 'L0_attn_scales_v': _L0_attn_in['scales_v'], 'L0_attn_scales_o': _L0_attn_in['scales_o'], 'L0_attn_qw_q': _L0_attn_in['qw_q'], 'L0_attn_qw_k': _L0_attn_in['qw_k'], 'L0_attn_qw_v': _L0_attn_in['qw_v'], 'L0_attn_qw_o': _L0_attn_in['qw_o'], 'L0_ffn_gate_w': _L0_ffn_in['gate_w'], 'L0_ffn_up_w': _L0_ffn_in['up_w'], 'L0_ffn_down_w': _L0_ffn_in['down_w'], 'L0_ffn_gate_a': _L0_ffn_in['gate_a'], 'L0_ffn_gate_b': _L0_ffn_in['gate_b'], 'L0_ffn_up_a': _L0_ffn_in['up_a'], 'L0_ffn_up_b': _L0_ffn_in['up_b'], 'L0_ffn_down_a': _L0_ffn_in['down_a'], 'L0_ffn_down_b': _L0_ffn_in['down_b'], 'L0_c': _L0_c, 'L0_wmod': _L0_wmod, 'L1_attn_w_qkv': _L1_attn_in['w_qkv'], 'L1_attn_b_qkv': _L1_attn_in['b_qkv'], 'L1_attn_w_o': _L1_attn_in['w_o'], 'L1_attn_b_o': _L1_attn_in['b_o'], 'L1_ffn_base_W': _L1_ffn_in['base_W'], 'L1_ffn_gate_W': _L1_ffn_in['gate_W'], 'L1_ffn_lora_A': _L1_ffn_in['lora_A'], 'L1_ffn_lora_B': _L1_ffn_in['lora_B'], 'L1_c': _L1_c, 'L1_wmod': _L1_wmod}
    _x0 = _d['L0_attn_hidden_states']
    _d['L0_attn_hidden_states'] = jax.random.normal(jax.random.fold_in(jax.random.key(seed), 1), (1, 1024, 512), dtype=_x0.dtype)
    del _x0
    return _d

def reference(L0_attn_hidden_states, L0_attn_scales_q, L0_attn_scales_k, L0_attn_scales_v, L0_attn_scales_o, L0_attn_qw_q, L0_attn_qw_k, L0_attn_qw_v, L0_attn_qw_o, L0_ffn_gate_w, L0_ffn_up_w, L0_ffn_down_w, L0_ffn_gate_a, L0_ffn_gate_b, L0_ffn_up_a, L0_ffn_up_b, L0_ffn_down_a, L0_ffn_down_b, L0_c, L0_wmod, L1_attn_w_qkv, L1_attn_b_qkv, L1_attn_w_o, L1_attn_b_o, L1_ffn_base_W, L1_ffn_gate_W, L1_ffn_lora_A, L1_ffn_lora_B, L1_c, L1_wmod):

    def _L0_attn_ref(hidden_states, scales_q, scales_k, scales_v, scales_o, qw_q, qw_k, qw_v, qw_o):
        import jax, jax.numpy as jnp
        import numpy as np
        import math
        B, S, H = (1, 256, 512)
        NH, NKV, HD = (32, 8, 128)
        GS = 128
        WBITS = 4
        ZERO = float(2 ** (WBITS - 1))
        THETA = 10000.0

        def _dequant_matmul(x, qw, scales):
            w = (qw.astype(jnp.float32) - ZERO) * jnp.repeat(scales, GS, axis=0)
            return x @ w

        def _rope_tables(seq_len, dtype):
            inv_freq = 1.0 / THETA ** (jnp.arange(0, HD, 2, dtype=jnp.float32) / HD)
            freqs = jnp.arange(seq_len, dtype=jnp.float32)[:, None] * inv_freq
            emb = jnp.concatenate([freqs, freqs], axis=-1)
            return (jnp.cos(emb).astype(dtype), jnp.sin(emb).astype(dtype))

        def _rotate_half(x):
            x1, x2 = jnp.split(x, 2, axis=-1)
            return jnp.concatenate([-x2, x1], axis=-1)

        def _apply_rope(x, cos, sin):
            return x * cos[None, None] + _rotate_half(x) * sin[None, None]
        b, s, _ = hidden_states.shape
        q = _dequant_matmul(hidden_states, qw_q, scales_q).reshape(b, s, NH, HD).transpose(0, 2, 1, 3)
        k = _dequant_matmul(hidden_states, qw_k, scales_k).reshape(b, s, NKV, HD).transpose(0, 2, 1, 3)
        v = _dequant_matmul(hidden_states, qw_v, scales_v).reshape(b, s, NKV, HD).transpose(0, 2, 1, 3)
        cos, sin = _rope_tables(s, hidden_states.dtype)
        q = _apply_rope(q, cos, sin)
        k = _apply_rope(k, cos, sin)
        rep = NH // NKV
        k = jnp.repeat(k, rep, axis=1)
        v = jnp.repeat(v, rep, axis=1)
        scores = jnp.einsum('bhqd,bhkd->bhqk', q, k) / math.sqrt(HD)
        causal = jnp.tril(jnp.ones((s, s), dtype=bool))
        scores = jnp.where(causal[None, None], scores, jnp.finfo(scores.dtype).min)
        attn = jax.nn.softmax(scores.astype(jnp.float32), axis=-1).astype(q.dtype)
        ctx = jnp.einsum('bhqk,bhkd->bhqd', attn, v)
        ctx = ctx.transpose(0, 2, 1, 3).reshape(b, s, NH * HD)
        return _dequant_matmul(ctx, qw_o, scales_o)

    def _L0_ffn_ref(x, gate_w, up_w, down_w, gate_a, gate_b, up_a, up_b, down_a, down_b):
        import jax, jax.numpy as jnp
        import numpy as np
        D_MODEL = 512
        D_HIDDEN = 1376
        RANK = 16
        BATCH, SEQ = (2, 256)

        def _matmul_lora(x, w, a, b, scale=1.0):
            out = jnp.einsum('bsd,hd->bsh', x, w)
            out = out + jnp.einsum('bsr,hr->bsh', jnp.einsum('bsd,rd->bsr', x, a), b) * scale
            return out
        gate = _matmul_lora(x, gate_w, gate_a, gate_b)
        up = _matmul_lora(x, up_w, up_a, up_b)
        hidden = jax.nn.silu(gate) * up
        out = _matmul_lora(hidden, down_w, down_a, down_b)
        return out

    def _L1_attn_ref(x, w_qkv, b_qkv, w_o, b_o):
        import jax, jax.numpy as jnp
        import numpy as np
        import math
        D_MODEL = 512
        NUM_HEADS = 32
        NUM_KV_HEADS = 8
        HEAD_DIM = D_MODEL // NUM_HEADS
        GROUP = NUM_HEADS // NUM_KV_HEADS
        SEQ_LEN = 256
        BATCH = 2
        ROPE_THETA = 10000.0

        def apply_rope(x, start_pos=0):
            b, h, s, hd = x.shape
            inv_freq = 1.0 / ROPE_THETA ** (jnp.arange(0, hd, 2, dtype=jnp.float32) / hd)
            pos = jnp.arange(start_pos, start_pos + s, dtype=jnp.float32)
            ang = pos[:, None] * inv_freq[None, :]
            cos = jnp.cos(ang).astype(x.dtype)
            sin = jnp.sin(ang).astype(x.dtype)
            xr = x[..., 0::2]
            xi = x[..., 1::2]
            out_r = xr * cos - xi * sin
            out_i = xr * sin + xi * cos
            return jnp.stack([out_r, out_i], axis=-1).reshape(b, h, s, hd)
        bs, seq_len, d_model = x.shape
        qkv = x @ w_qkv.T + b_qkv
        q_dim = NUM_HEADS * HEAD_DIM
        kv_dim = NUM_KV_HEADS * HEAD_DIM
        q, k, v = jnp.split(qkv, [q_dim, q_dim + kv_dim], axis=-1)
        q = q.reshape(bs, seq_len, NUM_HEADS, HEAD_DIM).transpose(0, 2, 1, 3)
        k = k.reshape(bs, seq_len, NUM_KV_HEADS, HEAD_DIM).transpose(0, 2, 1, 3)
        v = v.reshape(bs, seq_len, NUM_KV_HEADS, HEAD_DIM).transpose(0, 2, 1, 3)
        q = apply_rope(q, 0)
        k = apply_rope(k, 0)
        k = jnp.repeat(k, GROUP, axis=1)
        v = jnp.repeat(v, GROUP, axis=1)
        scores = jnp.einsum('bhqd,bhkd->bhqk', q, k) / math.sqrt(HEAD_DIM)
        causal = jnp.tril(jnp.ones((seq_len, seq_len), dtype=bool))
        scores = jnp.where(causal[None, None, :, :], scores, jnp.float32(-1e+20))
        attn = jax.nn.softmax(scores, axis=-1)
        out = jnp.einsum('bhqk,bhkd->bhqd', attn, v)
        out = out.transpose(0, 2, 1, 3).reshape(bs, seq_len, d_model)
        return out @ w_o.T + b_o

    def _L1_ffn_ref(x, base_W, gate_W, lora_A, lora_B):
        import jax, jax.numpy as jnp
        import numpy as np
        N_EXPERTS = 28
        TOP_K = 2
        RANK = 8
        LORA_ALPHA = 16
        SCALING = LORA_ALPHA / RANK
        TEMP = 1.0
        B, S, D_in = x.shape
        xf = x.reshape(B * S, D_in)
        base = xf @ base_W.T
        logits = xf @ gate_W.T
        top_vals, top_idx = jax.lax.top_k(logits, TOP_K)
        top_probs = jax.nn.softmax(top_vals / TEMP, axis=-1)
        N = xf.shape[0]
        gate_full = jnp.zeros((N, N_EXPERTS), dtype=xf.dtype).at[jnp.arange(N)[:, None], top_idx].add(top_probs)
        h = jnp.einsum('nd,erd->ner', xf, lora_A)
        h = h * (gate_full * SCALING)[:, :, None]
        lora_out = jnp.einsum('ner,eor->no', h, lora_B)
        out = base + lora_out
        return out.reshape(B, S, -1)
    x = L0_attn_hidden_states
    mod = (_silu(L0_c) @ L0_wmod).reshape(L0_c.shape[0], 6, 1, -1)
    sa, ca, ga, sb, cb, gb = (mod[:, 0], mod[:, 1], mod[:, 2], mod[:, 3], mod[:, 4], mod[:, 5])
    ga = (2 * (ga >= 0) - 1) * jnp.maximum(jnp.abs(ga), 0.25)
    gb = (2 * (gb >= 0) - 1) * jnp.maximum(jnp.abs(gb), 0.25)
    h = _layernorm(x, axis=-1) * (1 + ca) + sa
    x = x + ga * _L0_attn_ref(h, L0_attn_scales_q, L0_attn_scales_k, L0_attn_scales_v, L0_attn_scales_o, L0_attn_qw_q, L0_attn_qw_k, L0_attn_qw_v, L0_attn_qw_o)
    h = _layernorm(x, axis=-1) * (1 + cb) + sb
    x = x + gb * _L0_ffn_ref(h, L0_ffn_gate_w, L0_ffn_up_w, L0_ffn_down_w, L0_ffn_gate_a, L0_ffn_gate_b, L0_ffn_up_a, L0_ffn_up_b, L0_ffn_down_a, L0_ffn_down_b)
    mod = (_silu(L1_c) @ L1_wmod).reshape(L1_c.shape[0], 6, 1, -1)
    sa, ca, ga, sb, cb, gb = (mod[:, 0], mod[:, 1], mod[:, 2], mod[:, 3], mod[:, 4], mod[:, 5])
    ga = (2 * (ga >= 0) - 1) * jnp.maximum(jnp.abs(ga), 0.25)
    gb = (2 * (gb >= 0) - 1) * jnp.maximum(jnp.abs(gb), 0.25)
    h = _layernorm(x, axis=-1) * (1 + ca) + sa
    x = x + ga * _L1_attn_ref(h, L1_attn_w_qkv, L1_attn_b_qkv, L1_attn_w_o, L1_attn_b_o)
    h = _layernorm(x, axis=-1) * (1 + cb) + sb
    x = x + gb * _L1_ffn_ref(h, L1_ffn_base_W, L1_ffn_gate_W, L1_ffn_lora_A, L1_ffn_lora_B)
    return x

_drawn_inputs = setup_inputs


def setup_inputs(seed=0):
    import zlib

    import numpy as np

    out = dict(_drawn_inputs(seed))
    spreads = {}
    factors = {'L0_attn_scales_q': 8.0,
     'L0_attn_scales_k': 8.0,
     'L0_attn_scales_v': 3.783,
     'L0_attn_scales_o': 4.028,
     'L0_ffn_gate_a': 8.0,
     'L0_ffn_gate_b': 8.0,
     'L0_ffn_up_a': 8.0,
     'L0_ffn_up_b': 8.0,
     'L0_ffn_down_a': 8.0,
     'L0_ffn_down_b': 8.0,
     'L1_attn_b_qkv': 64.0,
     'L1_attn_b_o': 200.0,
     'L1_ffn_gate_W': 5.945,
     'L1_ffn_lora_A': 5.644,
     'L1_ffn_lora_B': 5.721,
     'L1_attn_w_qkv': 7.501,
     'L1_attn_w_o': 7.345,
     'L1_ffn_base_W': 3.369}
    for name, (base, spread) in spreads.items():
        noise = np.random.default_rng([zlib.crc32(name.encode()), seed]).standard_normal(out[name].shape)
        drawn = base * np.exp(spread * noise) if base else spread * noise
        out[name] = jnp.asarray(drawn.astype(out[name].dtype))
    for name, factor in factors.items():
        out[name] = (out[name] * factor).astype(out[name].dtype)
    return out
```

```python
import concourse.bass as bass
from concourse import mybir
from contextlib import ExitStack

F32 = mybir.dt.float32
F32R = mybir.dt.float32r
BF16 = mybir.dt.bfloat16
I32 = mybir.dt.int32
U32 = mybir.dt.uint32
ALU = mybir.AluOpType
ACT = mybir.ActivationFunctionType
AX = mybir.AxisListType

P = 128
S = 1024
D = 512
NT = S // P
KT = D // P
HALF = 512
NHALF = S // HALF
TPH = HALF // P
LN_EPS = 1e-5
MASKED = -3.0e38

NH0, NKV0, HD0 = 32, 8, 128
REP0 = NH0 // NKV0
ZERO_POINT = 8.0
SCALE0 = float(HD0) ** -0.5

HID = 1376
RANK0 = 16
NF = (HID + P - 1) // P
HID_LAST = HID - (NF - 1) * P

NH1, NKV1, HD1 = 32, 8, 16
REP1 = NH1 // NKV1
QK1 = (NH1 + NKV1) * HD1
QKV1 = (NH1 + 2 * NKV1) * HD1
SCALE1 = float(HD1) ** -0.5

NE, RANK1 = 28, 8
ER = NE * RANK1
LORA_SCALE = 2.0


class Turns:

    def __init__(self, sem, names):
        self.sem, self.names, self.n = sem, list(names), len(names)

    def open(self, engine, done_before_loop=0):
        engine.sem_inc(self.sem, self.n - done_before_loop)

    def now(self, turn, name):
        return self.sem, turn * self.n + self.n + self.names.index(name) + 1

    def last(self, turn, name):
        return self.sem, turn * self.n + self.names.index(name) + 1


class Memory:
    pass


def split_products(pe, out, lhs, rhs, start, stop):
    (lhs_hi, lhs_lo), (rhs_hi, rhs_lo) = lhs, rhs
    pe.matmul(out, lhs_lo, rhs_hi, start=start, stop=False)
    pe.matmul(out, lhs_hi, rhs_lo, start=False, stop=False)
    return pe.matmul(out, lhs_hi, rhs_hi, start=False, stop=stop)


def constants_phase(nc, mem):
    with ExitStack() as ctx:
        cleared = mem.semaphores.enter_context(nc.semaphore("const_cleared"))
        drawn = mem.semaphores.enter_context(nc.semaphore("const_drawn"))
        block = ctx.enter_context(nc.Block())

        @block.gpsimd
        def _(pool):
            pool.memset(mem.ident[:, :], 0.0).then_inc(cleared, 1)
            pool.memset(mem.causal[:, :], 0.0).then_inc(cleared, 1)
            pool.memset(mem.ones[:, :], 1.0).then_inc(cleared, 1)
            pool.wait_ge(cleared, 3)
            pool.affine_select(out=mem.ident[:, :], in_=mem.ident[:, :], compare_op=ALU.not_equal,
                               fill=1.0, base=0, pattern=[[-1, P]], channel_multiplier=1).then_inc(drawn, 1)
            pool.affine_select(out=mem.causal[:, :], in_=mem.causal[:, :], compare_op=ALU.is_ge,
                               fill=MASKED, base=0, pattern=[[-1, P]], channel_multiplier=1).then_inc(drawn, 1)
            pool.wait_ge(drawn, 1)
            pool.tensor_copy(mem.ident_bf[:, :], mem.ident[:, :]).then_inc(drawn, 1)
            pool.wait_ge(drawn, 3)


def modulation_phase(nc, mem, x, c_dram, wmod_dram):
    SLOTS = 4
    CHUNKS = 6
    with ExitStack() as ctx:
        sem = lambda name: mem.semaphores.enter_context(nc.semaphore(name))
        sb = lambda name, shape, dt=F32: ctx.enter_context(nc.sbuf_tensor(name, shape, dt))
        c_col = sb("mod_c", [P, 2, KT])
        silu_c = sb("mod_silu", [P, 2, KT])
        silu_rows = sb("mod_silu_rows", [P, 2 * KT, P])
        w = sb("mod_w", [P, SLOTS, KT, D])
        sign = sb("mod_sign", [P, D])
        size = sb("mod_size", [P, D])
        diag = sb("mod_diag", [P, P])
        x_in, c_in = sem("x_in"), sem("mod_c_in")
        w_in = [sem(f"mod_w_in{s}") for s in range(SLOTS)]
        silu_done, rows_done = sem("mod_silu_done"), sem("mod_rows_done")
        product_done, taken, step = sem("mod_product"), sem("mod_taken"), sem("mod_step")
        bank = mem.bank
        block = ctx.enter_context(nc.Block())

        @block.sync
        def _(sp):
            for layer in range(2):
                sp.dma_start(c_col[:, layer, :], c_dram[layer][0, :].rearrange("(k p) -> p k", p=P),
                             allow_slow_non_contiguous=True).then_inc(c_in, 16)
            for j in range(2 * CHUNKS):
                if j == 2:
                    sp.dma_start(mem.x[:, :, :], x[0].rearrange("(t p) d -> p t d", p=P)).then_inc(x_in, 16)
                if j >= SLOTS:
                    sp.wait_ge(product_done, j - SLOTS + 1)
                n = j % CHUNKS
                sp.dma_start(w[:, j % SLOTS, :, :],
                             wmod_dram[j // CHUNKS][:, n * D:(n + 1) * D].rearrange("(k p) n -> p k n", p=P)
                             ).then_inc(w_in[j % SLOTS], 16)
            sp.wait_ge(x_in, 16)

        @block.scalar
        def _(act):
            act.wait_ge(c_in, 32)
            nc.scalar.activation(silu_c[:, :, :], c_col[:, :, :], ACT.Silu).then_inc(silu_done, 1)

        @block.tensor
        def _(pe):
            pe.wait_ge(rows_done, 2 * KT)
            for j in range(2 * CHUNKS):
                pe.wait_ge(w_in[j % SLOTS], 16 * (j // SLOTS + 1))
                if j >= 2:
                    pe.wait_ge(taken, j - 1)
                for k in range(KT):
                    last = nc.tensor.matmul(bank[j % 2][:, :], silu_rows[:, (j // CHUNKS) * KT + k, :],
                                            w[:, j % SLOTS, k, :], start=(k == 0), stop=(k == KT - 1))
                last.then_inc(product_done, 1)

        @block.vector
        def _(dve):
            steps = 0
            dve.wait_ge(silu_done, 1)
            for layer in range(2):
                for k in range(KT):
                    nc.vector.tensor_scalar(silu_rows[:, layer * KT + k, :], mem.ones[:, :],
                                            silu_c[:, layer, k:k + 1], None, ALU.mult).then_inc(rows_done, 1)
            for j in range(2 * CHUNKS):
                layer, n = j // CHUNKS, j % CHUNKS
                product = bank[j % 2]
                dve.wait_ge(product_done, j + 1)
                if n in (2, 5):
                    gate = mem.gate[:, 2 * layer + (n == 5), :]
                    nc.vector.tensor_scalar(sign[:, :], product[:, :], 0.0, 2.0, ALU.is_ge, ALU.mult).then_inc(step, 1)
                    nc.vector.tensor_scalar(size[:, :], product[:, :], -1.0, 0.25, ALU.mult, ALU.max).then_inc(step, 1)
                    steps += 2
                    dve.wait_ge(step, steps)
                    nc.vector.tensor_tensor(size[:, :], size[:, :], product[:, :], ALU.max).then_inc(step, 1)
                    steps += 1
                    dve.wait_ge(step, steps)
                    nc.vector.scalar_tensor_tensor(out=gate, in0=sign[:, :], scalar=-1.0, in1=size[:, :],
                                                   op0=ALU.add, op1=ALU.mult).then_inc(taken, 1)
                    dve.wait_ge(taken, j + 1)
                else:
                    column = mem.column[:, 4 * layer + {0: 0, 1: 1, 3: 2, 4: 3}[n], :]
                    for k in range(KT):
                        done = nc.vector.scalar_tensor_tensor(
                            out=diag[:, :], in0=product[:, k * P:(k + 1) * P], scalar=1.0, in1=mem.ident[:, :],
                            op0=ALU.mult, op1=ALU.mult, accum_out=column[:, k:k + 1])
                        if k < KT - 1 or n in (1, 4):
                            done.then_inc(step, 1)
                            steps += 1
                            dve.wait_ge(step, steps)
                    if n in (1, 4):
                        done = nc.vector.tensor_scalar(column, column, 1.0, None, ALU.add)
                    done.then_inc(taken, 1)
                    dve.wait_ge(taken, j + 1)


class Counted:

    def __init__(self, sem, total):
        self.sem, self.total = sem, total

    def after(self, run, k):
        return self.sem, run * self.total + k


def layernorm_counts(nc, mem):
    pieces = NHALF * KT
    totals = {"stats_done": NT, "moments": NT, "y_done": 1, "root_done": 1, "rstd_done": 5, "normed_done": NT,
              "turned": pieces, "modulated": pieces, "hi_done": pieces, "lo_done": pieces}
    return [Counted(mem.semaphores.enter_context(nc.semaphore("ln_" + name)), n) for name, n in totals.items()]


def layernorm_phase(nc, mem, run, scale_col, shift_col):
    with ExitStack() as ctx:
        sb = lambda name, shape, dt=F32: ctx.enter_context(nc.sbuf_tensor(f"ln{run}_{name}", shape, dt))
        stats = sb("stats", [P, NT, 6])
        mean_var = sb("mean_var", [P, NT, 2])
        y, std, root = sb("y", [P, NT]), sb("std", [P, NT]), sb("root", [P, NT])
        newton, rstd = sb("newton", [P, NT]), sb("rstd", [P, NT])
        normed = sb("normed", [P, NT, D])
        h = sb("h", [P, 4, HALF])
        (stats_done, moments, y_done, root_done, rstd_done, normed_done,
         turned, modulated, hi_done, lo_done) = mem.layernorm_counts
        pieces = [(half, k) for half in range(NHALF) for k in range(KT)]
        block = ctx.enter_context(nc.Block())

        @block.vector
        def _(dve):
            for t in range(NT):
                nc.vector.bn_stats(stats[:, t, :], mem.x[:, t, :]).then_inc(stats_done.sem, 1)
            for t in range(NT):
                dve.wait_ge(*stats_done.after(run, t + 1))
                nc.vector.bn_aggr(mean_var[:, t, :], stats[:, t, :]).then_inc(moments.sem, 1)
            dve.wait_ge(*moments.after(run, NT))
            nc.vector.tensor_scalar(y[:, :], mean_var[:, :, 1], LN_EPS, None, ALU.add).then_inc(y_done.sem, 1)
            dve.wait_ge(*root_done.after(run, 1))
            nc.vector.reciprocal(root[:, :], std[:, :]).then_inc(rstd_done.sem, 1)
            dve.wait_ge(*rstd_done.after(run, 1))
            nc.vector.tensor_tensor(newton[:, :], root[:, :], root[:, :], ALU.mult).then_inc(rstd_done.sem, 1)
            dve.wait_ge(*rstd_done.after(run, 2))
            nc.vector.tensor_tensor(newton[:, :], newton[:, :], y[:, :], ALU.mult).then_inc(rstd_done.sem, 1)
            dve.wait_ge(*rstd_done.after(run, 3))
            nc.vector.tensor_scalar(newton[:, :], newton[:, :], -0.5, 1.5, ALU.mult, ALU.add).then_inc(rstd_done.sem, 1)
            dve.wait_ge(*rstd_done.after(run, 4))
            nc.vector.tensor_tensor(rstd[:, :], root[:, :], newton[:, :], ALU.mult).then_inc(rstd_done.sem, 1)
            dve.wait_ge(*rstd_done.after(run, 5))
            for t in range(NT):
                nc.vector.tensor_scalar(normed[:, t, :], mem.x[:, t, :], mean_var[:, t, 0:1], rstd[:, t:t + 1],
                                        ALU.subtract, ALU.mult).then_inc(normed_done.sem, 1)

            def low(i):
                half, k = pieces[i]
                dve.wait_ge(*hi_done.after(run, i + 1))
                nc.vector.tensor_tensor(mem.hT[1][:, k, half * HALF:(half + 1) * HALF], h[:, i % 4, :],
                                        mem.hT[0][:, k, half * HALF:(half + 1) * HALF].bitcast(F32),
                                        ALU.subtract).then_inc(lo_done.sem, 1)

            for i, (half, k) in enumerate(pieces):
                dve.wait_ge(*modulated.after(run, i + 1))
                nc.vector.tensor_copy(mem.hT[0][:, k, half * HALF:(half + 1) * HALF], h[:, i % 4, :]).then_inc(hi_done.sem, 1)
                if i:
                    low(i - 1)
            low(len(pieces) - 1)

        @block.tensor
        def _(pe):
            for i, (half, k) in enumerate(pieces):
                pe.wait_ge(*normed_done.after(run, TPH * (half + 1)))
                if i >= 4:
                    pe.wait_ge(*modulated.after(run, i - 3))
                for t in range(TPH):
                    last = nc.tensor.transpose(mem.bank[i % 4][:, t * P:(t + 1) * P],
                                               normed[:, half * TPH + t, k * P:(k + 1) * P], mem.ident[:, :])
                last.then_inc(turned.sem, 1)

        @block.scalar
        def _(act):
            act.wait_ge(*y_done.after(run, 1))
            nc.scalar.activation(std[:, :], y[:, :], ACT.Sqrt).then_inc(root_done.sem, 1)
            for i, (half, k) in enumerate(pieces):
                act.wait_ge(*turned.after(run, i + 1))
                if i >= 4:
                    act.wait_ge(*lo_done.after(run, i - 3))
                nc.scalar.activation(h[:, i % 4, :], mem.bank[i % 4][:, :], ACT.Identity,
                                     scale=scale_col[:, k:k + 1], bias=shift_col[:, k:k + 1]).then_inc(modulated.sem, 1)


def layer0_attention_phase(nc, mem, rope_dram, qw, scales):
    HH = HD0 // 2
    heads, tiles, halves = range(REP0), range(NT), range(NHALF)
    use6 = [("k", 0), ("v", 0), ("q", 0, 0)]
    use7 = [("k", 1), ("v", 1), ("q", 0, 1)]
    for h in heads:
        for i in tiles:
            if h > 0:
                use6.append(("o", h - 1, i))
            if i % TPH == TPH - 1:
                use7.append(("pv", h, i // TPH))
            if h < REP0 - 1 and i in (4, 6):
                use6.append(("q", h + 1, (i - 4) // 2))
    for t in tiles:
        (use6, use7)[t % 2].append(("o", REP0 - 1, t))
    pieces = [(h, i, c) for h in heads for i in tiles for c in range(i // TPH + 1)]
    weights = [("o", 0)] + [(w, h) for h in range(1, REP0) for w in ("q", "o")] + [("k", 0), ("v", 0), ("q", 0)]
    AHEAD, RING = 3, 5
    roped_halves = [("k", b) for b in halves] + [("q", h, b) for h in heads for b in halves]
    with ExitStack() as ctx:
        sem = lambda name: mem.semaphores.enter_context(nc.semaphore("a0_" + name))
        turns = lambda name, names: Turns(sem(name), names)
        sb = lambda name, shape, dt=F32: ctx.enter_context(nc.sbuf_tensor("a0_" + name, shape, dt))
        pair = lambda name, shape: (sb(name + "_hi", shape, F32R), sb(name + "_lo", shape, F32R))
        rope = sb("rope", [P, 2, S])
        raw, scale = sb("raw", [P, RING, D], I32), sb("scale", [P, RING, D])
        shifted, weight, with_gate = sb("shifted", [P, 2, D]), sb("weight", [P, D]), sb("with_gate", [P, D])
        nothing = sb("nothing", [P, D])
        wkv = pair("wkv", [P, 2, KT, HD0])
        wq, wo = pair("wq", [P, 2, KT, HD0]), pair("wo", [P, 2, D])
        kT, qT = pair("kT", [P, S]), pair("qT", [P, 2, S])
        vT, v = sb("vT", [P, S]), sb("v", [P, NT, HD0])
        by_cos, by_sin, roped = sb("by_cos", [P, HALF]), sb("by_sin", [P, HALF]), sb("roped", [P, HALF])
        probs = sb("probs", [P, 2, S])
        probsT = [sb(f"probsT{b}", [P, TPH * (b + 1), HALF]) for b in halves]
        ctxT = pair("ctxT", [P, 2, S])
        neg_max, row_sum, row_inv = sb("neg_max", [P, 2, NT]), sb("row_sum", [P, 2, NT]), sb("row_inv", [P, 2, NT])

        rope_in, filled = sem("rope_in"), sem("filled")
        raw_in = [sem(f"raw_in{s}") for s in range(RING)]
        shift_done, scaled = turns("shift_done", weights), turns("scaled", weights)
        gated, hi_made, made = turns("gated", heads), turns("hi_made", weights), turns("made", weights)
        full6, full7 = turns("full6", use6), turns("full7", use7)
        v_turned = turns("v_turned", halves)
        scored = turns("scored", [(h, i) for h in heads for i in tiles])
        turned = turns("turned", pieces)
        free6, free7 = turns("free6", use6), turns("free7", use7)
        rope_mul, rope_sum = turns("rope_mul", roped_halves), turns("rope_sum", roped_halves)
        rope_hi = turns("rope_hi", roped_halves)
        v_done = turns("v_done", halves)
        maxed = turns("maxed", [(h, i) for h in heads for i in tiles])
        inverted = turns("inverted", heads)
        exped = turns("exped", [(h, i) for h in heads for i in tiles])
        turned_out = turns("turned_out", pieces)
        ctx_hi = turns("ctx_hi", [(h, b) for h in heads for b in halves])
        score = mem.bank_pair
        turn_bank = mem.bank[4:6]
        bank6, bank7 = mem.bank[6], mem.bank[7]
        full = lambda use: full6 if use in use6 else full7
        free = lambda use: free6 if use in use6 else free7
        bank = lambda use: bank6 if use in use6 else bank7
        half = lambda b: slice(b * HALF, (b + 1) * HALF)
        tile = lambda i: slice(i * P, (i + 1) * P)

        def former(use):
            uses = use6 if use in use6 else use7
            return uses[uses.index(use) - 1]

        def wait_free(pe, g, use):
            uses = use6 if use in use6 else use7
            counter = free(use)
            pe.wait_ge(*(counter.now(g, former(use)) if uses.index(use) else counter.last(g, former(use))))

        def loaded(g, n):
            s = n % RING
            return raw_in[s], g * 64 + 32 * (n // RING) + 32 + (32 if s >= len(weights) - AHEAD - RING else 0)

        def steps_before(counter, g, n, back):
            return counter.now(g, weights[n - back]) if n >= back else counter.last(g, weights[n - back])

        block = ctx.enter_context(nc.Block())

        @block.sync
        def _(sp):
            def load(n, group):
                name, h = weights[n]
                slot = n % RING
                if name == "o":
                    rows = bass.ds(group * (REP0 * HD0) + h * HD0, HD0)
                    sp.dma_start(raw[:, slot, :], qw["o"][rows, :]).then_inc(raw_in[slot], 16)
                    sp.dma_start(scale[:, slot, :], scales["o"][bass.ds(group * REP0 + h, 1), :].broadcast_to([P, D])
                                 ).then_inc(raw_in[slot], 16)
                    return
                cols = bass.ds(group * (REP0 * HD0) + h * HD0, HD0) if name == "q" else bass.ds(group * HD0, HD0)
                sp.dma_start(raw[:, slot, :].rearrange("p (k n) -> p k n", k=KT),
                             qw[name][:, cols].rearrange("(k p) n -> p k n", p=P)).then_inc(raw_in[slot], 16)
                sp.dma_start(scale[:, slot, :].rearrange("p (k n) -> p k n", k=KT),
                             scales[name][:, cols].unsqueeze(0).broadcast_to([P, KT, HD0])).then_inc(raw_in[slot], 16)

            AT_HOME = len(weights) - AHEAD
            for n in range(AT_HOME, len(weights)):
                load(n, 0)
            sp.dma_start(rope[:, :, :], rope_dram.rearrange("a p s -> p a s")).then_inc(rope_in, 16)
            with sp.Fori(0, NKV0) as g:
                for n in range(len(weights)):
                    sp.wait_ge(*steps_before(scaled, g, n, RING))
                    load(n, g if n < AT_HOME else (g + 1) % NKV0)

        @block.gpsimd
        def _(pool):
            pool.memset(nothing[:, :], 0.0).then_inc(filled, 1)
            for counter in (scaled, hi_made, made):
                counter.open(pool, AHEAD)
            gated.open(pool)
            pool.wait_ge(filled, 1)

            def make(g, n, prologue=False):
                name, h = key = weights[n]
                done = lambda counter: counter.last(0, key) if prologue else counter.now(g, key)
                hi, lo = ((part[:, n - (len(weights) - AHEAD), :, :] for part in wkv) if name in "kv" else
                          (part[:, h % 2] for part in (wq if name == "q" else wo)))
                flat = lambda a: a.rearrange("p k n -> p (k n)") if len(a.shape) == 3 else a
                pool.wait_ge(*done(shift_done))
                pool.tensor_tensor(weight[:, :], shifted[:, n % 2, :], scale[:, n % RING, :], ALU.mult).then_inc(scaled.sem, 1)
                pool.wait_ge(*done(scaled))
                whole = weight
                if name == "o":
                    pool.tensor_tensor(with_gate[:, :], weight[:, :], mem.gate[:, 0, :], ALU.mult).then_inc(gated.sem, 1)
                    pool.wait_ge(*gated.now(g, h))
                    whole = with_gate
                if not prologue:
                    if name in "kv":
                        pool.wait_ge(*full7.now(g, (name, 1)))
                    else:
                        use = (name, (h - 2) % REP0) + ((1,) if name == "q" else (NT - 1,))
                        this_turn = h >= 2 or key == ("q", 0)
                        pool.wait_ge(*(full(use).now(g, use) if this_turn else full(use).last(g, use)))
                pool.tensor_tensor(flat(hi), whole[:, :], nothing[:, :], ALU.add).then_inc(hi_made.sem, 1)
                pool.wait_ge(*done(hi_made))
                pool.tensor_tensor(flat(lo), whole[:, :], flat(hi).bitcast(F32), ALU.subtract).then_inc(made.sem, 1)
                pool.wait_ge(*done(made))

            for n in range(len(weights) - AHEAD, len(weights)):
                make(0, n, prologue=True)
            with pool.Fori(0, NKV0) as g:
                for n in range(len(weights)):
                    make(g, n)

        @block.tensor
        def _(pe):
            for counter in (full6, full7, v_turned, scored, turned):
                counter.open(pe)
            pe.wait_ge(rope_in, 16)
            with pe.Fori(0, NKV0) as g:
                def project(use, w, slot, b):
                    wait_free(pe, g, use)
                    for k in range(KT):
                        last = split_products(nc.tensor, bank(use)[:, :], [part[:, slot, k, :] for part in w],
                                              [part[:, k, half(b)] for part in mem.hT], k == 0, k == KT - 1)
                    last.then_inc(full(use).sem, 1)

                def scores(h, i):
                    if i % TPH == 0:
                        pe.wait_ge(*free(("q", h, i // TPH)).now(g, ("q", h, i // TPH)))
                        if h == 0:
                            pe.wait_ge(*free(("k", i // TPH)).now(g, ("k", i // TPH)))
                    before = (h, i - 2) if i >= 2 else (h - 1, NT + i - 2)
                    pe.wait_ge(*(exped.now(g, before) if before[0] >= 0 else
                                 exped.last(g, (REP0 - 1, NT + i - 2))))
                    out = score[i % 2]
                    for c in range(i // TPH + 1):
                        keys = slice(c * HALF, min((c + 1) * HALF, (i + 1) * P))
                        diagonal = c == i // TPH
                        last = split_products(nc.tensor, out[:, keys], [part[:, h % 2, tile(i)] for part in qT],
                                              [part[:, keys] for part in kT], True, not diagonal)
                        if diagonal:
                            last = nc.tensor.matmul(out[:, tile(i)], mem.ident_bf[:, :], mem.causal[:, :],
                                                    start=False, stop=True)
                    last.then_inc(scored.sem, 1)

                def turn(h, i):
                    pe.wait_ge(*exped.now(g, (h, i)))
                    for c in range(i // TPH + 1):
                        n = pieces.index((h, i, c))
                        pe.wait_ge(*(turned_out.now(g, pieces[n - 2]) if n >= 2 else
                                     turned_out.last(g, pieces[n - 2])))
                        for j in range(c * TPH, min((c + 1) * TPH, i + 1)):
                            last = nc.tensor.transpose(turn_bank[n % 2][:, tile(j - c * TPH)], probs[:, i % 2, tile(j)],
                                                       mem.ident[:, :])
                        last.then_inc(turned.sem, 1)

                def values(h, b):
                    use = ("pv", h, b)
                    wait_free(pe, g, use)
                    if b == 0 and h == 0:
                        pe.wait_ge(*v_done.now(g, 1))
                    pe.wait_ge(*turned_out.now(g, (h, TPH * (b + 1) - 1, b)))
                    keys = TPH * (b + 1)
                    for j in range(keys):
                        first = max(0, j - TPH * b) * P
                        last = nc.tensor.matmul(bank7[:, first:HALF], v[:, j, :], probsT[b][:, j, first:HALF],
                                                start=(j == 0), stop=(j == keys - 1))
                    last.then_inc(full7.sem, 1)

                def output(h, t):
                    use = ("o", h, t)
                    wait_free(pe, g, use)
                    if t == 0:
                        pe.wait_ge(*free7.now(g, ("pv", h, 1)))
                        pe.wait_ge(*made.now(g, ("o", h)))
                    split_products(nc.tensor, bank(use)[:, :], [part[:, h % 2, tile(t)] for part in ctxT],
                                   [part[:, h % 2, :] for part in wo], True, True).then_inc(full(use).sem, 1)

                for n, name in enumerate(("k", "v")):
                    pe.wait_ge(*made.last(g, (name, 0)))
                    for b in halves:
                        project((name, b), wkv, n, b)
                pe.wait_ge(*made.last(g, ("q", 0)))
                for b in halves:
                    project(("q", 0, b), wq, 0, b)
                for b in halves:
                    pe.wait_ge(*free(("v", b)).now(g, ("v", b)))
                    p0 = pieces[len(pieces) - 2 + b]
                    pe.wait_ge(*turned_out.last(g, p0))
                    for t in range(TPH):
                        last = nc.tensor.transpose(turn_bank[b][:, tile(t)], vT[:, tile(b * TPH + t)], mem.ident[:, :])
                    last.then_inc(v_turned.sem, 1)
                for b in halves:
                    pe.wait_ge(*v_done.now(g, b))
                for h in heads:
                    scores(h, 0)
                    for i in tiles:
                        if i < NT - 1:
                            scores(h, i + 1)
                        if h > 0:
                            output(h - 1, i)
                        turn(h, i)
                        if i % TPH == TPH - 1:
                            values(h, i // TPH)
                        if h < REP0 - 1 and i in (4, 6):
                            if i == 4:
                                pe.wait_ge(*made.now(g, ("q", h + 1)))
                            project(("q", h + 1, (i - 4) // 2), wq, (h + 1) % 2, (i - 4) // 2)
                for t in tiles:
                    output(REP0 - 1, t)

        @block.vector
        def _(dve):
            for counter in (free6, free7, rope_mul, rope_sum, rope_hi, v_done, maxed, inverted):
                counter.open(dve)
            dve.wait_ge(rope_in, 16)
            with dve.Fori(0, NKV0) as g:
                def turn_half(name, scale, out):
                    b = name[-1]
                    b_in = bank(name)
                    dve.wait_ge(*full(name).now(g, name))
                    nc.vector.scalar_tensor_tensor(out=by_cos[:, :], in0=b_in[:, :], scalar=scale,
                                                   in1=rope[:, 0, half(b)], op0=ALU.mult, op1=ALU.mult)
                    for to, of in ((slice(0, HH), slice(HH, HD0)), (slice(HH, HD0), slice(0, HH))):
                        last = nc.vector.scalar_tensor_tensor(out=by_sin[to, :], in0=b_in[of, :], scalar=scale,
                                                              in1=rope[to, 1, half(b)], op0=ALU.mult, op1=ALU.mult)
                    last.then_inc(rope_mul.sem, 1)
                    dve.wait_ge(*rope_mul.now(g, name))
                    nc.vector.tensor_tensor(roped[:, :], by_cos[:, :], by_sin[:, :], ALU.add).then_inc(rope_sum.sem, 1)
                    dve.wait_ge(*rope_sum.now(g, name))
                    nc.vector.tensor_copy(out[0], roped[:, :]).then_inc(rope_hi.sem, 1)
                    dve.wait_ge(*rope_hi.now(g, name))
                    nc.vector.tensor_tensor(out[1], roped[:, :], out[0].bitcast(F32), ALU.subtract
                                            ).then_inc(free(name).sem, 1)

                def maximum(h, i):
                    dve.wait_ge(*scored.now(g, (h, i)))
                    nc.vector.reduce_max(neg_max[:, h % 2, i:i + 1], score[i % 2][:, 0:(i + 1) * P], AX.X,
                                         negate=True).then_inc(maxed.sem, 1)

                def add_output(h, t):
                    use = ("o", h, t)
                    dve.wait_ge(*full(use).now(g, use))
                    nc.vector.scalar_tensor_tensor(out=mem.x[:, t, :], in0=bank(use)[:, :],
                                                   scalar=row_inv[:, h % 2, t:t + 1], in1=mem.x[:, t, :],
                                                   op0=ALU.mult, op1=ALU.add).then_inc(free(use).sem, 1)

                def split_values(h, b):
                    dve.wait_ge(*ctx_hi.now(g, (h, b)))
                    nc.vector.tensor_tensor(ctxT[1][:, h % 2, half(b)], bank7[:, :],
                                            ctxT[0][:, h % 2, half(b)].bitcast(F32), ALU.subtract
                                            ).then_inc(free7.sem, 1)

                for b in halves:
                    turn_half(("k", b), 1.0, [part[:, half(b)] for part in kT])
                for b in halves:
                    dve.wait_ge(*full(("v", b)).now(g, ("v", b)))
                    nc.vector.tensor_copy(vT[:, half(b)], bank(("v", b))[:, :]).then_inc(free(("v", b)).sem, 1)
                for b in halves:
                    turn_half(("q", 0, b), SCALE0, [part[:, 0, half(b)] for part in qT])
                for b in halves:
                    dve.wait_ge(*v_turned.now(g, b))
                    nc.vector.tensor_copy(v[:, b * TPH:(b + 1) * TPH, :],
                                          turn_bank[b][:, :].rearrange("p (t d) -> p t d", t=TPH)
                                          ).then_inc(v_done.sem, 1)
                for h in heads:
                    maximum(h, 0)
                    for i in tiles:
                        if i < NT - 1:
                            maximum(h, i + 1)
                        if h > 0:
                            add_output(h - 1, i)
                        if i == TPH:
                            split_values(h, 0)
                        if h < REP0 - 1 and i in (4, 6):
                            turn_half(("q", h + 1, (i - 4) // 2), SCALE0,
                                      [part[:, (h + 1) % 2, half((i - 4) // 2)] for part in qT])
                    split_values(h, 1)
                    nc.vector.reciprocal(row_inv[:, h % 2, :], row_sum[:, h % 2, :]).then_inc(inverted.sem, 1)
                    dve.wait_ge(*inverted.now(g, h))
                for t in tiles:
                    add_output(REP0 - 1, t)

        @block.scalar
        def _(act):
            for counter in (exped, turned_out, ctx_hi):
                counter.open(act)
            shift_done.open(act, AHEAD)

            def shift(g, n):
                nc.scalar.activation(shifted[:, n % 2, :], raw[:, n % RING, :], ACT.Copy, bias=-ZERO_POINT
                                     ).then_inc(shift_done.sem, 1)

            for n in range(len(weights) - AHEAD, len(weights)):
                act.wait_ge(raw_in[n % RING], 32)
                if n == len(weights) - 1:
                    act.wait_ge(*scaled.last(0, weights[n - 2]))
                shift(0, n)
            with act.Fori(0, NKV0) as g:
                def shift_next(n):
                    act.wait_ge(*loaded(g, n))
                    act.wait_ge(*steps_before(scaled, g, n, 2))
                    shift(g, n)

                def exponential(h, i):
                    act.wait_ge(*maxed.now(g, (h, i)))
                    if i == 0:
                        act.wait_ge(*(inverted.now(g, h - 2) if h >= 2 else inverted.last(g, h - 2 + REP0)))
                    nc.scalar.activation(probs[:, i % 2, 0:(i + 1) * P], score[i % 2][:, 0:(i + 1) * P], ACT.Exp,
                                         bias=neg_max[:, h % 2, i:i + 1],
                                         accum_out=row_sum[:, h % 2, i:i + 1]).then_inc(exped.sem, 1)

                def take_turned(h, i):
                    b = i // TPH
                    if i % TPH == 0:
                        act.wait_ge(*(full7.now(g, ("pv", h - 1, b)) if h else full7.last(g, ("pv", REP0 - 1, b))))
                    for c in range(b + 1):
                        n = pieces.index((h, i, c))
                        act.wait_ge(*turned.now(g, (h, i, c)))
                        keys = min(TPH, i + 1 - c * TPH)
                        nc.scalar.copy(probsT[b][:, c * TPH:c * TPH + keys, tile(i % TPH)],
                                       turn_bank[n % 2][:, 0:keys * P].rearrange("p (j q) -> p j q", j=keys)
                                       ).then_inc(turned_out.sem, 1)

                def high_values(h, b):
                    act.wait_ge(*full7.now(g, ("pv", h, b)))
                    nc.scalar.copy(ctxT[0][:, h % 2, half(b)], bank7[:, :]).then_inc(ctx_hi.sem, 1)

                n = 0
                for h in heads:
                    exponential(h, 0)
                    for i in tiles:
                        if i < NT - 1:
                            exponential(h, i + 1)
                        take_turned(h, i)
                        if i in (0, 2, 4) and n < (4, 6, 8, 10)[h]:
                            shift_next(n)
                            n += 1
                        if i == TPH:
                            high_values(h, 0)
                    high_values(h, 1)


def layer0_ffn_phase(nc, mem, w):
    slots = range(2)
    kts = range(KT)
    with ExitStack() as ctx:
        sem = lambda name: mem.semaphores.enter_context(nc.semaphore("f0_" + name))
        turns = lambda name, names: Turns(sem(name), names)
        sb = lambda name, shape, dt=F32: ctx.enter_context(nc.sbuf_tensor("f0_" + name, shape, dt))
        pair = lambda name, shape: (sb(name + "_hi", shape, F32R), sb(name + "_lo", shape, F32R))
        raw = sb("raw", [P, 2, 3, D])
        raw_b = sb("raw_b", [P, 2, 2, RANK0])
        low_a = sb("low_a", [RANK0, 2, D])
        down_a = sb("down_a", [RANK0, 2, P])
        down_b, down_bT = sb("down_b", [P, KT, RANK0]), sb("down_bT", [RANK0, D])
        low_bT = sb("low_bT", [RANK0, 2, 2, P])
        wT = pair("wT", [P, 2, 2, KT, P])
        downT = pair("downT", [P, NF, D])
        down_full = sb("down_full", [P, D])
        hidden = sb("hidden", [P, NF, S])
        act_t = pair("act_t", [P, 2, NF, P])

        low_in, w_in = sem("low_in"), [sem(f"w_in{s}") for s in slots]
        bT_turned, wT_turned, projected = turns("bT_turned", slots), turns("wT_turned", [(s, m) for s in slots for m in (2, 0, 1)]), turns("projected", slots)
        down_bT_turned, down_bT_out = sem("down_bT_turned"), sem("down_bT_out")
        bT_out, w_hi, silu_done = turns("bT_out", slots), turns("w_hi", [(s, m) for s in slots for m in range(2)]), turns("silu_done", slots)
        w_split, down_gated = turns("w_split", [(s, m) for s in slots for m in (2, 0, 1)]), turns("down_gated", slots)
        down_hi, hidden_done = turns("down_hi", slots), turns("hidden_done", slots)
        cleared, act_hi, act_split, produced, added = sem("cleared"), sem("act_hi"), sem("act_split"), sem("produced"), sem("added")
        wT_bank, small_bank = mem.bank[0:3], mem.bank[3]
        out_pair = [mem.bank_pair4(0), mem.bank_pair4(1)]
        half = lambda b: slice(b * HALF, (b + 1) * HALF)
        LAST = NF - 1
        rows_of = lambda f: HID_LAST if isinstance(f, int) and f == LAST else P
        block = ctx.enter_context(nc.Block())

        def tiles_in_turn(g):
            return [(s, g * 2 + s) for s in slots] if not isinstance(g, int) or g < LAST // 2 else [(0, LAST)]

        @block.sync
        def _(sp):
            sp.dma_start(low_a[:, 0, :], w["gate_a"][:, :]).then_inc(low_in, 16)
            sp.dma_start(low_a[:, 1, :], w["up_a"][:, :]).then_inc(low_in, 16)
            sp.dma_start(down_b[:, :, :], w["down_b"].rearrange("(k p) r -> p k r", p=P)).then_inc(low_in, 16)

            def load(g):
                for s, f in tiles_in_turn(g):
                    r = rows_of(f)
                    rows = bass.ds(f * P, r)
                    sp.wait_ge(*wT_turned.last(g, (s, 1)))
                    sp.dma_start(raw[:r, s, 0, :], w["gate_w"][rows, :]).then_inc(w_in[s], 16)
                    sp.dma_start(raw[:r, s, 1, :], w["up_w"][rows, :]).then_inc(w_in[s], 16)
                    sp.dma_start(raw[:, s, 2, 0:KT * r].rearrange("p (k n) -> p k n", k=KT),
                                 w["down_w"][:, rows].rearrange("(k p) n -> p k n", p=P)).then_inc(w_in[s], 16)
                    sp.dma_start(raw_b[:r, s, 0, :], w["gate_b"][rows, :]).then_inc(w_in[s], 16)
                    sp.dma_start(raw_b[:r, s, 1, :], w["up_b"][rows, :]).then_inc(w_in[s], 16)
                    sp.dma_start(down_a[:, s, 0:r], w["down_a"][:, rows]).then_inc(w_in[s], 16)

            with sp.Fori(0, LAST // 2) as g:
                load(g)
            load(LAST // 2)

        @block.gpsimd
        def _(pool):
            pool.memset(hidden[:, LAST, :], 0.0).then_inc(cleared, 1)

        @block.tensor
        def _(pe):
            for counter in (bT_turned, wT_turned, projected):
                counter.open(pe)
            pe.wait_ge(low_in, 48)
            for k in kts:
                last = nc.tensor.transpose(small_bank[:RANK0, k * P:(k + 1) * P], down_b[:, k, :], mem.ident[:, :])
            last.then_inc(down_bT_turned, 1)
            pe.wait_ge(down_bT_out, 1)

            def prepare(g, s, f):
                r = rows_of(f)
                pe.wait_ge(w_in[s], g * 96 + 96)
                pe.wait_ge(*(bT_out.now(g, 0) if s else bT_out.last(g, 1)))
                for m in range(2):
                    last = nc.tensor.transpose(small_bank[:RANK0, m * P:m * P + r], raw_b[:r, s, m, :],
                                               mem.ident[:r, :r])
                last.then_inc(bT_turned.sem, 1)
                for m in (2, 0, 1):
                    pe.wait_ge(*(w_split.now(g, (0, m)) if s else w_split.last(g, (1, m))))
                    if m == 2:
                        for k in kts:
                            nc.tensor.matmul(wT_bank[2][:r, k * P:(k + 1) * P], raw[:, s, 2, k * r:(k + 1) * r],
                                             mem.ident[:, :], is_transpose=True, start=(k == 0), stop=False)
                        last = nc.tensor.matmul(wT_bank[2][:r, :], down_a[:, s, 0:r], down_bT[:, :],
                                                start=False, stop=True)
                    else:
                        if m == 0:
                            pe.wait_ge(*bT_out.now(g, s))
                        for k in kts:
                            nc.tensor.matmul(wT_bank[m][:, k * P:k * P + r], raw[:r, s, m, k * P:(k + 1) * P],
                                             mem.ident[:r, :r], is_transpose=True, start=(k == 0), stop=False)
                        for k in kts:
                            last = nc.tensor.matmul(wT_bank[m][:, k * P:k * P + r], low_a[:, m, k * P:(k + 1) * P],
                                                    low_bT[:, s, m, 0:r], start=False, stop=(k == KT - 1))
                    last.then_inc(wT_turned.sem, 1)

            def project(g, s, f):
                r = rows_of(f)
                pe.wait_ge(*w_split.now(g, (s, 1)))
                pe.wait_ge(*(hidden_done.now(g, 0) if s else hidden_done.last(g, 1)))
                for m in range(2):
                    for b in range(NHALF):
                        for k in kts:
                            last = split_products(nc.tensor, out_pair[m][:r, half(b)], [part[:, s, m, k, 0:r] for part in wT],
                                                  [part[:, k, half(b)] for part in mem.hT], k == 0, k == KT - 1)
                last.then_inc(projected.sem, 1)

            def turn(g):
                for s, f in tiles_in_turn(g):
                    prepare(g, s, f)
                    project(g, s, f)

            with pe.Fori(0, LAST // 2) as g:
                turn(g)
            turn(LAST // 2)
            for t in range(NT):
                pe.wait_ge(act_split, t + 1)
                if t >= 2:
                    pe.wait_ge(added, t - 1)
                for f in range(NF):
                    r = rows_of(f)
                    last = split_products(nc.tensor, mem.bank[t % 2][:, :], [part[:r, t % 2, f, :] for part in act_t],
                                          [part[:r, f, :] for part in downT], f == 0, f == NF - 1)
                last.then_inc(produced, 1)

        @block.scalar
        def _(act):
            for counter in (bT_out, w_hi, silu_done):
                counter.open(act)
            act.wait_ge(cleared, 1)
            act.wait_ge(down_bT_turned, 1)
            nc.scalar.copy(down_bT[:, :], small_bank[:RANK0, :]).then_inc(down_bT_out, 1)

            def turn(g):
                for s, f in tiles_in_turn(g):
                    r = rows_of(f)
                    act.wait_ge(*bT_turned.now(g, s))
                    nc.scalar.copy(low_bT[:, s, :, 0:r],
                                   small_bank[:RANK0, 0:2 * P].rearrange("r (m n) -> r m n", m=2)[:, :, 0:r]
                                   ).then_inc(bT_out.sem, 1)
                    for m in range(2):
                        act.wait_ge(*wT_turned.now(g, (s, m)))
                        nc.scalar.copy(wT[0][:, s, m, :, 0:r],
                                       wT_bank[m].rearrange("p (k n) -> p k n", k=KT)[:, :, 0:r]).then_inc(w_hi.sem, 1)
                    act.wait_ge(*projected.now(g, s))
                    nc.scalar.activation(hidden[:r, bass.ds(f, 1), :], out_pair[0][:r, :], ACT.Silu).then_inc(silu_done.sem, 1)

            with act.Fori(0, LAST // 2) as g:
                turn(g)
            turn(LAST // 2)

        @block.vector
        def _(dve):
            for counter in (w_split, down_gated, down_hi, hidden_done):
                counter.open(dve)
            dve.wait_ge(cleared, 1)

            def turn(g):
                for s, f in tiles_in_turn(g):
                    r = rows_of(f)
                    at = bass.ds(f, 1)
                    dve.wait_ge(*wT_turned.now(g, (s, 2)))
                    nc.vector.tensor_tensor(down_full[:r, :], wT_bank[2][:r, :], mem.gate[:r, 1, :],
                                            ALU.mult).then_inc(down_gated.sem, 1)
                    dve.wait_ge(*down_gated.now(g, s))
                    nc.vector.tensor_copy(downT[0][:r, at, :], down_full[:r, :]).then_inc(down_hi.sem, 1)
                    dve.wait_ge(*down_hi.now(g, s))
                    nc.vector.tensor_tensor(downT[1][:r, at, :], down_full[:r, :],
                                            downT[0][:r, at, :].bitcast(F32), ALU.subtract).then_inc(w_split.sem, 1)
                    for m in range(2):
                        dve.wait_ge(*w_hi.now(g, (s, m)))
                        nc.vector.tensor_tensor(wT[1][:, s, m, :, 0:r],
                                                wT_bank[m].rearrange("p (k n) -> p k n", k=KT)[:, :, 0:r],
                                                wT[0][:, s, m, :, 0:r].bitcast(F32), ALU.subtract
                                                ).then_inc(w_split.sem, 1)
                    dve.wait_ge(*silu_done.now(g, s))
                    nc.vector.tensor_tensor(hidden[:r, at, :], out_pair[1][:r, :], hidden[:r, at, :], ALU.mult
                                            ).then_inc(hidden_done.sem, 1)

            with dve.Fori(0, LAST // 2) as g:
                turn(g)
            turn(LAST // 2)
            dve.wait_ge(*hidden_done.now(LAST // 2, 0))

            def add(t):
                dve.wait_ge(produced, t + 1)
                nc.vector.tensor_tensor(mem.x[:, t, :], mem.bank[t % 2][:, :], mem.x[:, t, :], ALU.add).then_inc(added, 1)

            for t in range(NT):
                part = hidden[:, :, t * P:(t + 1) * P]
                nc.vector.tensor_copy(act_t[0][:, t % 2, :, :], part).then_inc(act_hi, 1)
                dve.wait_ge(act_hi, t + 1)
                nc.vector.tensor_tensor(act_t[1][:, t % 2, :, :], part, act_t[0][:, t % 2, :, :].bitcast(F32),
                                        ALU.subtract).then_inc(act_split, 1)
                if t:
                    add(t - 1)
            add(NT - 1)


def layer1_qkv_phase(nc, mem, k1, v1, rope_dram, w_dram, b_dram):
    NC = QKV1 // P
    NH, NP = NH1 + NKV1, HD1 // 2
    QW = NH1 * HD1
    with ExitStack() as ctx:
        sem = lambda name: mem.semaphores.enter_context(nc.semaphore("p1_" + name))
        sb = lambda name, shape, dt=F32: ctx.enter_context(nc.sbuf_tensor("p1_" + name, shape, dt))
        raw = sb("raw", [P, NC, D])
        bias = sb("bias", [P, QKV1])
        rope = sb("rope", [P, NT, 2, NP])
        wT = (sb("wT_hi", [P, KT, QKV1], F32R), sb("wT_lo", [P, KT, QKV1], F32R))
        qkv = sb("qkv", [P, NT, QKV1])
        part = [sb(f"part{n}", [P, 2, NH, NP]) for n in range(4)]
        roped = sb("roped", [P, 2, NH, HD1])
        q1 = [mem.hT[n].rearrange("p k s -> p (k s)").rearrange("p (t d) -> p t d", t=NT) for n in range(2)]
        w_in, small_in = sem("w_in"), sem("small_in")
        wT_turned, w_hi, w_split = sem("wT_turned"), sem("w_hi"), sem("w_split")
        projected, biased, rotated, summed, hi_done, split = (sem("projected"), sem("biased"), sem("rotated"),
                                                              sem("summed"), sem("hi_done"), sem("split"))
        block = ctx.enter_context(nc.Block())

        @block.sync
        def _(sp):
            sp.dma_start(raw[:, :, :], w_dram.rearrange("(c p) d -> p c d", p=P)).then_inc(w_in, 16)
            sp.dma_start(bias[:, :], b_dram.unsqueeze(0).broadcast_to([P, QKV1])).then_inc(small_in, 16)
            sp.dma_start(rope[:, :, :, :], rope_dram.rearrange("(t p) a f -> p t a f", p=P)).then_inc(small_in, 16)

        @block.tensor
        def _(pe):
            pe.wait_ge(w_in, 16)
            for k in range(KT):
                if k >= 2:
                    pe.wait_ge(w_split, k - 1)
                for c in range(NC):
                    last = nc.tensor.transpose(mem.bank_pair[k % 2][:, c * P:(c + 1) * P],
                                               raw[:, c, k * P:(k + 1) * P], mem.ident[:, :])
                last.then_inc(wT_turned, 1)
            pe.wait_ge(w_split, KT)
            for t in range(NT):
                if t >= 2:
                    pe.wait_ge(biased, t - 1)
                for cols in (slice(0, HALF), slice(HALF, QKV1)):
                    for k in range(KT):
                        last = split_products(nc.tensor, mem.bank_pair4(t % 2)[:, cols],
                                              [a[:, k, t * P:(t + 1) * P] for a in mem.hT],
                                              [a[:, k, cols] for a in wT], k == 0, k == KT - 1)
                last.then_inc(projected, 1)

        @block.scalar
        def _(act):
            for k in range(KT):
                act.wait_ge(wT_turned, k + 1)
                nc.scalar.copy(wT[0][:, k, :], mem.bank_pair[k % 2][:, 0:QKV1]).then_inc(w_hi, 1)

        @block.vector
        def _(dve):
            for k in range(KT):
                dve.wait_ge(w_hi, k + 1)
                nc.vector.tensor_tensor(wT[1][:, k, :], mem.bank_pair[k % 2][:, 0:QKV1],
                                        wT[0][:, k, :].bitcast(F32), ALU.subtract).then_inc(w_split, 1)
            dve.wait_ge(small_in, 32)
            for t in range(NT):
                dve.wait_ge(projected, t + 1)
                nc.vector.tensor_tensor(qkv[:, t, :], mem.bank_pair4(t % 2)[:, 0:QKV1], bias[:, :], ALU.add
                                        ).then_inc(biased, 1)
            dve.wait_ge(biased, NT)

            def rotate(t):
                x = qkv[:, t, 0:QK1].rearrange("p (h f two) -> p h f two", two=2, f=NP)
                turn = [rope[:, t, n, :].unsqueeze(1).broadcast_to([P, NH, NP]) for n in range(2)]
                for n, (a, b) in enumerate(((0, 0), (1, 1), (0, 1), (1, 0))):
                    last = nc.vector.tensor_tensor(part[n][:, t % 2, :, :], x[:, :, :, a], turn[b], ALU.mult)
                last.then_inc(rotated, 1)
                nc.vector.tensor_copy(v1[:, t, :], qkv[:, t, QK1:QKV1])

            def combine(t):
                dve.wait_ge(rotated, t + 1)
                r = roped[:, t % 2, :, :]
                nc.vector.tensor_tensor(r[:, :, 0:NP], part[0][:, t % 2], part[1][:, t % 2], ALU.subtract)
                nc.vector.tensor_tensor(r[:, :, NP:HD1], part[2][:, t % 2], part[3][:, t % 2], ALU.add).then_inc(summed, 1)

            def high(t):
                dve.wait_ge(summed, t + 1)
                r = roped[:, t % 2, :, :].rearrange("p h d -> p (h d)")
                nc.vector.tensor_scalar(q1[0][:, t, :], r[:, 0:QW], SCALE1, None, ALU.mult)
                nc.vector.tensor_copy(k1[0][:, t, :], r[:, QW:QK1]).then_inc(hi_done, 1)

            def low(t):
                dve.wait_ge(hi_done, t + 1)
                r = roped[:, t % 2, :, :].rearrange("p h d -> p (h d)")
                nc.vector.scalar_tensor_tensor(out=q1[1][:, t, :], in0=r[:, 0:QW], scalar=SCALE1,
                                               in1=q1[0][:, t, :].bitcast(F32), op0=ALU.mult, op1=ALU.subtract)
                nc.vector.tensor_tensor(k1[1][:, t, :], r[:, QW:QK1], k1[0][:, t, :].bitcast(F32),
                                        ALU.subtract).then_inc(split, 1)

            rotate(0)
            for t in range(NT):
                combine(t)
                if t < NT - 1:
                    rotate(t + 1)
                high(t)
                low(t)
                dve.wait_ge(split, t + 1)


def layer1_attention_phase(nc, mem, k1, v1, attended):
    heads, tiles, halves = range(REP1), range(NT), range(NHALF)
    PARTS = 4
    STACK = PARTS * HD1
    PAIRS = REP1 // 2
    VW = 32
    units = [(h, i) for b in halves for h in heads for i in range(b * TPH, (b + 1) * TPH)]
    pieces = [(h, i, c) for h, i in units for c in range(i // TPH + 1)]
    by_vector = lambda piece: piece[1] >= TPH and piece[2] == 0
    stages = [("k", b) for b in halves] + [("q", n, b) for n in range(PAIRS) for b in halves]
    q1 = [mem.hT[n].rearrange("p k s -> p (k s)").rearrange("p (t d) -> p t d", t=NT) for n in range(2)]
    with ExitStack() as ctx:
        sem = lambda name: mem.semaphores.enter_context(nc.semaphore("a1_" + name))
        turns = lambda name, names: Turns(sem(name), names)
        sb = lambda name, shape, dt=F32: ctx.enter_context(nc.sbuf_tensor("a1_" + name, shape, dt))
        q_stack, k_stack = sb("q_stack", [P, NT, PAIRS, 2 * STACK]), sb("k_stack", [P, NT, 2 * STACK])
        v, nothing = sb("v", [P, NT, VW]), sb("nothing", [P, NT, HD1])
        qT, kT = sb("qT", [P, PAIRS, S], F32R), sb("kT", [P, 2, S], F32R)
        probs, probsT = sb("probs", [P, 2, S]), sb("probsT", [P, REP1, NT, HALF])
        ctxT = sb("ctxT", [P, HALF])
        neg_max, row_sum, row_inv = (sb("neg_max", [P, NT, REP1]), sb("row_sum", [P, NT, REP1]),
                                     sb("row_inv", [P, NT, REP1]))
        cleared = sem("cleared")
        stacked = turns("stacked", ["v", "k", "q"])
        stage_turned, stage_out = turns("stage_turned", stages), turns("stage_out", stages)
        scored, maxed, exped = turns("scored", units), turns("maxed", units), turns("exped", units)
        turned = turns("turned", pieces)
        out_act = turns("out_act", [p for p in pieces if not by_vector(p)])
        out_dve = turns("out_dve", [p for p in pieces if by_vector(p)])
        valued, ctx_out, ctx_turned = turns("valued", halves), turns("ctx_out", halves), turns("ctx_turned", halves)
        inverted, attended_done = turns("inverted", halves), turns("attended_done", halves)
        turned_out = lambda piece: out_dve if by_vector(piece) else out_act
        score, turn_bank, value_bank, ctx_bank = mem.bank_pair, mem.bank[4:6], mem.bank[6], mem.bank[7]
        tile = lambda i: slice(i * P, (i + 1) * P)
        half = lambda b: slice(b * HALF, (b + 1) * HALF)
        block = ctx.enter_context(nc.Block())

        @block.gpsimd
        def _(pool):
            pool.memset(v[:, :, :], 0.0).then_inc(cleared, 1)
            pool.memset(kT[:, :, :].bitcast(F32), 0.0).then_inc(cleared, 1)
            pool.memset(nothing[:, :, :], 0.0).then_inc(cleared, 1)
            stacked.open(pool)
            pool.wait_ge(cleared, 3)
            with pool.Fori(0, NKV1) as g:
                keys = bass.ds(g * HD1, HD1)
                pool.wait_ge(*valued.last(g, 1))
                pool.tensor_tensor(v[:, :, 0:HD1], v1[:, :, keys], nothing[:, :, :], ALU.add).then_inc(stacked.sem, 1)
                pool.wait_ge(*stage_turned.last(g, ("k", 1)))
                for n, of in enumerate((0, 0, 1, 1) * 2):
                    last = pool.tensor_tensor(k_stack[:, :, n * HD1:(n + 1) * HD1], k1[of][:, :, keys].bitcast(F32),
                                              nothing[:, :, :], ALU.add)
                last.then_inc(stacked.sem, 1)
                pool.wait_ge(*stage_turned.last(g, stages[-1]))
                for h in heads:
                    for n, of in enumerate((0, 1, 0, 1)):
                        at = (h % 2) * STACK + n * HD1
                        last = pool.tensor_tensor(q_stack[:, :, h // 2, at:at + HD1],
                                                  q1[of][:, :, bass.ds(g * (REP1 * HD1) + h * HD1, HD1)].bitcast(F32),
                                                  nothing[:, :, :], ALU.add)
                last.then_inc(stacked.sem, 1)

        @block.tensor
        def _(pe):
            for counter in (stage_turned, scored, turned, valued, ctx_turned):
                counter.open(pe)
            pe.wait_ge(cleared, 2)
            with pe.Fori(0, NKV1) as g:
                def stage(name):
                    n = stages.index(name)
                    out = (value_bank, ctx_bank)[n % 2]
                    if n >= 2:
                        pe.wait_ge(*stage_out.now(g, stages[n - 2]))
                    else:
                        pe.wait_ge(*(ctx_out, attended_done)[n].last(g, 1))
                    for t in range(TPH):
                        i = name[-1] * TPH + t
                        if name[0] == "k":
                            last = nc.tensor.transpose(out[:, tile(t)], k_stack[:, i, :], mem.ident[:, :])
                        else:
                            last = nc.tensor.transpose(out[:, tile(t)], q_stack[:, i, name[1], :], mem.ident[:, :])
                    last.then_inc(stage_turned.sem, 1)

                def scores(u):
                    h, i = units[u]
                    pe.wait_ge(*(exped.now(g, units[u - 2]) if u >= 2 else exped.last(g, units[u - 2])))
                    for c in range(i // TPH + 1):
                        keys = slice(c * HALF, min((c + 1) * HALF, (i + 1) * P))
                        diagonal = c == i // TPH
                        last = nc.tensor.matmul(score[u % 2][:, keys], qT[:, h // 2, tile(i)], kT[:, h % 2, keys],
                                                start=True, stop=not diagonal)
                        if diagonal:
                            last = nc.tensor.matmul(score[u % 2][:, tile(i)], mem.ident_bf[:, :], mem.causal[:, :],
                                                    start=False, stop=True)
                    last.then_inc(scored.sem, 1)

                def turn(u):
                    h, i = units[u]
                    pe.wait_ge(*exped.now(g, (h, i)))
                    for c in range(i // TPH + 1):
                        n = pieces.index((h, i, c))
                        before = pieces[n - 2]
                        pe.wait_ge(*(turned_out(before).now(g, before) if n >= 2 else
                                     turned_out(before).last(g, before)))
                        for j in range(c * TPH, min((c + 1) * TPH, i + 1)):
                            last = nc.tensor.transpose(turn_bank[n % 2][:, tile(j - c * TPH)], probs[:, u % 2, tile(j)],
                                                       mem.ident[:, :])
                        last.then_inc(turned.sem, 1)

                def values(b):
                    if b:
                        pe.wait_ge(*ctx_out.now(g, 0))
                    else:
                        pe.wait_ge(*stage_out.now(g, stages[-2]))
                        pe.wait_ge(*stacked.now(g, "v"))
                    done = [p for p in pieces if p[1] // TPH == b]
                    for counter, which in ((out_act, False), (out_dve, True)):
                        of = [p for p in done if by_vector(p) == which]
                        if of:
                            pe.wait_ge(*counter.now(g, of[-1]))
                    keys = TPH * (b + 1)
                    for j in range(keys):
                        first = max(0, j - TPH * b) * P
                        for h in heads:
                            last = nc.tensor.matmul(value_bank[h * VW:(h + 1) * VW, first:HALF], v[:, j, :],
                                                    probsT[:, h, j, first:HALF], start=(j == 0), stop=(j == keys - 1))
                    last.then_inc(valued.sem, 1)

                def turn_values(b):
                    pe.wait_ge(*ctx_out.now(g, b))
                    pe.wait_ge(*(attended_done.now(g, 0) if b else stage_out.now(g, stages[-1])))
                    for t in range(TPH):
                        last = nc.tensor.transpose(ctx_bank[:, tile(t)], ctxT[:, tile(t)], mem.ident[:, :])
                    last.then_inc(ctx_turned.sem, 1)

                for name in stages:
                    if name == ("k", 0):
                        pe.wait_ge(*stacked.now(g, "k"))
                    if name == ("q", 0, 0):
                        pe.wait_ge(*stacked.now(g, "q"))
                    stage(name)
                pe.wait_ge(*stage_out.now(g, stages[-1]))
                scores(0)
                for u in range(len(units)):
                    if u < len(units) - 1:
                        scores(u + 1)
                    turn(u)
                    if u == len(units) // 2 - 1:
                        values(0)
                    if u == len(units) // 2 + 1:
                        turn_values(0)
                values(1)
                turn_values(1)

        @block.vector
        def _(dve):
            for counter in (maxed, out_dve, inverted, attended_done):
                counter.open(dve)
            with dve.Fori(0, NKV1) as g:
                def maximum(u):
                    h, i = units[u]
                    dve.wait_ge(*scored.now(g, (h, i)))
                    nc.vector.reduce_max(neg_max[:, i, h:h + 1], score[u % 2][:, 0:(i + 1) * P], AX.X,
                                         negate=True).then_inc(maxed.sem, 1)

                def normalize(b):
                    tb = slice(b * TPH, (b + 1) * TPH)
                    dve.wait_ge(*exped.now(g, units[(b + 1) * len(units) // 2 - 1]))
                    nc.vector.reciprocal(row_inv[:, tb, :], row_sum[:, tb, :]).then_inc(inverted.sem, 1)
                    dve.wait_ge(*inverted.now(g, b))
                    dve.wait_ge(*ctx_turned.now(g, b))
                    for t in range(TPH):
                        i = b * TPH + t
                        last = nc.vector.tensor_tensor(
                            attended[:, i, bass.ds(g * (REP1 * HD1), REP1 * HD1)].rearrange("p (h d) -> p h d", h=REP1),
                            ctx_bank[:, tile(t)].rearrange("p (h d) -> p h d", h=REP1)[:, :, 0:HD1],
                            row_inv[:, i, :].unsqueeze(2).broadcast_to([P, REP1, HD1]), ALU.mult)
                    last.then_inc(attended_done.sem, 1)

                def take_turned(u):
                    h, i = units[u]
                    n = pieces.index((h, i, 0))
                    dve.wait_ge(*turned.now(g, (h, i, 0)))
                    nc.vector.tensor_copy(probsT[:, h, 0:TPH, tile(i % TPH)],
                                          turn_bank[n % 2].rearrange("p (j q) -> p j q", j=TPH)).then_inc(out_dve.sem, 1)

                maximum(0)
                for u in range(len(units)):
                    if u < len(units) - 1:
                        maximum(u + 1)
                    if units[u][1] >= TPH:
                        take_turned(u)
                    if u == len(units) // 2 + 1:
                        normalize(0)
                normalize(1)

        @block.scalar
        def _(act):
            for counter in (stage_out, exped, out_act, ctx_out):
                counter.open(act)
            act.wait_ge(cleared, 2)
            with act.Fori(0, NKV1) as g:
                def take_stage(name):
                    act.wait_ge(*stage_turned.now(g, name))
                    out = (value_bank, ctx_bank)[stages.index(name) % 2]
                    b = name[-1]
                    if name[0] == "k":
                        nc.scalar.copy(kT[0:STACK, 0, half(b)], out[0:STACK, :])
                        last = nc.scalar.copy(kT[STACK:P, 1, half(b)], out[STACK:P, :])
                    else:
                        last = nc.scalar.copy(qT[:, name[1], half(b)], out[:, :])
                    last.then_inc(stage_out.sem, 1)

                def exponential(u):
                    h, i = units[u]
                    if h == 0 and i % TPH == 0:
                        act.wait_ge(*inverted.last(g, i // TPH))
                    act.wait_ge(*maxed.now(g, (h, i)))
                    nc.scalar.activation(probs[:, u % 2, 0:(i + 1) * P], score[u % 2][:, 0:(i + 1) * P], ACT.Exp,
                                         bias=neg_max[:, i, h:h + 1],
                                         accum_out=row_sum[:, i, h:h + 1]).then_inc(exped.sem, 1)

                def take_turned(u):
                    h, i = units[u]
                    if h == 0 and i % TPH == 0:
                        act.wait_ge(*(valued.now(g, 0) if i else valued.last(g, 1)))
                    for c in range(i // TPH + 1):
                        piece = (h, i, c)
                        if by_vector(piece):
                            continue
                        act.wait_ge(*turned.now(g, piece))
                        keys = min(TPH, i + 1 - c * TPH)
                        nc.scalar.copy(probsT[:, h, c * TPH:c * TPH + keys, tile(i % TPH)],
                                       turn_bank[pieces.index(piece) % 2][:, 0:keys * P]
                                       .rearrange("p (j q) -> p j q", j=keys)).then_inc(out_act.sem, 1)

                def take_values(b):
                    act.wait_ge(*valued.now(g, b))
                    act.wait_ge(*(ctx_turned.now(g, 0) if b else ctx_turned.last(g, 1)))
                    nc.scalar.copy(ctxT[:, :], value_bank[:, :]).then_inc(ctx_out.sem, 1)

                for name in stages:
                    take_stage(name)
                exponential(0)
                for u in range(len(units)):
                    if u < len(units) - 1:
                        exponential(u + 1)
                    take_turned(u)
                    if u == len(units) // 2:
                        take_values(0)
                take_values(1)


def layer1_output_phase(nc, mem, attended, w_dram, b_dram):
    with ExitStack() as ctx:
        sem = lambda name: mem.semaphores.enter_context(nc.semaphore("o1_" + name))
        sb = lambda name, shape, dt=F32: ctx.enter_context(nc.sbuf_tensor("o1_" + name, shape, dt))
        raw, bias = sb("raw", [P, KT, D]), sb("bias", [P, D])
        gated = sb("gated", [P, KT, D])
        wT = (sb("wT_hi", [P, KT, D], F32R), sb("wT_lo", [P, KT, D], F32R))
        aT = mem.hT
        w_in, b_in = sem("w_in"), sem("b_in")
        w_turned, w_gated, w_hi, w_split = sem("w_turned"), sem("w_gated"), sem("w_hi"), sem("w_split")
        a_turned, a_hi, a_split = sem("a_turned"), sem("a_hi"), sem("a_split")
        bias_gated, biased, produced, added = sem("bias_gated"), sem("biased"), sem("produced"), sem("added")
        pieces = [(half, k) for half in range(NHALF) for k in range(KT)]
        block = ctx.enter_context(nc.Block())

        @block.sync
        def _(sp):
            sp.dma_start(raw[:, :, :], w_dram.rearrange("(c p) d -> p c d", p=P)).then_inc(w_in, 16)
            sp.dma_start(bias[:, :], b_dram.unsqueeze(0).broadcast_to([P, D])).then_inc(b_in, 16)

        @block.gpsimd
        def _(pool):
            pool.wait_ge(b_in, 16)
            pool.tensor_tensor(bias[:, :], bias[:, :], mem.gate[:, 2, :], ALU.mult).then_inc(bias_gated, 1)
            pool.wait_ge(bias_gated, 1)
            for t in range(NT):
                last = pool.tensor_tensor(mem.x[:, t, :], mem.x[:, t, :], bias[:, :], ALU.add).then_inc(biased, 1)

        @block.tensor
        def _(pe):
            for i, (half, k) in enumerate(pieces):
                if i >= 2:
                    pe.wait_ge(a_split, i - 1)
                for t in range(TPH):
                    last = nc.tensor.transpose(mem.bank[i % 2][:, t * P:(t + 1) * P],
                                               attended[:, half * TPH + t, k * P:(k + 1) * P], mem.ident[:, :])
                last.then_inc(a_turned, 1)
            pe.wait_ge(w_in, 16)
            for k in range(KT):
                if k >= 2:
                    pe.wait_ge(w_gated, k - 1)
                for c in range(KT):
                    last = nc.tensor.transpose(mem.bank[2 + k % 2][:, c * P:(c + 1) * P], raw[:, c, k * P:(k + 1) * P],
                                               mem.ident[:, :])
                last.then_inc(w_turned, 1)
            pe.wait_ge(w_split, KT)
            for t in range(NT):
                if t >= 2:
                    pe.wait_ge(added, t - 1)
                for k in range(KT):
                    last = split_products(nc.tensor, mem.bank[4 + t % 2][:, :], [a[:, k, t * P:(t + 1) * P] for a in aT],
                                          [a[:, k, :] for a in wT], k == 0, k == KT - 1)
                last.then_inc(produced, 1)

        @block.scalar
        def _(act):
            for i, (half, k) in enumerate(pieces):
                act.wait_ge(a_turned, i + 1)
                nc.scalar.copy(aT[0][:, k, half * HALF:(half + 1) * HALF], mem.bank[i % 2][:, :]).then_inc(a_hi, 1)
            for k in range(KT):
                act.wait_ge(w_gated, k + 1)
                nc.scalar.copy(wT[0][:, k, :], gated[:, k, :]).then_inc(w_hi, 1)

        @block.vector
        def _(dve):
            for i, (half, k) in enumerate(pieces):
                cols = slice(half * HALF, (half + 1) * HALF)
                dve.wait_ge(a_hi, i + 1)
                nc.vector.tensor_tensor(aT[1][:, k, cols], mem.bank[i % 2][:, :], aT[0][:, k, cols].bitcast(F32),
                                        ALU.subtract).then_inc(a_split, 1)
            for k in range(KT):
                dve.wait_ge(w_turned, k + 1)
                nc.vector.tensor_tensor(gated[:, k, :], mem.bank[2 + k % 2][:, :], mem.gate[:, 2, :], ALU.mult
                                        ).then_inc(w_gated, 1)
            for k in range(KT):
                dve.wait_ge(w_hi, k + 1)
                nc.vector.tensor_tensor(wT[1][:, k, :], gated[:, k, :], wT[0][:, k, :].bitcast(F32), ALU.subtract
                                        ).then_inc(w_split, 1)
            for t in range(NT):
                dve.wait_ge(produced, t + 1)
                dve.wait_ge(biased, t + 1)
                nc.vector.tensor_tensor(mem.x[:, t, :], mem.bank[4 + t % 2][:, :], mem.x[:, t, :], ALU.add
                                        ).then_inc(added, 1)


def layer1_experts_phase(nc, mem, x_out, w):
    RT = (ER + P - 1) // P
    R_OF = [P, ER - P]
    LW = NE + ER
    with ExitStack() as ctx:
        sem = lambda name: mem.semaphores.enter_context(nc.semaphore("e1_" + name))
        sb = lambda name, shape, dt=F32: ctx.enter_context(nc.sbuf_tensor("e1_" + name, shape, dt))
        pair = lambda name, shape: (sb(name + "_hi", shape, F32R), sb(name + "_lo", shape, F32R))
        raw, raw_a, raw_g = sb("raw", [P, KT, D]), sb("raw_a", [P, RT, D]), sb("raw_g", [NE, D])
        raw_b = sb("raw_b", [P, KT, NE, RANK1])
        gated = sb("gated", [P, 2, D])
        wT, aT = pair("wT", [P, KT, D]), pair("aT", [P, KT, LW])
        bT = pair("bT", [P, RT, D])
        number = sb("number", [P, NE], I32)
        numberf = sb("numberf", [P, NE])
        low_all = sb("low_all", [P, NT, LW])
        top, index, indexf = sb("top", [P, NT, 8]), sb("index", [P, NT, 8], U32), sb("indexf", [P, NT, 2])
        gap, exped, prob = sb("gap", [P, NT]), sb("exped", [P, NT]), sb("prob", [P, NT, 2])
        chosen, mix = sb("chosen", [P, 2, NE]), sb("mix", [P, NE])
        scaled = sb("scaled", [P, 2, ER])
        sT = pair("sT", [P, 2, RT, P])
        w_in, a_in, b_in = sem("w_in"), sem("a_in"), sem("b_in")
        w_turned, w_gated, w_hi, w_split = sem("w_turned"), sem("w_gated"), sem("w_hi"), sem("w_split")
        a_turned, a_hi, a_split = sem("a_turned"), sem("a_hi"), sem("a_split")
        counted, numbered = sem("counted"), sem("numbered")
        logits_done, logits_out, topped, indexed = sem("logits_done"), sem("logits_out"), sem("topped"), sem("indexed")
        step, gapped, exp_done = sem("step"), sem("gapped"), sem("exp_done")
        scaled_done, s_turned, s_hi, s_split = sem("scaled_done"), sem("s_turned"), sem("s_hi"), sem("s_split")
        produced, added, stored = sem("produced"), sem("added"), sem("stored")
        mats = [("w", k) for k in range(KT)] + [("b", r) for r in range(RT)]
        block = ctx.enter_context(nc.Block())

        @block.sync
        def _(sp):
            sp.dma_start(raw_g[:, :], w["gate"][:, :]).then_inc(a_in, 16)
            a = w["a"].rearrange("e r d -> (e r) d")
            sp.dma_start(raw_a[:, 0, :], a[0:P, :]).then_inc(a_in, 16)
            sp.dma_start(raw_a[:R_OF[1], 1, :], a[P:ER, :]).then_inc(a_in, 16)
            sp.dma_start(raw[:, :, :], w["base"].rearrange("(c p) d -> p c d", p=P)).then_inc(w_in, 16)
            for c in range(KT):
                sp.dma_start(raw_b[:, c, :, :], w["b"][:, c * P:(c + 1) * P, :].rearrange("e p r -> p e r")
                             ).then_inc(b_in, 16)
            for t in range(NT):
                sp.wait_ge(added, t + 1)
                sp.dma_start(x_out[0, t * P:(t + 1) * P, :], mem.x[:, t, :]).then_inc(stored, 16)
            sp.wait_ge(stored, 16 * NT)

        @block.gpsimd
        def _(pool):
            pool.iota(number[:, :], [[1, NE]], base=0, channel_multiplier=0).then_inc(counted, 1)

        @block.tensor
        def _(pe):
            pe.wait_ge(a_in, 48)
            for k in range(KT):
                if k >= 2:
                    pe.wait_ge(a_split, k - 1)
                out = mem.bank[k % 2]
                cols = slice(k * P, (k + 1) * P)
                nc.tensor.transpose(out[:, 0:NE], raw_g[:, cols], mem.ident[:NE, :NE])
                nc.tensor.transpose(out[:, NE:NE + P], raw_a[:, 0, cols], mem.ident[:, :])
                nc.tensor.transpose(out[:, NE + P:LW], raw_a[:R_OF[1], 1, cols], mem.ident[:R_OF[1], :R_OF[1]]
                                    ).then_inc(a_turned, 1)
            pe.wait_ge(w_in, 16)
            for n, (m, k) in enumerate(mats):
                if m == "b" and k == 0:
                    pe.wait_ge(b_in, 16 * KT)
                if n >= 2:
                    pe.wait_ge(w_gated, n - 1)
                out = mem.bank[2 + n % 2]
                for c in range(KT):
                    if m == "w":
                        last = nc.tensor.transpose(out[:, c * P:(c + 1) * P], raw[:, c, k * P:(k + 1) * P], mem.ident[:, :])
                    else:
                        rows = raw_b[:, c, :, :].rearrange("p e r -> p (e r)")[:, k * P:k * P + R_OF[k]]
                        last = nc.tensor.transpose(out[:R_OF[k], c * P:(c + 1) * P], rows, mem.ident[:, :])
                last.then_inc(w_turned, 1)
            pe.wait_ge(a_split, KT)

            def low(t):
                if t >= 2:
                    pe.wait_ge(logits_out, t - 1)
                for k in range(KT):
                    last = split_products(nc.tensor, mem.bank[t % 2][:, 0:LW], [a[:, k, t * P:(t + 1) * P] for a in mem.hT],
                                          [a[:, k, :] for a in aT], k == 0, k == KT - 1)
                last.then_inc(logits_done, 1)

            for t in range(NT):
                low(t)
            pe.wait_ge(w_split, len(mats))
            for t in range(NT):
                out = mem.bank[6 + t % 2]
                if t >= 2:
                    pe.wait_ge(added, t - 1)
                for k in range(KT):
                    split_products(nc.tensor, out[:, :], [a[:, k, t * P:(t + 1) * P] for a in mem.hT],
                                   [a[:, k, :] for a in wT], k == 0, False)
                pe.wait_ge(scaled_done, t + 1)
                if t >= 2:
                    pe.wait_ge(s_split, t - 1)
                for r in range(RT):
                    last = nc.tensor.transpose(mem.bank[4 + t % 2][:R_OF[r], r * P:(r + 1) * P],
                                               scaled[:, t % 2, r * P:r * P + R_OF[r]], mem.ident[:, :])
                last.then_inc(s_turned, 1)
                pe.wait_ge(s_split, t + 1)
                for r in range(RT):
                    n = R_OF[r]
                    last = split_products(nc.tensor, out[:, :], [a[:n, t % 2, r, :] for a in sT],
                                          [a[:n, r, :] for a in bT], False, r == RT - 1)
                last.then_inc(produced, 1)

        @block.scalar
        def _(act):
            for k in range(KT):
                act.wait_ge(a_turned, k + 1)
                nc.scalar.copy(aT[0][:, k, :], mem.bank[k % 2][:, 0:LW]).then_inc(a_hi, 1)
            for n, (m, k) in enumerate(mats):
                act.wait_ge(w_gated, n + 1)
                rows = P if m == "w" else R_OF[k]
                nc.scalar.copy((wT if m == "w" else bT)[0][:rows, k, :], gated[:rows, n % 2, :]).then_inc(w_hi, 1)
            act.wait_ge(gapped, 1)
            nc.scalar.activation(exped[:, :], gap[:, :], ACT.Exp).then_inc(exp_done, 1)
            for t in range(NT):
                act.wait_ge(s_turned, t + 1)
                for r in range(RT):
                    last = nc.scalar.copy(sT[0][:R_OF[r], t % 2, r, :], mem.bank[4 + t % 2][:R_OF[r], r * P:(r + 1) * P])
                last.then_inc(s_hi, 1)

        @block.vector
        def _(dve):
            steps = [0]

            def link(instruction):
                steps[0] += 1
                instruction.then_inc(step, 1)
                dve.wait_ge(step, steps[0])

            for k in range(KT):
                dve.wait_ge(a_hi, k + 1)
                nc.vector.tensor_tensor(aT[1][:, k, :], mem.bank[k % 2][:, 0:LW], aT[0][:, k, :].bitcast(F32),
                                        ALU.subtract).then_inc(a_split, 1)
            for n, (m, k) in enumerate(mats):
                rows = P if m == "w" else R_OF[k]
                dve.wait_ge(w_turned, n + 1)
                nc.vector.tensor_tensor(gated[:rows, n % 2, :], mem.bank[2 + n % 2][:rows, :], mem.gate[:rows, 3, :],
                                        ALU.mult).then_inc(w_gated, 1)
                out = (wT if m == "w" else bT)
                dve.wait_ge(w_hi, n + 1)
                nc.vector.tensor_tensor(out[1][:rows, k, :], gated[:rows, n % 2, :], out[0][:rows, k, :].bitcast(F32),
                                        ALU.subtract).then_inc(w_split, 1)
                dve.wait_ge(w_split, n + 1)
            dve.wait_ge(counted, 1)
            link(nc.vector.tensor_copy(numberf[:, :], number[:, :]))
            for t in range(NT):
                dve.wait_ge(logits_done, t + 1)
                nc.vector.tensor_copy(low_all[:, t, :], mem.bank[t % 2][:, 0:LW]).then_inc(logits_out, 1)
                dve.wait_ge(logits_out, t + 1)
                nc.vector.max(top[:, t, :], low_all[:, t, 0:NE]).then_inc(topped, 1)
                dve.wait_ge(topped, t + 1)
                nc.vector.max_index(index[:, t, :], top[:, t, :], low_all[:, t, 0:NE]).then_inc(indexed, 1)
            dve.wait_ge(indexed, NT)
            link(nc.vector.tensor_copy(indexf[:, :, :], index[:, :, 0:2]))
            nc.vector.tensor_tensor(gap[:, :], top[:, :, 1], top[:, :, 0], ALU.subtract).then_inc(gapped, 1)
            dve.wait_ge(exp_done, 1)
            link(nc.vector.tensor_scalar(gap[:, :], exped[:, :], 1.0, None, ALU.add))
            link(nc.vector.reciprocal(prob[:, :, 0], gap[:, :]))
            link(nc.vector.tensor_scalar(prob[:, :, 0], prob[:, :, 0], LORA_SCALE, None, ALU.mult))
            link(nc.vector.tensor_tensor(prob[:, :, 1], prob[:, :, 0], exped[:, :], ALU.mult))
            for t in range(NT):
                for n in range(2):
                    last = nc.vector.tensor_scalar(chosen[:, n, :], numberf[:, :], indexf[:, t, n:n + 1],
                                                   prob[:, t, n:n + 1], ALU.is_equal, ALU.mult)
                link(last)
                link(nc.vector.tensor_tensor(mix[:, :], chosen[:, 0, :], chosen[:, 1, :], ALU.add))
                if t >= 2:
                    dve.wait_ge(s_turned, t - 1)
                nc.vector.tensor_tensor(scaled[:, t % 2, :].rearrange("p (e r) -> p e r", e=NE),
                                        low_all[:, t, NE:LW].rearrange("p (e r) -> p e r", e=NE),
                                        mix[:, :].unsqueeze(2).broadcast_to([P, NE, RANK1]), ALU.mult
                                        ).then_inc(scaled_done, 1)
                dve.wait_ge(scaled_done, t + 1)
                dve.wait_ge(s_hi, t + 1)
                for r in range(RT):
                    n = R_OF[r]
                    last = nc.vector.tensor_tensor(sT[1][:n, t % 2, r, :], mem.bank[4 + t % 2][:n, r * P:(r + 1) * P],
                                                   sT[0][:n, t % 2, r, :].bitcast(F32), ALU.subtract)
                last.then_inc(s_split, 1)
                dve.wait_ge(produced, t + 1)
                nc.vector.tensor_tensor(mem.x[:, t, :], mem.bank[6 + t % 2][:, :], mem.x[:, t, :], ALU.add
                                        ).then_inc(added, 1)


def program(nc, ins, out, rope0, rope1):
    with ExitStack() as ctx:
        sb = lambda name, shape, dt=F32: ctx.enter_context(nc.sbuf_tensor(name, shape, dt))
        mem = Memory()
        mem.semaphores = ctx
        mem.ident, mem.ident_bf = sb("ident", [P, P]), sb("ident_bf", [P, P], BF16)
        mem.causal, mem.ones = sb("causal", [P, P], BF16), sb("ones", [P, P])
        mem.x = sb("x", [P, NT, D])
        mem.hT = (sb("hT_hi", [P, KT, S], F32R), sb("hT_lo", [P, KT, S], F32R))
        mem.gate, mem.column = sb("gate", [P, 4, D]), sb("column", [P, 8, KT])
        psum = ctx.enter_context(nc.psum_tensor("psum", [P, 8, HALF], F32))
        mem.bank = [psum[:, b, :] for b in range(8)]
        mem.bank_pair = [psum[:, 2 * s:2 * s + 2, :].rearrange("p b n -> p (b n)") for s in range(2)]
        mem.bank_pair4 = lambda m: psum[:, 4 + 2 * m:6 + 2 * m, :].rearrange("p b n -> p (b n)")
        mem.layernorm_counts = layernorm_counts(nc, mem)
        constants_phase(nc, mem)
        modulation_phase(nc, mem, ins["L0_attn_hidden_states"], (ins["L0_c"], ins["L1_c"]),
                         (ins["L0_wmod"], ins["L1_wmod"]))
        layernorm_phase(nc, mem, 0, mem.column[:, 1, :], mem.column[:, 0, :])
        layer0_attention_phase(nc, mem, rope0, {w: ins["L0_attn_qw_" + w] for w in "qkvo"},
                               {w: ins["L0_attn_scales_" + w] for w in "qkvo"})
        layernorm_phase(nc, mem, 1, mem.column[:, 3, :], mem.column[:, 2, :])
        layer0_ffn_phase(nc, mem, {n: ins["L0_ffn_" + n] for n in
                                   ("gate_w", "up_w", "down_w", "gate_a", "gate_b", "up_a", "up_b", "down_a", "down_b")})
        layernorm_phase(nc, mem, 2, mem.column[:, 5, :], mem.column[:, 4, :])
        with ExitStack() as attention:
            sb1 = lambda name, shape, dt=F32: attention.enter_context(nc.sbuf_tensor(name, shape, dt))
            k1 = (sb1("k1_hi", [P, NT, NKV1 * HD1], F32R), sb1("k1_lo", [P, NT, NKV1 * HD1], F32R))
            v1, attended = sb1("v1", [P, NT, NKV1 * HD1]), sb1("attended", [P, NT, D])
            layer1_qkv_phase(nc, mem, k1, v1, rope1, ins["L1_attn_w_qkv"], ins["L1_attn_b_qkv"])
            layer1_attention_phase(nc, mem, k1, v1, attended)
            layer1_output_phase(nc, mem, attended, ins["L1_attn_w_o"], ins["L1_attn_b_o"])
        layernorm_phase(nc, mem, 3, mem.column[:, 7, :], mem.column[:, 6, :])
        layer1_experts_phase(nc, mem, out, {"base": ins["L1_ffn_base_W"], "gate": ins["L1_ffn_gate_W"],
                                            "a": ins["L1_ffn_lora_A"], "b": ins["L1_ffn_lora_B"]})


_INS = [
    "L0_attn_hidden_states", "L0_attn_scales_q", "L0_attn_scales_k", "L0_attn_scales_v", "L0_attn_scales_o",
    "L0_attn_qw_q", "L0_attn_qw_k", "L0_attn_qw_v", "L0_attn_qw_o", "L0_ffn_gate_w", "L0_ffn_up_w", "L0_ffn_down_w",
    "L0_ffn_gate_a", "L0_ffn_gate_b", "L0_ffn_up_a", "L0_ffn_up_b", "L0_ffn_down_a", "L0_ffn_down_b", "L0_c", "L0_wmod",
    "L1_attn_w_qkv", "L1_attn_b_qkv", "L1_attn_w_o", "L1_attn_b_o", "L1_ffn_base_W", "L1_ffn_gate_W", "L1_ffn_lora_A",
    "L1_ffn_lora_B", "L1_c", "L1_wmod",
]


def _rope_tables():
    import numpy as np

    def angles(width):
        inverse = np.float32(1) / np.float32(10000) ** (np.arange(0, width, 2, dtype=np.float32) / np.float32(width))
        return np.arange(S, dtype=np.float32)[:, None] * inverse[None, :]

    a0, a1 = angles(HD0), angles(HD1)
    cos0, sin0 = np.cos(a0).T, np.sin(a0).T
    return (np.stack([np.concatenate([cos0, cos0]), np.concatenate([-sin0, sin0])]).astype(np.float32),
            np.stack([np.cos(a1), np.sin(a1)], axis=1).astype(np.float32))


def kernel(**inputs):
    import numpy as np
    import concourse.bacc as bacc
    from concourse.bass_utils import run_bass_kernel_spmd

    nc = bacc.Bacc("TRN2", target_bir_lowering=False, num_devices=1)
    rope0, rope1 = _rope_tables()
    arrays = {f"in_{name}": np.ascontiguousarray(inputs[name]) for name in _INS}
    arrays["rope0"], arrays["rope1"] = rope0, rope1
    aps = {name: nc.dram_tensor(name, a.shape, mybir.dt.from_np(a.dtype), kind="ExternalInput").ap()
           for name, a in arrays.items()}
    out = nc.dram_tensor("out", (1, S, D), F32, kind="ExternalOutput").ap()
    program(nc, {name: aps[f"in_{name}"] for name in _INS}, out, aps["rope0"], aps["rope1"])
    result = run_bass_kernel_spmd(nc, [arrays], core_ids=[0])
    return result.results[0]["out"]
```

```python
import concourse.bass as bass
from concourse import mybir
from contextlib import ExitStack

F32 = mybir.dt.float32
F32R = mybir.dt.float32r
BF16 = mybir.dt.bfloat16
I32 = mybir.dt.int32
U32 = mybir.dt.uint32
ALU = mybir.AluOpType
ACT = mybir.ActivationFunctionType
AX = mybir.AxisListType

P = 128
S = 1024
D = 512
NT = S // P
KT = D // P
HALF = 512
NHALF = S // HALF
TPH = HALF // P
LN_EPS = 1e-5
MASKED = -3.0e38

NH0, NKV0, HD0 = 32, 8, 128
REP0 = NH0 // NKV0
ZERO_POINT = 8.0
SCALE0 = float(HD0) ** -0.5

HID = 1376
RANK0 = 16
NF = (HID + P - 1) // P
HID_LAST = HID - (NF - 1) * P

NH1, NKV1, HD1 = 32, 8, 16
REP1 = NH1 // NKV1
QK1 = (NH1 + NKV1) * HD1
QKV1 = (NH1 + 2 * NKV1) * HD1
SCALE1 = float(HD1) ** -0.5

NE, RANK1 = 28, 8
ER = NE * RANK1
LORA_SCALE = 2.0


class Turns:

    def __init__(self, sem, names):
        self.sem, self.names, self.n = sem, list(names), len(names)

    def open(self, engine, done_before_loop=0):
        engine.sem_inc(self.sem, self.n - done_before_loop)

    def now(self, turn, name):
        return self.sem, turn * self.n + self.n + self.names.index(name) + 1

    def last(self, turn, name):
        return self.sem, turn * self.n + self.names.index(name) + 1


class Memory:
    pass


def split_products(pe, out, lhs, rhs, start, stop):
    (lhs_hi, lhs_lo), (rhs_hi, rhs_lo) = lhs, rhs
    pe.matmul(out, lhs_lo, rhs_hi, start=start, stop=False)
    pe.matmul(out, lhs_hi, rhs_lo, start=False, stop=False)
    return pe.matmul(out, lhs_hi, rhs_hi, start=False, stop=stop)


def constants_phase(nc, mem):
    with ExitStack() as ctx:
        cleared = mem.semaphores.enter_context(nc.semaphore("const_cleared"))
        drawn = mem.semaphores.enter_context(nc.semaphore("const_drawn"))
        block = ctx.enter_context(nc.Block())

        @block.gpsimd
        def _(pool):
            pool.memset(mem.ident[:, :], 0.0).then_inc(cleared, 1)
            pool.memset(mem.causal[:, :], 0.0).then_inc(cleared, 1)
            pool.memset(mem.ones[:, :], 1.0).then_inc(cleared, 1)
            pool.wait_ge(cleared, 3)
            pool.affine_select(out=mem.ident[:, :], in_=mem.ident[:, :], compare_op=ALU.not_equal,
                               fill=1.0, base=0, pattern=[[-1, P]], channel_multiplier=1).then_inc(drawn, 1)
            pool.affine_select(out=mem.causal[:, :], in_=mem.causal[:, :], compare_op=ALU.is_ge,
                               fill=MASKED, base=0, pattern=[[-1, P]], channel_multiplier=1).then_inc(drawn, 1)
            pool.wait_ge(drawn, 1)
            pool.tensor_copy(mem.ident_bf[:, :], mem.ident[:, :]).then_inc(drawn, 1)
            pool.wait_ge(drawn, 3)


def modulation_phase(nc, mem, x, c_dram, wmod_dram):
    SLOTS = 4
    CHUNKS = 6
    with ExitStack() as ctx:
        sem = lambda name: mem.semaphores.enter_context(nc.semaphore(name))
        sb = lambda name, shape, dt=F32: ctx.enter_context(nc.sbuf_tensor(name, shape, dt))
        c_col = sb("mod_c", [P, 2, KT])
        silu_c = sb("mod_silu", [P, 2, KT])
        silu_rows = sb("mod_silu_rows", [P, 2 * KT, P])
        w = sb("mod_w", [P, SLOTS, KT, D])
        sign = sb("mod_sign", [P, D])
        size = sb("mod_size", [P, D])
        diag = sb("mod_diag", [P, P])
        x_in, c_in = sem("x_in"), sem("mod_c_in")
        w_in = [sem(f"mod_w_in{s}") for s in range(SLOTS)]
        silu_done, rows_done = sem("mod_silu_done"), sem("mod_rows_done")
        product_done, taken, step = sem("mod_product"), sem("mod_taken"), sem("mod_step")
        bank = mem.bank
        block = ctx.enter_context(nc.Block())

        @block.sync
        def _(sp):
            for layer in range(2):
                sp.dma_start(c_col[:, layer, :], c_dram[layer][0, :].rearrange("(k p) -> p k", p=P),
                             allow_slow_non_contiguous=True).then_inc(c_in, 16)
            for j in range(2 * CHUNKS):
                if j == 2:
                    sp.dma_start(mem.x[:, :, :], x[0].rearrange("(t p) d -> p t d", p=P)).then_inc(x_in, 16)
                if j >= SLOTS:
                    sp.wait_ge(product_done, j - SLOTS + 1)
                n = j % CHUNKS
                sp.dma_start(w[:, j % SLOTS, :, :],
                             wmod_dram[j // CHUNKS][:, n * D:(n + 1) * D].rearrange("(k p) n -> p k n", p=P)
                             ).then_inc(w_in[j % SLOTS], 16)
            sp.wait_ge(x_in, 16)

        @block.scalar
        def _(act):
            act.wait_ge(c_in, 32)
            nc.scalar.activation(silu_c[:, :, :], c_col[:, :, :], ACT.Silu).then_inc(silu_done, 1)

        @block.tensor
        def _(pe):
            pe.wait_ge(rows_done, 2 * KT)
            for j in range(2 * CHUNKS):
                pe.wait_ge(w_in[j % SLOTS], 16 * (j // SLOTS + 1))
                if j >= 2:
                    pe.wait_ge(taken, j - 1)
                for k in range(KT):
                    last = nc.tensor.matmul(bank[j % 2][:, :], silu_rows[:, (j // CHUNKS) * KT + k, :],
                                            w[:, j % SLOTS, k, :], start=(k == 0), stop=(k == KT - 1))
                last.then_inc(product_done, 1)

        @block.vector
        def _(dve):
            steps = 0
            dve.wait_ge(silu_done, 1)
            for layer in range(2):
                for k in range(KT):
                    nc.vector.tensor_scalar(silu_rows[:, layer * KT + k, :], mem.ones[:, :],
                                            silu_c[:, layer, k:k + 1], None, ALU.mult).then_inc(rows_done, 1)
            for j in range(2 * CHUNKS):
                layer, n = j // CHUNKS, j % CHUNKS
                product = bank[j % 2]
                dve.wait_ge(product_done, j + 1)
                if n in (2, 5):
                    gate = mem.gate[:, 2 * layer + (n == 5), :]
                    nc.vector.tensor_scalar(sign[:, :], product[:, :], 0.0, 2.0, ALU.is_ge, ALU.mult).then_inc(step, 1)
                    nc.vector.tensor_scalar(size[:, :], product[:, :], -1.0, 0.25, ALU.mult, ALU.max).then_inc(step, 1)
                    steps += 2
                    dve.wait_ge(step, steps)
                    nc.vector.tensor_tensor(size[:, :], size[:, :], product[:, :], ALU.max).then_inc(step, 1)
                    steps += 1
                    dve.wait_ge(step, steps)
                    nc.vector.scalar_tensor_tensor(out=gate, in0=sign[:, :], scalar=-1.0, in1=size[:, :],
                                                   op0=ALU.add, op1=ALU.mult).then_inc(taken, 1)
                    dve.wait_ge(taken, j + 1)
                else:
                    column = mem.column[:, 4 * layer + {0: 0, 1: 1, 3: 2, 4: 3}[n], :]
                    for k in range(KT):
                        done = nc.vector.scalar_tensor_tensor(
                            out=diag[:, :], in0=product[:, k * P:(k + 1) * P], scalar=1.0, in1=mem.ident[:, :],
                            op0=ALU.mult, op1=ALU.mult, accum_out=column[:, k:k + 1])
                        if k < KT - 1 or n in (1, 4):
                            done.then_inc(step, 1)
                            steps += 1
                            dve.wait_ge(step, steps)
                    if n in (1, 4):
                        done = nc.vector.tensor_scalar(column, column, 1.0, None, ALU.add)
                    done.then_inc(taken, 1)
                    dve.wait_ge(taken, j + 1)


class Counted:

    def __init__(self, sem, total):
        self.sem, self.total = sem, total

    def after(self, run, k):
        return self.sem, run * self.total + k


def layernorm_counts(nc, mem):
    pieces = NHALF * KT
    totals = {"stats_done": NT, "moments": NT, "y_done": 1, "root_done": 1, "rstd_done": 5, "normed_done": NT,
              "turned": pieces, "modulated": pieces, "hi_done": pieces, "lo_done": pieces}
    return [Counted(mem.semaphores.enter_context(nc.semaphore("ln_" + name)), n) for name, n in totals.items()]


def layernorm_phase(nc, mem, run, scale_col, shift_col):
    with ExitStack() as ctx:
        sb = lambda name, shape, dt=F32: ctx.enter_context(nc.sbuf_tensor(f"ln{run}_{name}", shape, dt))
        stats = sb("stats", [P, NT, 6])
        mean_var = sb("mean_var", [P, NT, 2])
        y, std, root = sb("y", [P, NT]), sb("std", [P, NT]), sb("root", [P, NT])
        newton, rstd = sb("newton", [P, NT]), sb("rstd", [P, NT])
        normed = sb("normed", [P, NT, D])
        h = sb("h", [P, 4, HALF])
        (stats_done, moments, y_done, root_done, rstd_done, normed_done,
         turned, modulated, hi_done, lo_done) = mem.layernorm_counts
        pieces = [(half, k) for half in range(NHALF) for k in range(KT)]
        block = ctx.enter_context(nc.Block())

        @block.vector
        def _(dve):
            for t in range(NT):
                nc.vector.bn_stats(stats[:, t, :], mem.x[:, t, :]).then_inc(stats_done.sem, 1)
            for t in range(NT):
                dve.wait_ge(*stats_done.after(run, t + 1))
                nc.vector.bn_aggr(mean_var[:, t, :], stats[:, t, :]).then_inc(moments.sem, 1)
            dve.wait_ge(*moments.after(run, NT))
            nc.vector.tensor_scalar(y[:, :], mean_var[:, :, 1], LN_EPS, None, ALU.add).then_inc(y_done.sem, 1)
            dve.wait_ge(*root_done.after(run, 1))
            nc.vector.reciprocal(root[:, :], std[:, :]).then_inc(rstd_done.sem, 1)
            dve.wait_ge(*rstd_done.after(run, 1))
            nc.vector.tensor_tensor(newton[:, :], root[:, :], root[:, :], ALU.mult).then_inc(rstd_done.sem, 1)
            dve.wait_ge(*rstd_done.after(run, 2))
            nc.vector.tensor_tensor(newton[:, :], newton[:, :], y[:, :], ALU.mult).then_inc(rstd_done.sem, 1)
            dve.wait_ge(*rstd_done.after(run, 3))
            nc.vector.tensor_scalar(newton[:, :], newton[:, :], -0.5, 1.5, ALU.mult, ALU.add).then_inc(rstd_done.sem, 1)
            dve.wait_ge(*rstd_done.after(run, 4))
            nc.vector.tensor_tensor(rstd[:, :], root[:, :], newton[:, :], ALU.mult).then_inc(rstd_done.sem, 1)
            dve.wait_ge(*rstd_done.after(run, 5))
            for t in range(NT):
                nc.vector.tensor_scalar(normed[:, t, :], mem.x[:, t, :], mean_var[:, t, 0:1], rstd[:, t:t + 1],
                                        ALU.subtract, ALU.mult).then_inc(normed_done.sem, 1)

            def low(i):
                half, k = pieces[i]
                dve.wait_ge(*hi_done.after(run, i + 1))
                nc.vector.tensor_tensor(mem.hT[1][:, k, half * HALF:(half + 1) * HALF], h[:, i % 4, :],
                                        mem.hT[0][:, k, half * HALF:(half + 1) * HALF].bitcast(F32),
                                        ALU.subtract).then_inc(lo_done.sem, 1)

            for i, (half, k) in enumerate(pieces):
                dve.wait_ge(*modulated.after(run, i + 1))
                nc.vector.tensor_copy(mem.hT[0][:, k, half * HALF:(half + 1) * HALF], h[:, i % 4, :]).then_inc(hi_done.sem, 1)
                if i:
                    low(i - 1)
            low(len(pieces) - 1)

        @block.tensor
        def _(pe):
            for i, (half, k) in enumerate(pieces):
                pe.wait_ge(*normed_done.after(run, TPH * (half + 1)))
                if i >= 4:
                    pe.wait_ge(*modulated.after(run, i - 3))
                for t in range(TPH):
                    last = nc.tensor.transpose(mem.bank[i % 4][:, t * P:(t + 1) * P],
                                               normed[:, half * TPH + t, k * P:(k + 1) * P], mem.ident[:, :])
                last.then_inc(turned.sem, 1)

        @block.scalar
        def _(act):
            act.wait_ge(*y_done.after(run, 1))
            nc.scalar.activation(std[:, :], y[:, :], ACT.Sqrt).then_inc(root_done.sem, 1)
            for i, (half, k) in enumerate(pieces):
                act.wait_ge(*turned.after(run, i + 1))
                if i >= 4:
                    act.wait_ge(*lo_done.after(run, i - 3))
                nc.scalar.activation(h[:, i % 4, :], mem.bank[i % 4][:, :], ACT.Identity,
                                     scale=scale_col[:, k:k + 1], bias=shift_col[:, k:k + 1]).then_inc(modulated.sem, 1)


def layer0_attention_phase(nc, mem, rope_dram, qw, scales):
    HH = HD0 // 2
    LAST = NKV0 - 1
    heads, tiles, halves = range(REP0), range(NT), range(NHALF)
    units = [(h, i) for h in heads for i in tiles]
    use6, use7 = [], []
    for h, i in units:
        if h > 0:
            use6.append(("o", h - 1, i))
            if i == 0:
                use7.append(("pv", h - 1, 1))
        if i == TPH:
            use7.append(("pv", h, 0))
        if h < REP0 - 1 and i in (0, 3):
            use6.append(("q", h + 1, i // 3))
    use7.append(("pv", REP0 - 1, 1))
    AHEAD6 = [("k", 0), ("k", 1), ("q", 0, 1), ("v", 1), ("vt", 1)]
    AHEAD7 = [("q", 0, 0), ("v", 0), ("vt", 0)]
    use6, use7 = use6 + AHEAD6, use7 + AHEAD7
    pieces = [(h, i, c) for h, i in units for c in range(i // TPH + 1)]
    weights = [("o", 0), ("q", 2), ("o", 1), ("q", 3), ("o", 2), ("o", 3), ("k", 0), ("v", 0), ("q", 0), ("q", 1)]
    AHEAD, RING = 4, 5
    AT_HOME = len(weights) - AHEAD
    roped_halves = [("q", h, b) for h in range(1, REP0) for b in halves] + [("k", b) for b in halves] + \
                   [("q", 0, b) for b in halves]
    ROPED_AHEAD = 4
    with ExitStack() as ctx:
        sem = lambda name: mem.semaphores.enter_context(nc.semaphore("a0_" + name))
        turns = lambda name, names: Turns(sem(name), names)
        sb = lambda name, shape, dt=F32: ctx.enter_context(nc.sbuf_tensor("a0_" + name, shape, dt))
        pair = lambda name, shape: (sb(name + "_hi", shape, F32R), sb(name + "_lo", shape, F32R))
        rope = sb("rope", [P, 2, S])
        raw, scale = sb("raw", [P, RING, D], I32), sb("scale", [P, RING, D])
        shifted, weight, with_gate = sb("shifted", [P, 2, D]), sb("weight", [P, D]), sb("with_gate", [P, D])
        zero = sb("zero", [P, 1])
        wkv = pair("wkv", [P, 2, KT, HD0])
        wq, wo = pair("wq", [P, 2, KT, HD0]), pair("wo", [P, 2, D])
        kT, qT = pair("kT", [P, S]), pair("qT", [P, 2, S])
        vT, v = sb("vT", [P, S]), sb("v", [P, NT, HD0])
        plain, exchanged, roped = sb("plain", [P, 2, HALF]), sb("exchanged", [P, 2, HALF]), sb("roped", [P, HALF])
        probs = sb("probs", [P, 2, S])
        probsT = [sb(f"probsT{b}", [P, TPH * (b + 1), HALF]) for b in halves]
        ctxT = pair("ctxT", [P, 2, S])
        neg_max, row_sum, row_inv = sb("neg_max", [P, 2, NT]), sb("row_sum", [P, 2, NT]), sb("row_inv", [P, 2, NT])

        rope_in, filled = sem("rope_in"), sem("filled")
        raw_in = [sem(f"raw_in{s}") for s in range(RING)]
        shift_done, scaled = turns("shift_done", weights), turns("scaled", weights)
        gated, hi_made, made = turns("gated", heads), turns("hi_made", weights), turns("made", weights)
        full6, full7 = turns("full6", use6), turns("full7", use7)
        scored = turns("scored", units)
        turned = turns("turned", pieces)
        last_output = turns("last_output", tiles)
        rope_mul, rope_sum = turns("rope_mul", roped_halves), turns("rope_sum", roped_halves)
        rope_hi, rope_lo = turns("rope_hi", roped_halves), turns("rope_lo", roped_halves)
        maxed = turns("maxed", units)
        values_split = turns("values_split", [(h, b) for h in heads for b in halves])
        v_done = turns("v_done", halves)
        inverted = turns("inverted", heads)
        output_added = turns("output_added", [(h, t) for h in heads for t in tiles])
        exped = turns("exped", units)
        turned_out = turns("turned_out", pieces)
        projected_out = turns("projected_out", roped_halves + [("v", b) for b in halves])
        ctx_hi = turns("ctx_hi", [(h, b) for h in heads for b in halves])
        score = mem.bank_pair
        turn_bank = mem.bank[4:6]
        bank6, bank7 = mem.bank[6], mem.bank[7]
        full = lambda use: full6 if use in use6 else full7
        bank = lambda use: bank6 if use in use6 else bank7
        half = lambda b: slice(b * HALF, (b + 1) * HALF)
        tile = lambda i: slice(i * P, (i + 1) * P)

        def taken_out(use):
            if use[0] == "o":
                return output_added, use[1:]
            if use[0] == "pv":
                return values_split, use[1:]
            if use[0] == "vt":
                return v_done, use[1]
            return projected_out, use

        def loaded(g, n):
            s = n % RING
            return raw_in[s], g * 64 + 32 * (n // RING) + 32 + (32 if s >= AT_HOME - RING else 0)

        def steps_before(counter, g, n, back):
            return counter.now(g, weights[n - back]) if n >= back else counter.last(g, weights[n - back])

        block = ctx.enter_context(nc.Block())

        @block.sync
        def _(sp):
            def load(n, group):
                name, h = weights[n]
                slot = n % RING
                if name == "o":
                    rows = bass.ds(group * (REP0 * HD0) + h * HD0, HD0)
                    sp.dma_start(raw[:, slot, :], qw["o"][rows, :]).then_inc(raw_in[slot], 16)
                    sp.dma_start(scale[:, slot, :], scales["o"][bass.ds(group * REP0 + h, 1), :].broadcast_to([P, D])
                                 ).then_inc(raw_in[slot], 16)
                    return
                cols = bass.ds(group * (REP0 * HD0) + h * HD0, HD0) if name == "q" else bass.ds(group * HD0, HD0)
                sp.dma_start(raw[:, slot, :].rearrange("p (k n) -> p k n", k=KT),
                             qw[name][:, cols].rearrange("(k p) n -> p k n", p=P)).then_inc(raw_in[slot], 16)
                sp.dma_start(scale[:, slot, :].rearrange("p (k n) -> p k n", k=KT),
                             scales[name][:, cols].unsqueeze(0).broadcast_to([P, KT, HD0])).then_inc(raw_in[slot], 16)

            def turn(g, last=False):
                for n in range(AT_HOME if last else len(weights)):
                    sp.wait_ge(*steps_before(scaled, g, n, RING))
                    load(n, g if n < AT_HOME else g + 1)

            for n in range(AT_HOME, len(weights)):
                load(n, 0)
            sp.dma_start(rope[:, :, :], rope_dram.rearrange("a p s -> p a s")).then_inc(rope_in, 16)
            with sp.Fori(0, LAST) as g:
                turn(g)
            turn(LAST, last=True)

        @block.gpsimd
        def _(pool):
            pool.memset(zero[:, :], 0.0).then_inc(filled, 1)
            for counter in (scaled, hi_made, made):
                counter.open(pool, AHEAD)
            gated.open(pool)
            pool.wait_ge(filled, 1)

            def make(g, n, prologue=False):
                name, h = key = weights[n]
                done = lambda counter: counter.last(0, key) if prologue else counter.now(g, key)
                hi, lo = ((part[:, n - AT_HOME, :, :] for part in wkv) if name in "kv" else
                          (part[:, h % 2] for part in (wq if name == "q" else wo)))
                flat = lambda a: a.rearrange("p k n -> p (k n)") if len(a.shape) == 3 else a
                pool.wait_ge(*done(shift_done))
                pool.tensor_tensor(weight[:, :], shifted[:, n % 2, :], scale[:, n % RING, :], ALU.mult).then_inc(scaled.sem, 1)
                pool.wait_ge(*done(scaled))
                whole = weight
                if name == "o":
                    pool.tensor_tensor(with_gate[:, :], weight[:, :], mem.gate[:, 0, :], ALU.mult).then_inc(gated.sem, 1)
                    pool.wait_ge(*gated.now(g, h))
                    whole = with_gate
                if not prologue:
                    if name in "kv":
                        use = (name, 1)
                        pool.wait_ge(*full(use).last(g, use))
                    elif name == "o":
                        if h >= 2:
                            pool.wait_ge(*full6.now(g, ("o", h - 2, NT - 1)))
                        elif h == 1:
                            pool.wait_ge(*last_output.last(g, NT - 1))
                        else:
                            pool.wait_ge(*full6.last(g, ("o", 2, NT - 1)))
                    elif h == 0:
                        pool.wait_ge(*full6.now(g, ("q", 2, 1)))
                    else:
                        use = ("q", (h - 2) % REP0, 1)
                        pool.wait_ge(*(full6.now(g, use) if h != 2 else full6.last(g, use)))
                pool.tensor_tensor(flat(hi), whole[:, :], zero[:, :].broadcast_to([P, D]), ALU.add).then_inc(hi_made.sem, 1)
                pool.wait_ge(*done(hi_made))
                pool.tensor_tensor(flat(lo), whole[:, :], flat(hi).bitcast(F32), ALU.subtract).then_inc(made.sem, 1)
                pool.wait_ge(*done(made))

            for n in range(AT_HOME, len(weights)):
                make(0, n, prologue=True)
            with pool.Fori(0, LAST) as g:
                for n in range(len(weights)):
                    make(g, n)
            for n in range(AT_HOME):
                make(LAST, n)

        @block.tensor
        def _(pe):
            full6.open(pe, len(AHEAD6))
            full7.open(pe, len(AHEAD7))
            for counter in (scored, turned, last_output):
                counter.open(pe)

            def wait_free(g, use, before_loop=False):
                uses = use6 if use in use6 else use7
                n = uses.index(use)
                counter, name = taken_out(uses[n - 1])
                if before_loop:
                    if use not in (AHEAD6[0], AHEAD7[0]):
                        pe.wait_ge(*counter.last(0, name))
                else:
                    pe.wait_ge(*(counter.now(g, name) if n else counter.last(g, name)))

            def project(g, use, w, slot, b, before_loop=False):
                wait_free(g, use, before_loop)
                for k in range(KT):
                    last = split_products(nc.tensor, bank(use)[:, :], [part[:, slot, k, :] for part in w],
                                          [part[:, k, half(b)] for part in mem.hT], k == 0, k == KT - 1)
                last.then_inc(full(use).sem, 1)

            def made_before(g, name, before_loop):
                pe.wait_ge(*(made.last(0, name) if before_loop else made.now(g, name)))

            def turn_v(g, b, before_loop=False):
                use = ("vt", b)
                pe.wait_ge(*(projected_out.last(0, ("v", b)) if before_loop else projected_out.now(g, ("v", b))))
                wait_free(g, use, before_loop)
                for t in range(TPH):
                    last = nc.tensor.transpose(bank(use)[:, tile(t)], vT[:, tile(b * TPH + t)], mem.ident[:, :])
                last.then_inc(full(use).sem, 1)

            made_before(0, ("k", 0), True)
            for b in halves:
                project(0, ("k", b), wkv, 0, b, True)
            made_before(0, ("v", 0), True)
            made_before(0, ("q", 0), True)
            for b in halves:
                project(0, ("q", 0, b), wq, 0, b, True)
            for b in halves:
                project(0, ("v", b), wkv, 1, b, True)
            for b in halves:
                turn_v(0, b, True)

            def turn(g, last_turn=False):
                def scores(u):
                    h, i = units[u]
                    if i % TPH == 0:
                        name = ("q", h, i // TPH)
                        pe.wait_ge(*(rope_lo.now(g, name) if h else rope_lo.last(g, name)))
                        if h == 0:
                            pe.wait_ge(*rope_lo.last(g, ("k", i // TPH)))
                    pe.wait_ge(*(exped.now(g, units[u - 2]) if u >= 2 else exped.last(g, units[u - 2])))
                    out = score[i % 2]
                    for c in range(i // TPH + 1):
                        keys = slice(c * HALF, min((c + 1) * HALF, (i + 1) * P))
                        diagonal = c == i // TPH
                        last = split_products(nc.tensor, out[:, keys], [part[:, h % 2, tile(i)] for part in qT],
                                              [part[:, keys] for part in kT], True, not diagonal)
                        if diagonal:
                            last = nc.tensor.matmul(out[:, tile(i)], mem.ident_bf[:, :], mem.causal[:, :],
                                                    start=False, stop=True)
                    last.then_inc(scored.sem, 1)

                def turn_probs(u):
                    h, i = units[u]
                    pe.wait_ge(*exped.now(g, (h, i)))
                    for c in range(i // TPH + 1):
                        n = pieces.index((h, i, c))
                        if n < 2:
                            pe.wait_ge(*output_added.last(g, (REP0 - 1, NT - 2 + n)))
                        else:
                            pe.wait_ge(*turned_out.now(g, pieces[n - 2]))
                        for j in range(c * TPH, min((c + 1) * TPH, i + 1)):
                            last = nc.tensor.transpose(turn_bank[n % 2][:, tile(j - c * TPH)], probs[:, i % 2, tile(j)],
                                                       mem.ident[:, :])
                        last.then_inc(turned.sem, 1)

                def values(h, b):
                    use = ("pv", h, b)
                    wait_free(g, use)
                    if h == 0:
                        pe.wait_ge(*v_done.last(g, b))
                    pe.wait_ge(*turned_out.now(g, (h, TPH * (b + 1) - 1, b)))
                    keys = TPH * (b + 1)
                    for j in range(keys):
                        first = max(0, j - TPH * b) * P
                        last = nc.tensor.matmul(bank7[:, first:HALF], v[:, j, :], probsT[b][:, j, first:HALF],
                                                start=(j == 0), stop=(j == keys - 1))
                    last.then_inc(full7.sem, 1)

                def output(h, t):
                    if t % TPH == 0:
                        pe.wait_ge(*values_split.now(g, (h, t // TPH)))
                    if t == 0:
                        pe.wait_ge(*made.now(g, ("o", h)))
                    if h < REP0 - 1:
                        wait_free(g, ("o", h, t))
                        out, done = bank6, full6
                    else:
                        pe.wait_ge(*(output_added.now(g, (h, t - 2)) if t >= 2 else turned_out.now(g, pieces[t - 2])))
                        out, done = turn_bank[t % 2], last_output
                    split_products(nc.tensor, out[:, :], [part[:, h % 2, tile(t)] for part in ctxT],
                                   [part[:, h % 2, :] for part in wo], True, True).then_inc(done.sem, 1)

                scores(0)
                for u, (h, i) in enumerate(units):
                    if u < len(units) - 1:
                        scores(u + 1)
                    if h > 0:
                        output(h - 1, i)
                        if i == 0:
                            values(h - 1, 1)
                    if i == TPH:
                        values(h, 0)
                    turn_probs(u)
                    if h < REP0 - 1 and i in (0, 3):
                        if i == 0:
                            pe.wait_ge(*(made.now if h else made.last)(g, ("q", h + 1)))
                        project(g, ("q", h + 1, i // 3), wq, (h + 1) % 2, i // 3)
                o = REP0 - 1
                if last_turn:
                    values(o, 1)
                    for t in tiles:
                        output(o, t)
                    return
                made_before(g, ("k", 0), False)
                project(g, ("k", 0), wkv, 0, 0)
                values(o, 1)
                project(g, ("k", 1), wkv, 0, 1)
                made_before(g, ("q", 0), False)
                project(g, ("q", 0, 0), wq, 0, 0)
                output(o, 0)
                project(g, ("q", 0, 1), wq, 0, 1)
                output(o, 1)
                project(g, ("v", 0), wkv, 1, 0)
                output(o, 2)
                project(g, ("v", 1), wkv, 1, 1)
                output(o, 3)
                output(o, 4)
                turn_v(g, 0)
                output(o, 5)
                turn_v(g, 1)
                output(o, 6)
                output(o, 7)

            with pe.Fori(0, LAST) as g:
                turn(g)
            turn(LAST, last_turn=True)

        @block.vector
        def _(dve):
            for counter in (rope_mul, rope_sum, rope_hi, rope_lo):
                counter.open(dve, ROPED_AHEAD)
            for counter in (maxed, values_split, inverted, output_added):
                counter.open(dve)
            dve.wait_ge(rope_in, 16)

            def rope_steps(g, name, before_loop=False):
                n, b = roped_halves.index(name), name[-1]
                done = lambda counter: counter.last(0, name) if before_loop else counter.now(g, name)
                hi, lo = ([part[:, half(b)] for part in kT] if name[0] == "k" else
                          [part[:, name[1] % 2, half(b)] for part in qT])
                x, y = plain[:, n % 2, :], exchanged[:, n % 2, :]

                def multiply():
                    dve.wait_ge(*done(projected_out))
                    nc.vector.tensor_tensor(x, x, rope[:, 0, half(b)], ALU.mult)
                    nc.vector.tensor_tensor(y, y, rope[:, 1, half(b)], ALU.mult).then_inc(rope_mul.sem, 1)

                def add():
                    dve.wait_ge(*done(rope_mul))
                    if not before_loop:
                        dve.wait_ge(*(rope_lo.now if n else rope_lo.last)(g, roped_halves[n - 1]))
                    elif n > len(roped_halves) - ROPED_AHEAD:
                        dve.wait_ge(*rope_lo.last(0, roped_halves[n - 1]))
                    nc.vector.tensor_tensor(roped[:, :], x, y, ALU.add).then_inc(rope_sum.sem, 1)

                def high():
                    dve.wait_ge(*done(rope_sum))
                    nc.vector.tensor_copy(hi, roped[:, :]).then_inc(rope_hi.sem, 1)

                def low():
                    dve.wait_ge(*done(rope_hi))
                    nc.vector.tensor_tensor(lo, roped[:, :], hi.bitcast(F32), ALU.subtract).then_inc(rope_lo.sem, 1)

                return multiply, add, high, low

            def take_v(g, b, before_loop=False):
                use = ("vt", b)
                dve.wait_ge(*(full(use).last(0, use) if before_loop else full(use).now(g, use)))
                nc.vector.tensor_copy(v[:, b * TPH:(b + 1) * TPH, :],
                                      bank(use).rearrange("p (t d) -> p t d", t=TPH)).then_inc(v_done.sem, 1)

            for name in roped_halves[-ROPED_AHEAD:]:
                for step in rope_steps(0, name, True):
                    step()
            for b in halves:
                take_v(0, b, True)

            def turn(g, last_turn=False):
                def maximum(u):
                    h, i = units[u]
                    dve.wait_ge(*scored.now(g, (h, i)))
                    nc.vector.reduce_max(neg_max[:, h % 2, i:i + 1], score[i % 2][:, 0:(i + 1) * P], AX.X,
                                         negate=True).then_inc(maxed.sem, 1)

                def invert(h):
                    dve.wait_ge(*exped.now(g, (h, NT - 1)))
                    nc.vector.reciprocal(row_inv[:, h % 2, :], row_sum[:, h % 2, :]).then_inc(inverted.sem, 1)
                    dve.wait_ge(*inverted.now(g, h))

                def add_output(h, t):
                    use = ("o", h, t)
                    last_head = h == REP0 - 1
                    dve.wait_ge(*(last_output.now(g, t) if last_head else full6.now(g, use)))
                    nc.vector.scalar_tensor_tensor(out=mem.x[:, t, :], in0=(turn_bank[t % 2] if last_head else bank6)[:, :],
                                                   scalar=row_inv[:, h % 2, t:t + 1], in1=mem.x[:, t, :],
                                                   op0=ALU.mult, op1=ALU.add).then_inc(output_added.sem, 1)

                def split_values(h, b):
                    dve.wait_ge(*ctx_hi.now(g, (h, b)))
                    nc.vector.tensor_tensor(ctxT[1][:, h % 2, half(b)], bank7[:, :],
                                            ctxT[0][:, h % 2, half(b)].bitcast(F32), ALU.subtract
                                            ).then_inc(values_split.sem, 1)

                maximum(0)
                for u, (h, i) in enumerate(units):
                    if u < len(units) - 1:
                        maximum(u + 1)
                    if i == 0 and h > 0:
                        invert(h - 1)
                    if h > 0:
                        add_output(h - 1, i)
                        if i == 1:
                            split_values(h - 1, 1)
                    if i == TPH + 1:
                        split_values(h, 0)
                    if i == 0 and h > 0:
                        rope_steps(g, ("q", h, 1))[3]()
                    if h < REP0 - 1:
                        first, second = rope_steps(g, ("q", h + 1, 0)), rope_steps(g, ("q", h + 1, 1))
                        for step in {2: first[0:1], 3: first[1:2], 4: first[2:3], 5: first[3:4] + second[0:1],
                                     6: second[1:2], 7: second[2:3]}.get(i, ()):
                            step()
                o = REP0 - 1
                invert(o)
                if last_turn:
                    split_values(o, 1)
                    for t in tiles:
                        add_output(o, t)
                    return
                k0, k1, q0, q1 = (rope_steps(g, name) for name in roped_halves[-ROPED_AHEAD:])
                for step in k0:
                    step()
                split_values(o, 1)
                for step in k1:
                    step()
                q0[0]()
                q0[1]()
                add_output(o, 0)
                q0[2]()
                q1[0]()
                q0[3]()
                q1[1]()
                add_output(o, 1)
                q1[2]()
                add_output(o, 2)
                q1[3]()
                add_output(o, 3)
                add_output(o, 4)
                take_v(g, 0)
                add_output(o, 5)
                take_v(g, 1)
                add_output(o, 6)
                add_output(o, 7)

            with dve.Fori(0, LAST) as g:
                turn(g)
            turn(LAST, last_turn=True)

        @block.scalar
        def _(act):
            for counter in (exped, turned_out, ctx_hi):
                counter.open(act)
            projected_out.open(act, ROPED_AHEAD + NHALF)
            shift_done.open(act, AHEAD)

            def shift(n):
                nc.scalar.activation(shifted[:, n % 2, :], raw[:, n % RING, :], ACT.Copy, bias=-ZERO_POINT
                                     ).then_inc(shift_done.sem, 1)

            def take_projected(g, name, before_loop=False):
                out, b = bank(name), name[-1]
                if before_loop:
                    act.wait_ge(*full(name).last(0, name))
                else:
                    act.wait_ge(*full(name).now(g, name))
                if name[0] == "v":
                    nc.scalar.copy(vT[:, half(b)], out[:, :]).then_inc(projected_out.sem, 1)
                    return
                n = roped_halves.index(name)
                if before_loop:
                    if n >= len(roped_halves) - ROPED_AHEAD + 2:
                        act.wait_ge(*rope_sum.last(0, roped_halves[n - 2]))
                else:
                    act.wait_ge(*(rope_sum.now(g, roped_halves[n - 2]) if n >= 2 else
                                  rope_sum.last(g, roped_halves[n - 2])))
                factor = SCALE0 if name[0] == "q" else 1.0
                nc.scalar.activation(plain[:, n % 2, :], out[:, :], ACT.Copy, scale=factor)
                nc.scalar.activation(exchanged[0:HH, n % 2, :], out[HH:HD0, :], ACT.Copy, scale=factor)
                nc.scalar.activation(exchanged[HH:HD0, n % 2, :], out[0:HH, :], ACT.Copy, scale=factor
                                     ).then_inc(projected_out.sem, 1)

            for n in range(AT_HOME, len(weights)):
                act.wait_ge(raw_in[n % RING], 32)
                if n >= AT_HOME + 2:
                    act.wait_ge(*scaled.last(0, weights[n - 2]))
                shift(n)
            for name in roped_halves[-ROPED_AHEAD:] + [("v", b) for b in halves]:
                take_projected(0, name, True)

            def turn(g, last_turn=False):
                def shift_next(n):
                    act.wait_ge(*loaded(g, n))
                    act.wait_ge(*steps_before(scaled, g, n, 2))
                    shift(n)

                def exponential(u):
                    h, i = units[u]
                    act.wait_ge(*maxed.now(g, (h, i)))
                    if i == 0:
                        act.wait_ge(*(inverted.now(g, h - 2) if h >= 2 else inverted.last(g, h - 2 + REP0)))
                    nc.scalar.activation(probs[:, i % 2, 0:(i + 1) * P], score[i % 2][:, 0:(i + 1) * P], ACT.Exp,
                                         bias=neg_max[:, h % 2, i:i + 1],
                                         accum_out=row_sum[:, h % 2, i:i + 1]).then_inc(exped.sem, 1)

                def take_turned(u):
                    h, i = units[u]
                    b = i // TPH
                    if i % TPH == 0:
                        act.wait_ge(*(full7.now(g, ("pv", h - 1, b)) if h else full7.last(g, ("pv", REP0 - 1, b))))
                    for c in range(b + 1):
                        n = pieces.index((h, i, c))
                        act.wait_ge(*turned.now(g, (h, i, c)))
                        keys = min(TPH, i + 1 - c * TPH)
                        nc.scalar.copy(probsT[b][:, c * TPH:c * TPH + keys, tile(i % TPH)],
                                       turn_bank[n % 2][:, 0:keys * P].rearrange("p (j q) -> p j q", j=keys)
                                       ).then_inc(turned_out.sem, 1)

                def high_values(h, b):
                    act.wait_ge(*full7.now(g, ("pv", h, b)))
                    nc.scalar.copy(ctxT[0][:, h % 2, half(b)], bank7[:, :]).then_inc(ctx_hi.sem, 1)

                n = 0
                exponential(0)
                for u, (h, i) in enumerate(units):
                    if u < len(units) - 1:
                        exponential(u + 1)
                    if i == 0 and h > 0:
                        high_values(h - 1, 1)
                    if i == TPH:
                        high_values(h, 0)
                    take_turned(u)
                    if h < REP0 - 1 and i in (0, 3):
                        take_projected(g, ("q", h + 1, i // 3))
                    if i in (1, 2, 5) and n < (3, 5, 8, 10)[h] and n < (AT_HOME if last_turn else len(weights)):
                        shift_next(n)
                        n += 1
                if not last_turn:
                    take_projected(g, ("k", 0))
                high_values(REP0 - 1, 1)
                if not last_turn:
                    for name in (("k", 1), ("q", 0, 0), ("q", 0, 1), ("v", 0), ("v", 1)):
                        take_projected(g, name)

            with act.Fori(0, LAST) as g:
                turn(g)
            turn(LAST, last_turn=True)


def layer0_ffn_phase(nc, mem, w):
    slots = range(2)
    kts = range(KT)
    with ExitStack() as ctx:
        sem = lambda name: mem.semaphores.enter_context(nc.semaphore("f0_" + name))
        turns = lambda name, names: Turns(sem(name), names)
        sb = lambda name, shape, dt=F32: ctx.enter_context(nc.sbuf_tensor("f0_" + name, shape, dt))
        pair = lambda name, shape: (sb(name + "_hi", shape, F32R), sb(name + "_lo", shape, F32R))
        raw = sb("raw", [P, 2, 3, D])
        raw_b = sb("raw_b", [P, 2, 2, RANK0])
        low_a = sb("low_a", [RANK0, 2, D])
        down_a = sb("down_a", [RANK0, 2, P])
        down_b, down_bT = sb("down_b", [P, KT, RANK0]), sb("down_bT", [RANK0, D])
        low_bT = sb("low_bT", [RANK0, 2, 2, P])
        wT = pair("wT", [P, 2, 2, KT, P])
        downT = pair("downT", [P, NF, D])
        down_full = sb("down_full", [P, D])
        hidden = sb("hidden", [P, NF, S])
        act_t = pair("act_t", [P, 2, NF, P])

        low_in, w_in = sem("low_in"), [sem(f"w_in{s}") for s in slots]
        bT_turned, wT_turned, projected = turns("bT_turned", slots), turns("wT_turned", [(s, m) for s in slots for m in (2, 0, 1)]), turns("projected", slots)
        down_bT_turned, down_bT_out = sem("down_bT_turned"), sem("down_bT_out")
        bT_out, w_hi, silu_done = turns("bT_out", slots), turns("w_hi", [(s, m) for s in slots for m in range(2)]), turns("silu_done", slots)
        w_split, down_gated = turns("w_split", [(s, m) for s in slots for m in (2, 0, 1)]), turns("down_gated", slots)
        down_hi, hidden_done = turns("down_hi", slots), turns("hidden_done", slots)
        cleared, act_hi, act_split, produced, added = sem("cleared"), sem("act_hi"), sem("act_split"), sem("produced"), sem("added")
        wT_bank, small_bank = mem.bank[0:3], mem.bank[3]
        out_pair = [mem.bank_pair4(0), mem.bank_pair4(1)]
        half = lambda b: slice(b * HALF, (b + 1) * HALF)
        LAST = NF - 1
        rows_of = lambda f: HID_LAST if isinstance(f, int) and f == LAST else P
        block = ctx.enter_context(nc.Block())

        def tiles_in_turn(g):
            return [(s, g * 2 + s) for s in slots] if not isinstance(g, int) or g < LAST // 2 else [(0, LAST)]

        @block.sync
        def _(sp):
            sp.dma_start(low_a[:, 0, :], w["gate_a"][:, :]).then_inc(low_in, 16)
            sp.dma_start(low_a[:, 1, :], w["up_a"][:, :]).then_inc(low_in, 16)
            sp.dma_start(down_b[:, :, :], w["down_b"].rearrange("(k p) r -> p k r", p=P)).then_inc(low_in, 16)

            def load(g):
                for s, f in tiles_in_turn(g):
                    r = rows_of(f)
                    rows = bass.ds(f * P, r)
                    sp.wait_ge(*wT_turned.last(g, (s, 1)))
                    sp.dma_start(raw[:r, s, 0, :], w["gate_w"][rows, :]).then_inc(w_in[s], 16)
                    sp.dma_start(raw[:r, s, 1, :], w["up_w"][rows, :]).then_inc(w_in[s], 16)
                    sp.dma_start(raw[:, s, 2, 0:KT * r].rearrange("p (k n) -> p k n", k=KT),
                                 w["down_w"][:, rows].rearrange("(k p) n -> p k n", p=P)).then_inc(w_in[s], 16)
                    sp.dma_start(raw_b[:r, s, 0, :], w["gate_b"][rows, :]).then_inc(w_in[s], 16)
                    sp.dma_start(raw_b[:r, s, 1, :], w["up_b"][rows, :]).then_inc(w_in[s], 16)
                    sp.dma_start(down_a[:, s, 0:r], w["down_a"][:, rows]).then_inc(w_in[s], 16)

            with sp.Fori(0, LAST // 2) as g:
                load(g)
            load(LAST // 2)

        @block.gpsimd
        def _(pool):
            pool.memset(hidden[:, LAST, :], 0.0).then_inc(cleared, 1)

        @block.tensor
        def _(pe):
            for counter in (bT_turned, wT_turned, projected):
                counter.open(pe)
            pe.wait_ge(low_in, 48)
            for k in kts:
                last = nc.tensor.transpose(small_bank[:RANK0, k * P:(k + 1) * P], down_b[:, k, :], mem.ident[:, :])
            last.then_inc(down_bT_turned, 1)
            pe.wait_ge(down_bT_out, 1)

            def prepare(g, s, f):
                r = rows_of(f)
                pe.wait_ge(w_in[s], g * 96 + 96)
                pe.wait_ge(*(bT_out.now(g, 0) if s else bT_out.last(g, 1)))
                for m in range(2):
                    last = nc.tensor.transpose(small_bank[:RANK0, m * P:m * P + r], raw_b[:r, s, m, :],
                                               mem.ident[:r, :r])
                last.then_inc(bT_turned.sem, 1)
                for m in (2, 0, 1):
                    pe.wait_ge(*(w_split.now(g, (0, m)) if s else w_split.last(g, (1, m))))
                    if m == 2:
                        for k in kts:
                            nc.tensor.matmul(wT_bank[2][:r, k * P:(k + 1) * P], raw[:, s, 2, k * r:(k + 1) * r],
                                             mem.ident[:, :], is_transpose=True, start=(k == 0), stop=False)
                        last = nc.tensor.matmul(wT_bank[2][:r, :], down_a[:, s, 0:r], down_bT[:, :],
                                                start=False, stop=True)
                    else:
                        if m == 0:
                            pe.wait_ge(*bT_out.now(g, s))
                        for k in kts:
                            nc.tensor.matmul(wT_bank[m][:, k * P:k * P + r], raw[:r, s, m, k * P:(k + 1) * P],
                                             mem.ident[:r, :r], is_transpose=True, start=(k == 0), stop=False)
                        for k in kts:
                            last = nc.tensor.matmul(wT_bank[m][:, k * P:k * P + r], low_a[:, m, k * P:(k + 1) * P],
                                                    low_bT[:, s, m, 0:r], start=False, stop=(k == KT - 1))
                    last.then_inc(wT_turned.sem, 1)

            def project(g, s, f):
                r = rows_of(f)
                pe.wait_ge(*w_split.now(g, (s, 1)))
                pe.wait_ge(*(hidden_done.now(g, 0) if s else hidden_done.last(g, 1)))
                for m in range(2):
                    for b in range(NHALF):
                        for k in kts:
                            last = split_products(nc.tensor, out_pair[m][:r, half(b)], [part[:, s, m, k, 0:r] for part in wT],
                                                  [part[:, k, half(b)] for part in mem.hT], k == 0, k == KT - 1)
                last.then_inc(projected.sem, 1)

            def turn(g):
                for s, f in tiles_in_turn(g):
                    prepare(g, s, f)
                    project(g, s, f)

            with pe.Fori(0, LAST // 2) as g:
                turn(g)
            turn(LAST // 2)
            for t in range(NT):
                pe.wait_ge(act_split, t + 1)
                if t >= 2:
                    pe.wait_ge(added, t - 1)
                for f in range(NF):
                    r = rows_of(f)
                    last = split_products(nc.tensor, mem.bank[t % 2][:, :], [part[:r, t % 2, f, :] for part in act_t],
                                          [part[:r, f, :] for part in downT], f == 0, f == NF - 1)
                last.then_inc(produced, 1)

        @block.scalar
        def _(act):
            for counter in (bT_out, w_hi, silu_done):
                counter.open(act)
            act.wait_ge(cleared, 1)
            act.wait_ge(down_bT_turned, 1)
            nc.scalar.copy(down_bT[:, :], small_bank[:RANK0, :]).then_inc(down_bT_out, 1)

            def turn(g):
                for s, f in tiles_in_turn(g):
                    r = rows_of(f)
                    act.wait_ge(*bT_turned.now(g, s))
                    nc.scalar.copy(low_bT[:, s, :, 0:r],
                                   small_bank[:RANK0, 0:2 * P].rearrange("r (m n) -> r m n", m=2)[:, :, 0:r]
                                   ).then_inc(bT_out.sem, 1)
                    for m in range(2):
                        act.wait_ge(*wT_turned.now(g, (s, m)))
                        nc.scalar.copy(wT[0][:, s, m, :, 0:r],
                                       wT_bank[m].rearrange("p (k n) -> p k n", k=KT)[:, :, 0:r]).then_inc(w_hi.sem, 1)
                    act.wait_ge(*projected.now(g, s))
                    nc.scalar.activation(hidden[:r, bass.ds(f, 1), :], out_pair[0][:r, :], ACT.Silu).then_inc(silu_done.sem, 1)

            with act.Fori(0, LAST // 2) as g:
                turn(g)
            turn(LAST // 2)

        @block.vector
        def _(dve):
            for counter in (w_split, down_gated, down_hi, hidden_done):
                counter.open(dve)
            dve.wait_ge(cleared, 1)

            def turn(g):
                for s, f in tiles_in_turn(g):
                    r = rows_of(f)
                    at = bass.ds(f, 1)
                    dve.wait_ge(*wT_turned.now(g, (s, 2)))
                    nc.vector.tensor_tensor(down_full[:r, :], wT_bank[2][:r, :], mem.gate[:r, 1, :],
                                            ALU.mult).then_inc(down_gated.sem, 1)
                    dve.wait_ge(*down_gated.now(g, s))
                    nc.vector.tensor_copy(downT[0][:r, at, :], down_full[:r, :]).then_inc(down_hi.sem, 1)
                    dve.wait_ge(*down_hi.now(g, s))
                    nc.vector.tensor_tensor(downT[1][:r, at, :], down_full[:r, :],
                                            downT[0][:r, at, :].bitcast(F32), ALU.subtract).then_inc(w_split.sem, 1)
                    for m in range(2):
                        dve.wait_ge(*w_hi.now(g, (s, m)))
                        nc.vector.tensor_tensor(wT[1][:, s, m, :, 0:r],
                                                wT_bank[m].rearrange("p (k n) -> p k n", k=KT)[:, :, 0:r],
                                                wT[0][:, s, m, :, 0:r].bitcast(F32), ALU.subtract
                                                ).then_inc(w_split.sem, 1)
                    dve.wait_ge(*silu_done.now(g, s))
                    nc.vector.tensor_tensor(hidden[:r, at, :], out_pair[1][:r, :], hidden[:r, at, :], ALU.mult
                                            ).then_inc(hidden_done.sem, 1)

            with dve.Fori(0, LAST // 2) as g:
                turn(g)
            turn(LAST // 2)
            dve.wait_ge(*hidden_done.now(LAST // 2, 0))

            def add(t):
                dve.wait_ge(produced, t + 1)
                nc.vector.tensor_tensor(mem.x[:, t, :], mem.bank[t % 2][:, :], mem.x[:, t, :], ALU.add).then_inc(added, 1)

            for t in range(NT):
                part = hidden[:, :, t * P:(t + 1) * P]
                nc.vector.tensor_copy(act_t[0][:, t % 2, :, :], part).then_inc(act_hi, 1)
                dve.wait_ge(act_hi, t + 1)
                nc.vector.tensor_tensor(act_t[1][:, t % 2, :, :], part, act_t[0][:, t % 2, :, :].bitcast(F32),
                                        ALU.subtract).then_inc(act_split, 1)
                if t:
                    add(t - 1)
            add(NT - 1)


def layer1_qkv_phase(nc, mem, k1, v1, rope_dram, w_dram, b_dram):
    NC = QKV1 // P
    NH, NP = NH1 + NKV1, HD1 // 2
    QW = NH1 * HD1
    with ExitStack() as ctx:
        sem = lambda name: mem.semaphores.enter_context(nc.semaphore("p1_" + name))
        sb = lambda name, shape, dt=F32: ctx.enter_context(nc.sbuf_tensor("p1_" + name, shape, dt))
        raw = sb("raw", [P, NC, D])
        bias = sb("bias", [P, QKV1])
        rope = sb("rope", [P, NT, 2, NP])
        wT = (sb("wT_hi", [P, KT, QKV1], F32R), sb("wT_lo", [P, KT, QKV1], F32R))
        qkv = sb("qkv", [P, NT, QKV1])
        part = [sb(f"part{n}", [P, 2, NH, NP]) for n in range(4)]
        roped = sb("roped", [P, 2, NH, HD1])
        q1 = [mem.hT[n].rearrange("p k s -> p (k s)").rearrange("p (t d) -> p t d", t=NT) for n in range(2)]
        w_in, small_in = sem("w_in"), sem("small_in")
        wT_turned, w_hi, w_split = sem("wT_turned"), sem("w_hi"), sem("w_split")
        projected, biased, rotated, summed, hi_done, split = (sem("projected"), sem("biased"), sem("rotated"),
                                                              sem("summed"), sem("hi_done"), sem("split"))
        block = ctx.enter_context(nc.Block())

        @block.sync
        def _(sp):
            sp.dma_start(raw[:, :, :], w_dram.rearrange("(c p) d -> p c d", p=P)).then_inc(w_in, 16)
            sp.dma_start(bias[:, :], b_dram.unsqueeze(0).broadcast_to([P, QKV1])).then_inc(small_in, 16)
            sp.dma_start(rope[:, :, :, :], rope_dram.rearrange("(t p) a f -> p t a f", p=P)).then_inc(small_in, 16)

        @block.tensor
        def _(pe):
            pe.wait_ge(w_in, 16)
            for k in range(KT):
                if k >= 2:
                    pe.wait_ge(w_split, k - 1)
                for c in range(NC):
                    last = nc.tensor.transpose(mem.bank_pair[k % 2][:, c * P:(c + 1) * P],
                                               raw[:, c, k * P:(k + 1) * P], mem.ident[:, :])
                last.then_inc(wT_turned, 1)
            pe.wait_ge(w_split, KT)
            for t in range(NT):
                if t >= 2:
                    pe.wait_ge(biased, t - 1)
                for cols in (slice(0, HALF), slice(HALF, QKV1)):
                    for k in range(KT):
                        last = split_products(nc.tensor, mem.bank_pair4(t % 2)[:, cols],
                                              [a[:, k, t * P:(t + 1) * P] for a in mem.hT],
                                              [a[:, k, cols] for a in wT], k == 0, k == KT - 1)
                last.then_inc(projected, 1)

        @block.scalar
        def _(act):
            for k in range(KT):
                act.wait_ge(wT_turned, k + 1)
                nc.scalar.copy(wT[0][:, k, :], mem.bank_pair[k % 2][:, 0:QKV1]).then_inc(w_hi, 1)

        @block.vector
        def _(dve):
            for k in range(KT):
                dve.wait_ge(w_hi, k + 1)
                nc.vector.tensor_tensor(wT[1][:, k, :], mem.bank_pair[k % 2][:, 0:QKV1],
                                        wT[0][:, k, :].bitcast(F32), ALU.subtract).then_inc(w_split, 1)
            dve.wait_ge(small_in, 32)
            for t in range(NT):
                dve.wait_ge(projected, t + 1)
                nc.vector.tensor_tensor(qkv[:, t, :], mem.bank_pair4(t % 2)[:, 0:QKV1], bias[:, :], ALU.add
                                        ).then_inc(biased, 1)
            dve.wait_ge(biased, NT)

            def rotate(t):
                x = qkv[:, t, 0:QK1].rearrange("p (h f two) -> p h f two", two=2, f=NP)
                turn = [rope[:, t, n, :].unsqueeze(1).broadcast_to([P, NH, NP]) for n in range(2)]
                for n, (a, b) in enumerate(((0, 0), (1, 1), (0, 1), (1, 0))):
                    last = nc.vector.tensor_tensor(part[n][:, t % 2, :, :], x[:, :, :, a], turn[b], ALU.mult)
                last.then_inc(rotated, 1)
                nc.vector.tensor_copy(v1[:, t, :], qkv[:, t, QK1:QKV1])

            def combine(t):
                dve.wait_ge(rotated, t + 1)
                r = roped[:, t % 2, :, :]
                nc.vector.tensor_tensor(r[:, :, 0:NP], part[0][:, t % 2], part[1][:, t % 2], ALU.subtract)
                nc.vector.tensor_tensor(r[:, :, NP:HD1], part[2][:, t % 2], part[3][:, t % 2], ALU.add).then_inc(summed, 1)

            def high(t):
                dve.wait_ge(summed, t + 1)
                r = roped[:, t % 2, :, :].rearrange("p h d -> p (h d)")
                nc.vector.tensor_scalar(q1[0][:, t, :], r[:, 0:QW], SCALE1, None, ALU.mult)
                nc.vector.tensor_copy(k1[0][:, t, :], r[:, QW:QK1]).then_inc(hi_done, 1)

            def low(t):
                dve.wait_ge(hi_done, t + 1)
                r = roped[:, t % 2, :, :].rearrange("p h d -> p (h d)")
                nc.vector.scalar_tensor_tensor(out=q1[1][:, t, :], in0=r[:, 0:QW], scalar=SCALE1,
                                               in1=q1[0][:, t, :].bitcast(F32), op0=ALU.mult, op1=ALU.subtract)
                nc.vector.tensor_tensor(k1[1][:, t, :], r[:, QW:QK1], k1[0][:, t, :].bitcast(F32),
                                        ALU.subtract).then_inc(split, 1)

            rotate(0)
            for t in range(NT):
                combine(t)
                if t < NT - 1:
                    rotate(t + 1)
                high(t)
                low(t)
                dve.wait_ge(split, t + 1)


def layer1_attention_phase(nc, mem, k1, v1, attended):
    heads, tiles, halves = range(REP1), range(NT), range(NHALF)
    PARTS = 4
    STACK = PARTS * HD1
    PAIRS = REP1 // 2
    VW = 32
    units = [(h, i) for b in halves for h in heads for i in range(b * TPH, (b + 1) * TPH)]
    pieces = [(h, i, c) for h, i in units for c in range(i // TPH + 1)]
    by_vector = lambda piece: piece[1] >= TPH and piece[2] == 0
    stages = [("k", b) for b in halves] + [("q", n, b) for n in range(PAIRS) for b in halves]
    q1 = [mem.hT[n].rearrange("p k s -> p (k s)").rearrange("p (t d) -> p t d", t=NT) for n in range(2)]
    with ExitStack() as ctx:
        sem = lambda name: mem.semaphores.enter_context(nc.semaphore("a1_" + name))
        turns = lambda name, names: Turns(sem(name), names)
        sb = lambda name, shape, dt=F32: ctx.enter_context(nc.sbuf_tensor("a1_" + name, shape, dt))
        q_stack, k_stack = sb("q_stack", [P, NT, PAIRS, 2 * STACK]), sb("k_stack", [P, NT, 2 * STACK])
        v, nothing = sb("v", [P, NT, VW]), sb("nothing", [P, NT, HD1])
        qT, kT = sb("qT", [P, PAIRS, S], F32R), sb("kT", [P, 2, S], F32R)
        probs, probsT = sb("probs", [P, 2, S]), sb("probsT", [P, REP1, NT, HALF])
        ctxT = sb("ctxT", [P, HALF])
        neg_max, row_sum, row_inv = (sb("neg_max", [P, NT, REP1]), sb("row_sum", [P, NT, REP1]),
                                     sb("row_inv", [P, NT, REP1]))
        cleared = sem("cleared")
        stacked = turns("stacked", ["v", "k", "q"])
        stage_turned, stage_out = turns("stage_turned", stages), turns("stage_out", stages)
        scored, maxed, exped = turns("scored", units), turns("maxed", units), turns("exped", units)
        turned = turns("turned", pieces)
        out_act = turns("out_act", [p for p in pieces if not by_vector(p)])
        out_dve = turns("out_dve", [p for p in pieces if by_vector(p)])
        valued, ctx_out, ctx_turned = turns("valued", halves), turns("ctx_out", halves), turns("ctx_turned", halves)
        inverted, attended_done = turns("inverted", halves), turns("attended_done", halves)
        turned_out = lambda piece: out_dve if by_vector(piece) else out_act
        score, turn_bank, value_bank, ctx_bank = mem.bank_pair, mem.bank[4:6], mem.bank[6], mem.bank[7]
        tile = lambda i: slice(i * P, (i + 1) * P)
        half = lambda b: slice(b * HALF, (b + 1) * HALF)
        block = ctx.enter_context(nc.Block())

        @block.gpsimd
        def _(pool):
            pool.memset(v[:, :, :], 0.0).then_inc(cleared, 1)
            pool.memset(kT[:, :, :].bitcast(F32), 0.0).then_inc(cleared, 1)
            pool.memset(nothing[:, :, :], 0.0).then_inc(cleared, 1)
            stacked.open(pool)
            pool.wait_ge(cleared, 3)
            with pool.Fori(0, NKV1) as g:
                keys = bass.ds(g * HD1, HD1)
                pool.wait_ge(*valued.last(g, 1))
                pool.tensor_tensor(v[:, :, 0:HD1], v1[:, :, keys], nothing[:, :, :], ALU.add).then_inc(stacked.sem, 1)
                pool.wait_ge(*stage_turned.last(g, ("k", 1)))
                for n, of in enumerate((0, 0, 1, 1) * 2):
                    last = pool.tensor_tensor(k_stack[:, :, n * HD1:(n + 1) * HD1], k1[of][:, :, keys].bitcast(F32),
                                              nothing[:, :, :], ALU.add)
                last.then_inc(stacked.sem, 1)
                pool.wait_ge(*stage_turned.last(g, stages[-1]))
                for h in heads:
                    for n, of in enumerate((0, 1, 0, 1)):
                        at = (h % 2) * STACK + n * HD1
                        last = pool.tensor_tensor(q_stack[:, :, h // 2, at:at + HD1],
                                                  q1[of][:, :, bass.ds(g * (REP1 * HD1) + h * HD1, HD1)].bitcast(F32),
                                                  nothing[:, :, :], ALU.add)
                last.then_inc(stacked.sem, 1)

        @block.tensor
        def _(pe):
            for counter in (stage_turned, scored, turned, valued, ctx_turned):
                counter.open(pe)
            pe.wait_ge(cleared, 2)
            with pe.Fori(0, NKV1) as g:
                def stage(name):
                    n = stages.index(name)
                    out = (value_bank, ctx_bank)[n % 2]
                    if n >= 2:
                        pe.wait_ge(*stage_out.now(g, stages[n - 2]))
                    else:
                        pe.wait_ge(*(ctx_out, attended_done)[n].last(g, 1))
                    for t in range(TPH):
                        i = name[-1] * TPH + t
                        if name[0] == "k":
                            last = nc.tensor.transpose(out[:, tile(t)], k_stack[:, i, :], mem.ident[:, :])
                        else:
                            last = nc.tensor.transpose(out[:, tile(t)], q_stack[:, i, name[1], :], mem.ident[:, :])
                    last.then_inc(stage_turned.sem, 1)

                def scores(u):
                    h, i = units[u]
                    pe.wait_ge(*(exped.now(g, units[u - 2]) if u >= 2 else exped.last(g, units[u - 2])))
                    for c in range(i // TPH + 1):
                        keys = slice(c * HALF, min((c + 1) * HALF, (i + 1) * P))
                        diagonal = c == i // TPH
                        last = nc.tensor.matmul(score[u % 2][:, keys], qT[:, h // 2, tile(i)], kT[:, h % 2, keys],
                                                start=True, stop=not diagonal)
                        if diagonal:
                            last = nc.tensor.matmul(score[u % 2][:, tile(i)], mem.ident_bf[:, :], mem.causal[:, :],
                                                    start=False, stop=True)
                    last.then_inc(scored.sem, 1)

                def turn(u):
                    h, i = units[u]
                    pe.wait_ge(*exped.now(g, (h, i)))
                    for c in range(i // TPH + 1):
                        n = pieces.index((h, i, c))
                        before = pieces[n - 2]
                        pe.wait_ge(*(turned_out(before).now(g, before) if n >= 2 else
                                     turned_out(before).last(g, before)))
                        for j in range(c * TPH, min((c + 1) * TPH, i + 1)):
                            last = nc.tensor.transpose(turn_bank[n % 2][:, tile(j - c * TPH)], probs[:, u % 2, tile(j)],
                                                       mem.ident[:, :])
                        last.then_inc(turned.sem, 1)

                def values(b):
                    if b:
                        pe.wait_ge(*ctx_out.now(g, 0))
                    else:
                        pe.wait_ge(*stage_out.now(g, stages[-2]))
                        pe.wait_ge(*stacked.now(g, "v"))
                    done = [p for p in pieces if p[1] // TPH == b]
                    for counter, which in ((out_act, False), (out_dve, True)):
                        of = [p for p in done if by_vector(p) == which]
                        if of:
                            pe.wait_ge(*counter.now(g, of[-1]))
                    keys = TPH * (b + 1)
                    for j in range(keys):
                        first = max(0, j - TPH * b) * P
                        for h in heads:
                            last = nc.tensor.matmul(value_bank[h * VW:(h + 1) * VW, first:HALF], v[:, j, :],
                                                    probsT[:, h, j, first:HALF], start=(j == 0), stop=(j == keys - 1))
                    last.then_inc(valued.sem, 1)

                def turn_values(b):
                    pe.wait_ge(*ctx_out.now(g, b))
                    pe.wait_ge(*(attended_done.now(g, 0) if b else stage_out.now(g, stages[-1])))
                    for t in range(TPH):
                        last = nc.tensor.transpose(ctx_bank[:, tile(t)], ctxT[:, tile(t)], mem.ident[:, :])
                    last.then_inc(ctx_turned.sem, 1)

                for name in stages:
                    if name == ("k", 0):
                        pe.wait_ge(*stacked.now(g, "k"))
                    if name == ("q", 0, 0):
                        pe.wait_ge(*stacked.now(g, "q"))
                    stage(name)
                pe.wait_ge(*stage_out.now(g, stages[-1]))
                scores(0)
                for u in range(len(units)):
                    if u < len(units) - 1:
                        scores(u + 1)
                    turn(u)
                    if u == len(units) // 2 - 1:
                        values(0)
                    if u == len(units) // 2 + 1:
                        turn_values(0)
                values(1)
                turn_values(1)

        @block.vector
        def _(dve):
            for counter in (maxed, out_dve, inverted, attended_done):
                counter.open(dve)
            with dve.Fori(0, NKV1) as g:
                def maximum(u):
                    h, i = units[u]
                    dve.wait_ge(*scored.now(g, (h, i)))
                    nc.vector.reduce_max(neg_max[:, i, h:h + 1], score[u % 2][:, 0:(i + 1) * P], AX.X,
                                         negate=True).then_inc(maxed.sem, 1)

                def normalize(b):
                    tb = slice(b * TPH, (b + 1) * TPH)
                    dve.wait_ge(*exped.now(g, units[(b + 1) * len(units) // 2 - 1]))
                    nc.vector.reciprocal(row_inv[:, tb, :], row_sum[:, tb, :]).then_inc(inverted.sem, 1)
                    dve.wait_ge(*inverted.now(g, b))
                    dve.wait_ge(*ctx_turned.now(g, b))
                    for t in range(TPH):
                        i = b * TPH + t
                        last = nc.vector.tensor_tensor(
                            attended[:, i, bass.ds(g * (REP1 * HD1), REP1 * HD1)].rearrange("p (h d) -> p h d", h=REP1),
                            ctx_bank[:, tile(t)].rearrange("p (h d) -> p h d", h=REP1)[:, :, 0:HD1],
                            row_inv[:, i, :].unsqueeze(2).broadcast_to([P, REP1, HD1]), ALU.mult)
                    last.then_inc(attended_done.sem, 1)

                def take_turned(u):
                    h, i = units[u]
                    n = pieces.index((h, i, 0))
                    dve.wait_ge(*turned.now(g, (h, i, 0)))
                    nc.vector.tensor_copy(probsT[:, h, 0:TPH, tile(i % TPH)],
                                          turn_bank[n % 2].rearrange("p (j q) -> p j q", j=TPH)).then_inc(out_dve.sem, 1)

                maximum(0)
                for u in range(len(units)):
                    if u < len(units) - 1:
                        maximum(u + 1)
                    if units[u][1] >= TPH:
                        take_turned(u)
                    if u == len(units) // 2 + 1:
                        normalize(0)
                normalize(1)

        @block.scalar
        def _(act):
            for counter in (stage_out, exped, out_act, ctx_out):
                counter.open(act)
            act.wait_ge(cleared, 2)
            with act.Fori(0, NKV1) as g:
                def take_stage(name):
                    act.wait_ge(*stage_turned.now(g, name))
                    out = (value_bank, ctx_bank)[stages.index(name) % 2]
                    b = name[-1]
                    if name[0] == "k":
                        nc.scalar.copy(kT[0:STACK, 0, half(b)], out[0:STACK, :])
                        last = nc.scalar.copy(kT[STACK:P, 1, half(b)], out[STACK:P, :])
                    else:
                        last = nc.scalar.copy(qT[:, name[1], half(b)], out[:, :])
                    last.then_inc(stage_out.sem, 1)

                def exponential(u):
                    h, i = units[u]
                    if h == 0 and i % TPH == 0:
                        act.wait_ge(*inverted.last(g, i // TPH))
                    act.wait_ge(*maxed.now(g, (h, i)))
                    nc.scalar.activation(probs[:, u % 2, 0:(i + 1) * P], score[u % 2][:, 0:(i + 1) * P], ACT.Exp,
                                         bias=neg_max[:, i, h:h + 1],
                                         accum_out=row_sum[:, i, h:h + 1]).then_inc(exped.sem, 1)

                def take_turned(u):
                    h, i = units[u]
                    if h == 0 and i % TPH == 0:
                        act.wait_ge(*(valued.now(g, 0) if i else valued.last(g, 1)))
                    for c in range(i // TPH + 1):
                        piece = (h, i, c)
                        if by_vector(piece):
                            continue
                        act.wait_ge(*turned.now(g, piece))
                        keys = min(TPH, i + 1 - c * TPH)
                        nc.scalar.copy(probsT[:, h, c * TPH:c * TPH + keys, tile(i % TPH)],
                                       turn_bank[pieces.index(piece) % 2][:, 0:keys * P]
                                       .rearrange("p (j q) -> p j q", j=keys)).then_inc(out_act.sem, 1)

                def take_values(b):
                    act.wait_ge(*valued.now(g, b))
                    act.wait_ge(*(ctx_turned.now(g, 0) if b else ctx_turned.last(g, 1)))
                    nc.scalar.copy(ctxT[:, :], value_bank[:, :]).then_inc(ctx_out.sem, 1)

                for name in stages:
                    take_stage(name)
                exponential(0)
                for u in range(len(units)):
                    if u < len(units) - 1:
                        exponential(u + 1)
                    take_turned(u)
                    if u == len(units) // 2:
                        take_values(0)
                take_values(1)


def layer1_output_phase(nc, mem, attended, w_dram, b_dram):
    with ExitStack() as ctx:
        sem = lambda name: mem.semaphores.enter_context(nc.semaphore("o1_" + name))
        sb = lambda name, shape, dt=F32: ctx.enter_context(nc.sbuf_tensor("o1_" + name, shape, dt))
        raw, bias = sb("raw", [P, KT, D]), sb("bias", [P, D])
        gated = sb("gated", [P, KT, D])
        wT = (sb("wT_hi", [P, KT, D], F32R), sb("wT_lo", [P, KT, D], F32R))
        aT = mem.hT
        w_in, b_in = sem("w_in"), sem("b_in")
        w_turned, w_gated, w_hi, w_split = sem("w_turned"), sem("w_gated"), sem("w_hi"), sem("w_split")
        a_turned, a_hi, a_split = sem("a_turned"), sem("a_hi"), sem("a_split")
        bias_gated, biased, produced, added = sem("bias_gated"), sem("biased"), sem("produced"), sem("added")
        pieces = [(half, k) for half in range(NHALF) for k in range(KT)]
        block = ctx.enter_context(nc.Block())

        @block.sync
        def _(sp):
            sp.dma_start(raw[:, :, :], w_dram.rearrange("(c p) d -> p c d", p=P)).then_inc(w_in, 16)
            sp.dma_start(bias[:, :], b_dram.unsqueeze(0).broadcast_to([P, D])).then_inc(b_in, 16)

        @block.gpsimd
        def _(pool):
            pool.wait_ge(b_in, 16)
            pool.tensor_tensor(bias[:, :], bias[:, :], mem.gate[:, 2, :], ALU.mult).then_inc(bias_gated, 1)
            pool.wait_ge(bias_gated, 1)
            for t in range(NT):
                last = pool.tensor_tensor(mem.x[:, t, :], mem.x[:, t, :], bias[:, :], ALU.add).then_inc(biased, 1)

        @block.tensor
        def _(pe):
            for i, (half, k) in enumerate(pieces):
                if i >= 2:
                    pe.wait_ge(a_split, i - 1)
                for t in range(TPH):
                    last = nc.tensor.transpose(mem.bank[i % 2][:, t * P:(t + 1) * P],
                                               attended[:, half * TPH + t, k * P:(k + 1) * P], mem.ident[:, :])
                last.then_inc(a_turned, 1)
            pe.wait_ge(w_in, 16)
            for k in range(KT):
                if k >= 2:
                    pe.wait_ge(w_gated, k - 1)
                for c in range(KT):
                    last = nc.tensor.transpose(mem.bank[2 + k % 2][:, c * P:(c + 1) * P], raw[:, c, k * P:(k + 1) * P],
                                               mem.ident[:, :])
                last.then_inc(w_turned, 1)
            pe.wait_ge(w_split, KT)
            for t in range(NT):
                if t >= 2:
                    pe.wait_ge(added, t - 1)
                for k in range(KT):
                    last = split_products(nc.tensor, mem.bank[4 + t % 2][:, :], [a[:, k, t * P:(t + 1) * P] for a in aT],
                                          [a[:, k, :] for a in wT], k == 0, k == KT - 1)
                last.then_inc(produced, 1)

        @block.scalar
        def _(act):
            for i, (half, k) in enumerate(pieces):
                act.wait_ge(a_turned, i + 1)
                nc.scalar.copy(aT[0][:, k, half * HALF:(half + 1) * HALF], mem.bank[i % 2][:, :]).then_inc(a_hi, 1)
            for k in range(KT):
                act.wait_ge(w_gated, k + 1)
                nc.scalar.copy(wT[0][:, k, :], gated[:, k, :]).then_inc(w_hi, 1)

        @block.vector
        def _(dve):
            for i, (half, k) in enumerate(pieces):
                cols = slice(half * HALF, (half + 1) * HALF)
                dve.wait_ge(a_hi, i + 1)
                nc.vector.tensor_tensor(aT[1][:, k, cols], mem.bank[i % 2][:, :], aT[0][:, k, cols].bitcast(F32),
                                        ALU.subtract).then_inc(a_split, 1)
            for k in range(KT):
                dve.wait_ge(w_turned, k + 1)
                nc.vector.tensor_tensor(gated[:, k, :], mem.bank[2 + k % 2][:, :], mem.gate[:, 2, :], ALU.mult
                                        ).then_inc(w_gated, 1)
            for k in range(KT):
                dve.wait_ge(w_hi, k + 1)
                nc.vector.tensor_tensor(wT[1][:, k, :], gated[:, k, :], wT[0][:, k, :].bitcast(F32), ALU.subtract
                                        ).then_inc(w_split, 1)
            for t in range(NT):
                dve.wait_ge(produced, t + 1)
                dve.wait_ge(biased, t + 1)
                nc.vector.tensor_tensor(mem.x[:, t, :], mem.bank[4 + t % 2][:, :], mem.x[:, t, :], ALU.add
                                        ).then_inc(added, 1)


def layer1_experts_phase(nc, mem, x_out, w):
    RT = (ER + P - 1) // P
    R_OF = [P, ER - P]
    LW = NE + ER
    with ExitStack() as ctx:
        sem = lambda name: mem.semaphores.enter_context(nc.semaphore("e1_" + name))
        sb = lambda name, shape, dt=F32: ctx.enter_context(nc.sbuf_tensor("e1_" + name, shape, dt))
        pair = lambda name, shape: (sb(name + "_hi", shape, F32R), sb(name + "_lo", shape, F32R))
        raw, raw_a, raw_g = sb("raw", [P, KT, D]), sb("raw_a", [P, RT, D]), sb("raw_g", [NE, D])
        raw_b = sb("raw_b", [P, KT, NE, RANK1])
        gated = sb("gated", [P, 2, D])
        wT, aT = pair("wT", [P, KT, D]), pair("aT", [P, KT, LW])
        bT = pair("bT", [P, RT, D])
        number = sb("number", [P, NE], I32)
        numberf = sb("numberf", [P, NE])
        low_all = sb("low_all", [P, NT, LW])
        top, index, indexf = sb("top", [P, NT, 8]), sb("index", [P, NT, 8], U32), sb("indexf", [P, NT, 2])
        gap, exped, prob = sb("gap", [P, NT]), sb("exped", [P, NT]), sb("prob", [P, NT, 2])
        chosen, mix = sb("chosen", [P, 2, NE]), sb("mix", [P, NE])
        scaled = sb("scaled", [P, 2, ER])
        sT = pair("sT", [P, 2, RT, P])
        w_in, a_in, b_in = sem("w_in"), sem("a_in"), sem("b_in")
        w_turned, w_gated, w_hi, w_split = sem("w_turned"), sem("w_gated"), sem("w_hi"), sem("w_split")
        a_turned, a_hi, a_split = sem("a_turned"), sem("a_hi"), sem("a_split")
        counted, numbered = sem("counted"), sem("numbered")
        logits_done, logits_out, topped, indexed = sem("logits_done"), sem("logits_out"), sem("topped"), sem("indexed")
        step, gapped, exp_done = sem("step"), sem("gapped"), sem("exp_done")
        scaled_done, s_turned, s_hi, s_split = sem("scaled_done"), sem("s_turned"), sem("s_hi"), sem("s_split")
        produced, added, stored = sem("produced"), sem("added"), sem("stored")
        mats = [("w", k) for k in range(KT)] + [("b", r) for r in range(RT)]
        block = ctx.enter_context(nc.Block())

        @block.sync
        def _(sp):
            sp.dma_start(raw_g[:, :], w["gate"][:, :]).then_inc(a_in, 16)
            a = w["a"].rearrange("e r d -> (e r) d")
            sp.dma_start(raw_a[:, 0, :], a[0:P, :]).then_inc(a_in, 16)
            sp.dma_start(raw_a[:R_OF[1], 1, :], a[P:ER, :]).then_inc(a_in, 16)
            sp.dma_start(raw[:, :, :], w["base"].rearrange("(c p) d -> p c d", p=P)).then_inc(w_in, 16)
            for c in range(KT):
                sp.dma_start(raw_b[:, c, :, :], w["b"][:, c * P:(c + 1) * P, :].rearrange("e p r -> p e r")
                             ).then_inc(b_in, 16)
            for t in range(NT):
                sp.wait_ge(added, t + 1)
                sp.dma_start(x_out[0, t * P:(t + 1) * P, :], mem.x[:, t, :]).then_inc(stored, 16)
            sp.wait_ge(stored, 16 * NT)

        @block.gpsimd
        def _(pool):
            pool.iota(number[:, :], [[1, NE]], base=0, channel_multiplier=0).then_inc(counted, 1)

        @block.tensor
        def _(pe):
            pe.wait_ge(a_in, 48)
            for k in range(KT):
                if k >= 2:
                    pe.wait_ge(a_split, k - 1)
                out = mem.bank[k % 2]
                cols = slice(k * P, (k + 1) * P)
                nc.tensor.transpose(out[:, 0:NE], raw_g[:, cols], mem.ident[:NE, :NE])
                nc.tensor.transpose(out[:, NE:NE + P], raw_a[:, 0, cols], mem.ident[:, :])
                nc.tensor.transpose(out[:, NE + P:LW], raw_a[:R_OF[1], 1, cols], mem.ident[:R_OF[1], :R_OF[1]]
                                    ).then_inc(a_turned, 1)
            pe.wait_ge(w_in, 16)
            for n, (m, k) in enumerate(mats):
                if m == "b" and k == 0:
                    pe.wait_ge(b_in, 16 * KT)
                if n >= 2:
                    pe.wait_ge(w_gated, n - 1)
                out = mem.bank[2 + n % 2]
                for c in range(KT):
                    if m == "w":
                        last = nc.tensor.transpose(out[:, c * P:(c + 1) * P], raw[:, c, k * P:(k + 1) * P], mem.ident[:, :])
                    else:
                        rows = raw_b[:, c, :, :].rearrange("p e r -> p (e r)")[:, k * P:k * P + R_OF[k]]
                        last = nc.tensor.transpose(out[:R_OF[k], c * P:(c + 1) * P], rows, mem.ident[:, :])
                last.then_inc(w_turned, 1)
            pe.wait_ge(a_split, KT)

            def low(t):
                if t >= 2:
                    pe.wait_ge(logits_out, t - 1)
                for k in range(KT):
                    last = split_products(nc.tensor, mem.bank[t % 2][:, 0:LW], [a[:, k, t * P:(t + 1) * P] for a in mem.hT],
                                          [a[:, k, :] for a in aT], k == 0, k == KT - 1)
                last.then_inc(logits_done, 1)

            for t in range(NT):
                low(t)
            pe.wait_ge(w_split, len(mats))
            for t in range(NT):
                out = mem.bank[6 + t % 2]
                if t >= 2:
                    pe.wait_ge(added, t - 1)
                for k in range(KT):
                    split_products(nc.tensor, out[:, :], [a[:, k, t * P:(t + 1) * P] for a in mem.hT],
                                   [a[:, k, :] for a in wT], k == 0, False)
                pe.wait_ge(scaled_done, t + 1)
                if t >= 2:
                    pe.wait_ge(s_split, t - 1)
                for r in range(RT):
                    last = nc.tensor.transpose(mem.bank[4 + t % 2][:R_OF[r], r * P:(r + 1) * P],
                                               scaled[:, t % 2, r * P:r * P + R_OF[r]], mem.ident[:, :])
                last.then_inc(s_turned, 1)
                pe.wait_ge(s_split, t + 1)
                for r in range(RT):
                    n = R_OF[r]
                    last = split_products(nc.tensor, out[:, :], [a[:n, t % 2, r, :] for a in sT],
                                          [a[:n, r, :] for a in bT], False, r == RT - 1)
                last.then_inc(produced, 1)

        @block.scalar
        def _(act):
            for k in range(KT):
                act.wait_ge(a_turned, k + 1)
                nc.scalar.copy(aT[0][:, k, :], mem.bank[k % 2][:, 0:LW]).then_inc(a_hi, 1)
            for n, (m, k) in enumerate(mats):
                act.wait_ge(w_gated, n + 1)
                rows = P if m == "w" else R_OF[k]
                nc.scalar.copy((wT if m == "w" else bT)[0][:rows, k, :], gated[:rows, n % 2, :]).then_inc(w_hi, 1)
            act.wait_ge(gapped, 1)
            nc.scalar.activation(exped[:, :], gap[:, :], ACT.Exp).then_inc(exp_done, 1)
            for t in range(NT):
                act.wait_ge(s_turned, t + 1)
                for r in range(RT):
                    last = nc.scalar.copy(sT[0][:R_OF[r], t % 2, r, :], mem.bank[4 + t % 2][:R_OF[r], r * P:(r + 1) * P])
                last.then_inc(s_hi, 1)

        @block.vector
        def _(dve):
            steps = [0]

            def link(instruction):
                steps[0] += 1
                instruction.then_inc(step, 1)
                dve.wait_ge(step, steps[0])

            for k in range(KT):
                dve.wait_ge(a_hi, k + 1)
                nc.vector.tensor_tensor(aT[1][:, k, :], mem.bank[k % 2][:, 0:LW], aT[0][:, k, :].bitcast(F32),
                                        ALU.subtract).then_inc(a_split, 1)
            for n, (m, k) in enumerate(mats):
                rows = P if m == "w" else R_OF[k]
                dve.wait_ge(w_turned, n + 1)
                nc.vector.tensor_tensor(gated[:rows, n % 2, :], mem.bank[2 + n % 2][:rows, :], mem.gate[:rows, 3, :],
                                        ALU.mult).then_inc(w_gated, 1)
                out = (wT if m == "w" else bT)
                dve.wait_ge(w_hi, n + 1)
                nc.vector.tensor_tensor(out[1][:rows, k, :], gated[:rows, n % 2, :], out[0][:rows, k, :].bitcast(F32),
                                        ALU.subtract).then_inc(w_split, 1)
                dve.wait_ge(w_split, n + 1)
            dve.wait_ge(counted, 1)
            link(nc.vector.tensor_copy(numberf[:, :], number[:, :]))
            for t in range(NT):
                dve.wait_ge(logits_done, t + 1)
                nc.vector.tensor_copy(low_all[:, t, :], mem.bank[t % 2][:, 0:LW]).then_inc(logits_out, 1)
                dve.wait_ge(logits_out, t + 1)
                nc.vector.max(top[:, t, :], low_all[:, t, 0:NE]).then_inc(topped, 1)
                dve.wait_ge(topped, t + 1)
                nc.vector.max_index(index[:, t, :], top[:, t, :], low_all[:, t, 0:NE]).then_inc(indexed, 1)
            dve.wait_ge(indexed, NT)
            link(nc.vector.tensor_copy(indexf[:, :, :], index[:, :, 0:2]))
            nc.vector.tensor_tensor(gap[:, :], top[:, :, 1], top[:, :, 0], ALU.subtract).then_inc(gapped, 1)
            dve.wait_ge(exp_done, 1)
            link(nc.vector.tensor_scalar(gap[:, :], exped[:, :], 1.0, None, ALU.add))
            link(nc.vector.reciprocal(prob[:, :, 0], gap[:, :]))
            link(nc.vector.tensor_scalar(prob[:, :, 0], prob[:, :, 0], LORA_SCALE, None, ALU.mult))
            link(nc.vector.tensor_tensor(prob[:, :, 1], prob[:, :, 0], exped[:, :], ALU.mult))
            for t in range(NT):
                for n in range(2):
                    last = nc.vector.tensor_scalar(chosen[:, n, :], numberf[:, :], indexf[:, t, n:n + 1],
                                                   prob[:, t, n:n + 1], ALU.is_equal, ALU.mult)
                link(last)
                link(nc.vector.tensor_tensor(mix[:, :], chosen[:, 0, :], chosen[:, 1, :], ALU.add))
                if t >= 2:
                    dve.wait_ge(s_turned, t - 1)
                nc.vector.tensor_tensor(scaled[:, t % 2, :].rearrange("p (e r) -> p e r", e=NE),
                                        low_all[:, t, NE:LW].rearrange("p (e r) -> p e r", e=NE),
                                        mix[:, :].unsqueeze(2).broadcast_to([P, NE, RANK1]), ALU.mult
                                        ).then_inc(scaled_done, 1)
                dve.wait_ge(scaled_done, t + 1)
                dve.wait_ge(s_hi, t + 1)
                for r in range(RT):
                    n = R_OF[r]
                    last = nc.vector.tensor_tensor(sT[1][:n, t % 2, r, :], mem.bank[4 + t % 2][:n, r * P:(r + 1) * P],
                                                   sT[0][:n, t % 2, r, :].bitcast(F32), ALU.subtract)
                last.then_inc(s_split, 1)
                dve.wait_ge(produced, t + 1)
                nc.vector.tensor_tensor(mem.x[:, t, :], mem.bank[6 + t % 2][:, :], mem.x[:, t, :], ALU.add
                                        ).then_inc(added, 1)


def program(nc, ins, out, rope0, rope1):
    with ExitStack() as ctx:
        sb = lambda name, shape, dt=F32: ctx.enter_context(nc.sbuf_tensor(name, shape, dt))
        mem = Memory()
        mem.semaphores = ctx
        mem.ident, mem.ident_bf = sb("ident", [P, P]), sb("ident_bf", [P, P], BF16)
        mem.causal, mem.ones = sb("causal", [P, P], BF16), sb("ones", [P, P])
        mem.x = sb("x", [P, NT, D])
        mem.hT = (sb("hT_hi", [P, KT, S], F32R), sb("hT_lo", [P, KT, S], F32R))
        mem.gate, mem.column = sb("gate", [P, 4, D]), sb("column", [P, 8, KT])
        psum = ctx.enter_context(nc.psum_tensor("psum", [P, 8, HALF], F32))
        mem.bank = [psum[:, b, :] for b in range(8)]
        mem.bank_pair = [psum[:, 2 * s:2 * s + 2, :].rearrange("p b n -> p (b n)") for s in range(2)]
        mem.bank_pair4 = lambda m: psum[:, 4 + 2 * m:6 + 2 * m, :].rearrange("p b n -> p (b n)")
        mem.layernorm_counts = layernorm_counts(nc, mem)
        constants_phase(nc, mem)
        modulation_phase(nc, mem, ins["L0_attn_hidden_states"], (ins["L0_c"], ins["L1_c"]),
                         (ins["L0_wmod"], ins["L1_wmod"]))
        layernorm_phase(nc, mem, 0, mem.column[:, 1, :], mem.column[:, 0, :])
        layer0_attention_phase(nc, mem, rope0, {w: ins["L0_attn_qw_" + w] for w in "qkvo"},
                               {w: ins["L0_attn_scales_" + w] for w in "qkvo"})
        layernorm_phase(nc, mem, 1, mem.column[:, 3, :], mem.column[:, 2, :])
        layer0_ffn_phase(nc, mem, {n: ins["L0_ffn_" + n] for n in
                                   ("gate_w", "up_w", "down_w", "gate_a", "gate_b", "up_a", "up_b", "down_a", "down_b")})
        layernorm_phase(nc, mem, 2, mem.column[:, 5, :], mem.column[:, 4, :])
        with ExitStack() as attention:
            sb1 = lambda name, shape, dt=F32: attention.enter_context(nc.sbuf_tensor(name, shape, dt))
            k1 = (sb1("k1_hi", [P, NT, NKV1 * HD1], F32R), sb1("k1_lo", [P, NT, NKV1 * HD1], F32R))
            v1, attended = sb1("v1", [P, NT, NKV1 * HD1]), sb1("attended", [P, NT, D])
            layer1_qkv_phase(nc, mem, k1, v1, rope1, ins["L1_attn_w_qkv"], ins["L1_attn_b_qkv"])
            layer1_attention_phase(nc, mem, k1, v1, attended)
            layer1_output_phase(nc, mem, attended, ins["L1_attn_w_o"], ins["L1_attn_b_o"])
        layernorm_phase(nc, mem, 3, mem.column[:, 7, :], mem.column[:, 6, :])
        layer1_experts_phase(nc, mem, out, {"base": ins["L1_ffn_base_W"], "gate": ins["L1_ffn_gate_W"],
                                            "a": ins["L1_ffn_lora_A"], "b": ins["L1_ffn_lora_B"]})


_INS = [
    "L0_attn_hidden_states", "L0_attn_scales_q", "L0_attn_scales_k", "L0_attn_scales_v", "L0_attn_scales_o",
    "L0_attn_qw_q", "L0_attn_qw_k", "L0_attn_qw_v", "L0_attn_qw_o", "L0_ffn_gate_w", "L0_ffn_up_w", "L0_ffn_down_w",
    "L0_ffn_gate_a", "L0_ffn_gate_b", "L0_ffn_up_a", "L0_ffn_up_b", "L0_ffn_down_a", "L0_ffn_down_b", "L0_c", "L0_wmod",
    "L1_attn_w_qkv", "L1_attn_b_qkv", "L1_attn_w_o", "L1_attn_b_o", "L1_ffn_base_W", "L1_ffn_gate_W", "L1_ffn_lora_A",
    "L1_ffn_lora_B", "L1_c", "L1_wmod",
]


def _rope_tables():
    import numpy as np

    def angles(width):
        inverse = np.float32(1) / np.float32(10000) ** (np.arange(0, width, 2, dtype=np.float32) / np.float32(width))
        return np.arange(S, dtype=np.float32)[:, None] * inverse[None, :]

    a0, a1 = angles(HD0), angles(HD1)
    cos0, sin0 = np.cos(a0).T, np.sin(a0).T
    return (np.stack([np.concatenate([cos0, cos0]), np.concatenate([-sin0, sin0])]).astype(np.float32),
            np.stack([np.cos(a1), np.sin(a1)], axis=1).astype(np.float32))


def kernel(**inputs):
    import numpy as np
    import concourse.bacc as bacc
    from concourse.bass_utils import run_bass_kernel_spmd

    nc = bacc.Bacc("TRN2", target_bir_lowering=False, num_devices=1)
    rope0, rope1 = _rope_tables()
    arrays = {f"in_{name}": np.ascontiguousarray(inputs[name]) for name in _INS}
    arrays["rope0"], arrays["rope1"] = rope0, rope1
    aps = {name: nc.dram_tensor(name, a.shape, mybir.dt.from_np(a.dtype), kind="ExternalInput").ap()
           for name, a in arrays.items()}
    out = nc.dram_tensor("out", (1, S, D), F32, kind="ExternalOutput").ap()
    program(nc, {name: aps[f"in_{name}"] for name in _INS}, out, aps["rope0"], aps["rope1"])
    result = run_bass_kernel_spmd(nc, [arrays], core_ids=[0])
    return result.results[0]["out"]
```

```python
import concourse.bass as bass
from concourse import mybir
from contextlib import ExitStack

F32 = mybir.dt.float32
F32R = mybir.dt.float32r
BF16 = mybir.dt.bfloat16
I32 = mybir.dt.int32
U32 = mybir.dt.uint32
ALU = mybir.AluOpType
ACT = mybir.ActivationFunctionType
AX = mybir.AxisListType

P = 128
S = 1024
D = 512
NT = S // P
KT = D // P
HALF = 512
NHALF = S // HALF
TPH = HALF // P
LN_EPS = 1e-5
MASKED = -3.0e38

NH0, NKV0, HD0 = 32, 8, 128
REP0 = NH0 // NKV0
ZERO_POINT = 8.0
SCALE0 = float(HD0) ** -0.5

HID = 1376
RANK0 = 16
NF = (HID + P - 1) // P
HID_LAST = HID - (NF - 1) * P

NH1, NKV1, HD1 = 32, 8, 16
REP1 = NH1 // NKV1
QK1 = (NH1 + NKV1) * HD1
QKV1 = (NH1 + 2 * NKV1) * HD1
SCALE1 = float(HD1) ** -0.5

NE, RANK1 = 28, 8
ER = NE * RANK1
LORA_SCALE = 2.0


class Turns:

    def __init__(self, sem, names):
        self.sem, self.names, self.n = sem, list(names), len(names)

    def open(self, engine, done_before_loop=0):
        engine.sem_inc(self.sem, self.n - done_before_loop)

    def now(self, turn, name):
        return self.sem, turn * self.n + self.n + self.names.index(name) + 1

    def last(self, turn, name):
        return self.sem, turn * self.n + self.names.index(name) + 1


class Memory:
    pass


def split_products(pe, out, lhs, rhs, start, stop):
    (lhs_hi, lhs_lo), (rhs_hi, rhs_lo) = lhs, rhs
    pe.matmul(out, lhs_lo, rhs_hi, start=start, stop=False)
    pe.matmul(out, lhs_hi, rhs_lo, start=False, stop=False)
    return pe.matmul(out, lhs_hi, rhs_hi, start=False, stop=stop)


def constants_phase(nc, mem):
    with ExitStack() as ctx:
        cleared = mem.semaphores.enter_context(nc.semaphore("const_cleared"))
        drawn = mem.semaphores.enter_context(nc.semaphore("const_drawn"))
        block = ctx.enter_context(nc.Block())

        @block.gpsimd
        def _(pool):
            pool.memset(mem.ident[:, :], 0.0).then_inc(cleared, 1)
            pool.memset(mem.causal[:, :], 0.0).then_inc(cleared, 1)
            pool.memset(mem.ones[:, :], 1.0).then_inc(cleared, 1)
            pool.wait_ge(cleared, 3)
            pool.affine_select(out=mem.ident[:, :], in_=mem.ident[:, :], compare_op=ALU.not_equal,
                               fill=1.0, base=0, pattern=[[-1, P]], channel_multiplier=1).then_inc(drawn, 1)
            pool.affine_select(out=mem.causal[:, :], in_=mem.causal[:, :], compare_op=ALU.is_ge,
                               fill=MASKED, base=0, pattern=[[-1, P]], channel_multiplier=1).then_inc(drawn, 1)
            pool.wait_ge(drawn, 1)
            pool.tensor_copy(mem.ident_bf[:, :], mem.ident[:, :]).then_inc(drawn, 1)
            pool.wait_ge(drawn, 3)


def modulation_phase(nc, mem, x, c_dram, wmod_dram):
    SLOTS = 4
    CHUNKS = 6
    with ExitStack() as ctx:
        sem = lambda name: mem.semaphores.enter_context(nc.semaphore(name))
        sb = lambda name, shape, dt=F32: ctx.enter_context(nc.sbuf_tensor(name, shape, dt))
        c_col = sb("mod_c", [P, 2, KT])
        silu_c = sb("mod_silu", [P, 2, KT])
        silu_rows = sb("mod_silu_rows", [P, 2 * KT, P])
        w = sb("mod_w", [P, SLOTS, KT, D])
        sign = sb("mod_sign", [P, D])
        size = sb("mod_size", [P, D])
        diag = sb("mod_diag", [P, P])
        x_in, c_in = sem("x_in"), sem("mod_c_in")
        w_in = [sem(f"mod_w_in{s}") for s in range(SLOTS)]
        silu_done, rows_done = sem("mod_silu_done"), sem("mod_rows_done")
        product_done, taken, step = sem("mod_product"), sem("mod_taken"), sem("mod_step")
        bank = mem.bank
        block = ctx.enter_context(nc.Block())

        @block.sync
        def _(sp):
            for layer in range(2):
                sp.dma_start(c_col[:, layer, :], c_dram[layer][0, :].rearrange("(k p) -> p k", p=P),
                             allow_slow_non_contiguous=True).then_inc(c_in, 16)
            for j in range(2 * CHUNKS):
                if j == 2:
                    sp.dma_start(mem.x[:, :, :], x[0].rearrange("(t p) d -> p t d", p=P)).then_inc(x_in, 16)
                if j >= SLOTS:
                    sp.wait_ge(product_done, j - SLOTS + 1)
                n = j % CHUNKS
                sp.dma_start(w[:, j % SLOTS, :, :],
                             wmod_dram[j // CHUNKS][:, n * D:(n + 1) * D].rearrange("(k p) n -> p k n", p=P)
                             ).then_inc(w_in[j % SLOTS], 16)
            sp.wait_ge(x_in, 16)

        @block.scalar
        def _(act):
            act.wait_ge(c_in, 32)
            nc.scalar.activation(silu_c[:, :, :], c_col[:, :, :], ACT.Silu).then_inc(silu_done, 1)

        @block.tensor
        def _(pe):
            pe.wait_ge(rows_done, 2 * KT)
            for j in range(2 * CHUNKS):
                pe.wait_ge(w_in[j % SLOTS], 16 * (j // SLOTS + 1))
                if j >= 2:
                    pe.wait_ge(taken, j - 1)
                for k in range(KT):
                    last = nc.tensor.matmul(bank[j % 2][:, :], silu_rows[:, (j // CHUNKS) * KT + k, :],
                                            w[:, j % SLOTS, k, :], start=(k == 0), stop=(k == KT - 1))
                last.then_inc(product_done, 1)

        @block.vector
        def _(dve):
            steps = 0
            dve.wait_ge(silu_done, 1)
            for layer in range(2):
                for k in range(KT):
                    nc.vector.tensor_scalar(silu_rows[:, layer * KT + k, :], mem.ones[:, :],
                                            silu_c[:, layer, k:k + 1], None, ALU.mult).then_inc(rows_done, 1)
            for j in range(2 * CHUNKS):
                layer, n = j // CHUNKS, j % CHUNKS
                product = bank[j % 2]
                dve.wait_ge(product_done, j + 1)
                if n in (2, 5):
                    gate = mem.gate[:, 2 * layer + (n == 5), :]
                    nc.vector.tensor_scalar(sign[:, :], product[:, :], 0.0, 2.0, ALU.is_ge, ALU.mult).then_inc(step, 1)
                    nc.vector.tensor_scalar(size[:, :], product[:, :], -1.0, 0.25, ALU.mult, ALU.max).then_inc(step, 1)
                    steps += 2
                    dve.wait_ge(step, steps)
                    nc.vector.tensor_tensor(size[:, :], size[:, :], product[:, :], ALU.max).then_inc(step, 1)
                    steps += 1
                    dve.wait_ge(step, steps)
                    nc.vector.scalar_tensor_tensor(out=gate, in0=sign[:, :], scalar=-1.0, in1=size[:, :],
                                                   op0=ALU.add, op1=ALU.mult).then_inc(taken, 1)
                    dve.wait_ge(taken, j + 1)
                else:
                    column = mem.column[:, 4 * layer + {0: 0, 1: 1, 3: 2, 4: 3}[n], :]
                    for k in range(KT):
                        done = nc.vector.scalar_tensor_tensor(
                            out=diag[:, :], in0=product[:, k * P:(k + 1) * P], scalar=1.0, in1=mem.ident[:, :],
                            op0=ALU.mult, op1=ALU.mult, accum_out=column[:, k:k + 1])
                        if k < KT - 1 or n in (1, 4):
                            done.then_inc(step, 1)
                            steps += 1
                            dve.wait_ge(step, steps)
                    if n in (1, 4):
                        done = nc.vector.tensor_scalar(column, column, 1.0, None, ALU.add)
                    done.then_inc(taken, 1)
                    dve.wait_ge(taken, j + 1)


class Counted:

    def __init__(self, sem, total):
        self.sem, self.total = sem, total

    def after(self, run, k):
        return self.sem, run * self.total + k


def layernorm_counts(nc, mem):
    pieces = NHALF * KT
    totals = {"stats_done": NT, "moments": NT, "y_done": 1, "root_done": 1, "rstd_done": 5, "normed_done": NT,
              "turned": pieces, "modulated": pieces, "hi_done": pieces, "lo_done": pieces}
    return [Counted(mem.semaphores.enter_context(nc.semaphore("ln_" + name)), n) for name, n in totals.items()]


def layernorm_phase(nc, mem, run, scale_col, shift_col):
    with ExitStack() as ctx:
        sb = lambda name, shape, dt=F32: ctx.enter_context(nc.sbuf_tensor(f"ln{run}_{name}", shape, dt))
        stats = sb("stats", [P, NT, 6])
        mean_var = sb("mean_var", [P, NT, 2])
        y, std, root = sb("y", [P, NT]), sb("std", [P, NT]), sb("root", [P, NT])
        newton, rstd = sb("newton", [P, NT]), sb("rstd", [P, NT])
        normed = sb("normed", [P, NT, D])
        h = sb("h", [P, 4, HALF])
        (stats_done, moments, y_done, root_done, rstd_done, normed_done,
         turned, modulated, hi_done, lo_done) = mem.layernorm_counts
        pieces = [(half, k) for half in range(NHALF) for k in range(KT)]
        block = ctx.enter_context(nc.Block())

        @block.vector
        def _(dve):
            for t in range(NT):
                nc.vector.bn_stats(stats[:, t, :], mem.x[:, t, :]).then_inc(stats_done.sem, 1)
            for t in range(NT):
                dve.wait_ge(*stats_done.after(run, t + 1))
                nc.vector.bn_aggr(mean_var[:, t, :], stats[:, t, :]).then_inc(moments.sem, 1)
            dve.wait_ge(*moments.after(run, NT))
            nc.vector.tensor_scalar(y[:, :], mean_var[:, :, 1], LN_EPS, None, ALU.add).then_inc(y_done.sem, 1)
            dve.wait_ge(*root_done.after(run, 1))
            nc.vector.reciprocal(root[:, :], std[:, :]).then_inc(rstd_done.sem, 1)
            dve.wait_ge(*rstd_done.after(run, 1))
            nc.vector.tensor_tensor(newton[:, :], root[:, :], root[:, :], ALU.mult).then_inc(rstd_done.sem, 1)
            dve.wait_ge(*rstd_done.after(run, 2))
            nc.vector.tensor_tensor(newton[:, :], newton[:, :], y[:, :], ALU.mult).then_inc(rstd_done.sem, 1)
            dve.wait_ge(*rstd_done.after(run, 3))
            nc.vector.tensor_scalar(newton[:, :], newton[:, :], -0.5, 1.5, ALU.mult, ALU.add).then_inc(rstd_done.sem, 1)
            dve.wait_ge(*rstd_done.after(run, 4))
            nc.vector.tensor_tensor(rstd[:, :], root[:, :], newton[:, :], ALU.mult).then_inc(rstd_done.sem, 1)
            dve.wait_ge(*rstd_done.after(run, 5))
            for t in range(NT):
                nc.vector.tensor_scalar(normed[:, t, :], mem.x[:, t, :], mean_var[:, t, 0:1], rstd[:, t:t + 1],
                                        ALU.subtract, ALU.mult).then_inc(normed_done.sem, 1)

            def low(i):
                half, k = pieces[i]
                dve.wait_ge(*hi_done.after(run, i + 1))
                nc.vector.tensor_tensor(mem.hT[1][:, k, half * HALF:(half + 1) * HALF], h[:, i % 4, :],
                                        mem.hT[0][:, k, half * HALF:(half + 1) * HALF].bitcast(F32),
                                        ALU.subtract).then_inc(lo_done.sem, 1)

            for i, (half, k) in enumerate(pieces):
                dve.wait_ge(*modulated.after(run, i + 1))
                nc.vector.tensor_copy(mem.hT[0][:, k, half * HALF:(half + 1) * HALF], h[:, i % 4, :]).then_inc(hi_done.sem, 1)
                if i:
                    low(i - 1)
            low(len(pieces) - 1)

        @block.tensor
        def _(pe):
            for i, (half, k) in enumerate(pieces):
                pe.wait_ge(*normed_done.after(run, TPH * (half + 1)))
                if i >= 4:
                    pe.wait_ge(*modulated.after(run, i - 3))
                for t in range(TPH):
                    last = nc.tensor.transpose(mem.bank[i % 4][:, t * P:(t + 1) * P],
                                               normed[:, half * TPH + t, k * P:(k + 1) * P], mem.ident[:, :])
                last.then_inc(turned.sem, 1)

        @block.scalar
        def _(act):
            act.wait_ge(*y_done.after(run, 1))
            nc.scalar.activation(std[:, :], y[:, :], ACT.Sqrt).then_inc(root_done.sem, 1)
            for i, (half, k) in enumerate(pieces):
                act.wait_ge(*turned.after(run, i + 1))
                if i >= 4:
                    act.wait_ge(*lo_done.after(run, i - 3))
                nc.scalar.activation(h[:, i % 4, :], mem.bank[i % 4][:, :], ACT.Identity,
                                     scale=scale_col[:, k:k + 1], bias=shift_col[:, k:k + 1]).then_inc(modulated.sem, 1)


def layer0_attention_phase(nc, mem, rope_dram, qw, scales):
    HH = HD0 // 2
    LAST = NKV0 - 1
    heads, tiles, halves = range(REP0), range(NT), range(NHALF)
    units = [(h, i) for h in heads for i in tiles]
    second_q = lambda h, i: i == (NT - 1 if h else 5)
    uses = []
    for h, i in units:
        if h < REP0 - 1 and second_q(h, i):
            uses.append(("q", h + 1, 1))
        if h > 0:
            uses.append(("o", h - 1, i))
            if i == 0:
                uses.append(("pv", h - 1, 1))
        if i == TPH:
            uses.append(("pv", h, 0))
        if h < REP0 - 1 and i == 0:
            uses.append(("q", h + 1, 0))
    AHEAD6 = [("k", 0), ("k", 1), ("q", 0, 0), ("v", 0), ("vt", 0)]
    AHEAD7 = [("q", 0, 1), ("v", 1), ("vt", 1)]
    use6, use7 = uses[1::2] + AHEAD6, uses[0::2] + [("pv", REP0 - 1, 1)] + AHEAD7
    pieces = [(h, i, c) for h, i in units for c in range(i // TPH + 1)]
    weights = [("o", 0), ("q", 2), ("o", 1), ("q", 3), ("o", 2), ("o", 3), ("k", 0), ("v", 0), ("q", 0), ("q", 1)]
    AHEAD, RING = 4, 5
    AT_HOME = len(weights) - AHEAD
    roped_halves = [("q", h, b) for h in range(1, REP0) for b in halves] + [("k", b) for b in halves] + \
                   [("q", 0, b) for b in halves]
    ROPED_AHEAD = 4
    with ExitStack() as ctx:
        sem = lambda name: mem.semaphores.enter_context(nc.semaphore("a0_" + name))
        turns = lambda name, names: Turns(sem(name), names)
        sb = lambda name, shape, dt=F32: ctx.enter_context(nc.sbuf_tensor("a0_" + name, shape, dt))
        pair = lambda name, shape: (sb(name + "_hi", shape, F32R), sb(name + "_lo", shape, F32R))
        rope = sb("rope", [P, 2, S])
        raw, scale = sb("raw", [P, RING, D], I32), sb("scale", [P, RING, D])
        shifted, weight, with_gate = sb("shifted", [P, 2, D]), sb("weight", [P, D]), sb("with_gate", [P, D])
        zero = sb("zero", [P, 1])
        wkv = pair("wkv", [P, 2, KT, HD0])
        wq, wo = pair("wq", [P, 2, KT, HD0]), pair("wo", [P, 2, D])
        kT, qT = pair("kT", [P, S]), pair("qT", [P, 2, S])
        vT, v = sb("vT", [P, S]), sb("v", [P, NT, HD0])
        plain, exchanged, roped = sb("plain", [P, 2, HALF]), sb("exchanged", [P, 2, HALF]), sb("roped", [P, HALF])
        probs = sb("probs", [P, 2, S])
        probsT = [sb(f"probsT{b}", [P, TPH * (b + 1), HALF]) for b in halves]
        ctxT = pair("ctxT", [P, 2, S])
        neg_max, row_sum, row_inv = sb("neg_max", [P, 2, NT]), sb("row_sum", [P, 2, NT]), sb("row_inv", [P, 2, NT])

        rope_in, filled = sem("rope_in"), sem("filled")
        raw_in = [sem(f"raw_in{s}") for s in range(RING)]
        shift_done, scaled = turns("shift_done", weights), turns("scaled", weights)
        gated, hi_made, made = turns("gated", heads), turns("hi_made", weights), turns("made", weights)
        full6, full7 = turns("full6", use6), turns("full7", use7)
        scored = turns("scored", units)
        turned = turns("turned", pieces)
        last_output = turns("last_output", tiles)
        rope_mul, rope_sum = turns("rope_mul", roped_halves), turns("rope_sum", roped_halves)
        rope_hi, rope_lo = turns("rope_hi", roped_halves), turns("rope_lo", roped_halves)
        maxed = turns("maxed", units)
        values_split = turns("values_split", [(h, b) for h in heads for b in halves])
        v_done = turns("v_done", halves)
        inverted = turns("inverted", heads)
        output_added = turns("output_added", [(h, t) for h in heads for t in tiles])
        exped = turns("exped", units)
        turned_out = turns("turned_out", pieces)
        projected_out = turns("projected_out", roped_halves + [("v", b) for b in halves])
        ctx_hi = turns("ctx_hi", [(h, b) for h in heads for b in halves])
        score = mem.bank_pair
        turn_bank = mem.bank[4:6]
        bank6, bank7 = mem.bank[6], mem.bank[7]
        full = lambda use: full6 if use in use6 else full7
        bank = lambda use: bank6 if use in use6 else bank7
        half = lambda b: slice(b * HALF, (b + 1) * HALF)
        tile = lambda i: slice(i * P, (i + 1) * P)

        def taken_out(use):
            if use[0] == "o":
                return output_added, use[1:]
            if use[0] == "pv":
                return values_split, use[1:]
            if use[0] == "vt":
                return v_done, use[1]
            return projected_out, use

        def loaded(g, n):
            s = n % RING
            return raw_in[s], g * 64 + 32 * (n // RING) + 32 + (32 if s >= AT_HOME - RING else 0)

        def steps_before(counter, g, n, back):
            return counter.now(g, weights[n - back]) if n >= back else counter.last(g, weights[n - back])

        block = ctx.enter_context(nc.Block())

        @block.sync
        def _(sp):
            def load(n, group):
                name, h = weights[n]
                slot = n % RING
                if name == "o":
                    rows = bass.ds(group * (REP0 * HD0) + h * HD0, HD0)
                    sp.dma_start(raw[:, slot, :], qw["o"][rows, :]).then_inc(raw_in[slot], 16)
                    sp.dma_start(scale[:, slot, :], scales["o"][bass.ds(group * REP0 + h, 1), :].broadcast_to([P, D])
                                 ).then_inc(raw_in[slot], 16)
                    return
                cols = bass.ds(group * (REP0 * HD0) + h * HD0, HD0) if name == "q" else bass.ds(group * HD0, HD0)
                sp.dma_start(raw[:, slot, :].rearrange("p (k n) -> p k n", k=KT),
                             qw[name][:, cols].rearrange("(k p) n -> p k n", p=P)).then_inc(raw_in[slot], 16)
                sp.dma_start(scale[:, slot, :].rearrange("p (k n) -> p k n", k=KT),
                             scales[name][:, cols].unsqueeze(0).broadcast_to([P, KT, HD0])).then_inc(raw_in[slot], 16)

            def turn(g, last=False):
                for n in range(AT_HOME if last else len(weights)):
                    sp.wait_ge(*steps_before(scaled, g, n, RING))
                    load(n, g if n < AT_HOME else g + 1)

            for n in range(AT_HOME, len(weights)):
                load(n, 0)
            sp.dma_start(rope[:, :, :], rope_dram.rearrange("a p s -> p a s")).then_inc(rope_in, 16)
            with sp.Fori(0, LAST) as g:
                turn(g)
            turn(LAST, last=True)

        @block.gpsimd
        def _(pool):
            pool.memset(zero[:, :], 0.0).then_inc(filled, 1)
            for counter in (scaled, hi_made, made):
                counter.open(pool, AHEAD)
            gated.open(pool)
            pool.wait_ge(filled, 1)

            def make(g, n, prologue=False):
                name, h = key = weights[n]
                done = lambda counter: counter.last(0, key) if prologue else counter.now(g, key)
                hi, lo = ((part[:, n - AT_HOME, :, :] for part in wkv) if name in "kv" else
                          (part[:, h % 2] for part in (wq if name == "q" else wo)))
                flat = lambda a: a.rearrange("p k n -> p (k n)") if len(a.shape) == 3 else a
                pool.wait_ge(*done(shift_done))
                pool.tensor_tensor(weight[:, :], shifted[:, n % 2, :], scale[:, n % RING, :], ALU.mult).then_inc(scaled.sem, 1)
                pool.wait_ge(*done(scaled))
                whole = weight
                if name == "o":
                    pool.tensor_tensor(with_gate[:, :], weight[:, :], mem.gate[:, 0, :], ALU.mult).then_inc(gated.sem, 1)
                    pool.wait_ge(*gated.now(g, h))
                    whole = with_gate
                if not prologue:
                    if name in "kv":
                        use = (name, 1)
                        pool.wait_ge(*full(use).last(g, use))
                    elif name == "o":
                        if h >= 2:
                            use = ("o", h - 2, NT - 1)
                            pool.wait_ge(*full(use).now(g, use))
                        elif h == 1:
                            pool.wait_ge(*last_output.last(g, NT - 1))
                        else:
                            use = ("o", 2, NT - 1)
                            pool.wait_ge(*full(use).last(g, use))
                    elif h == 0:
                        use = ("q", 2, 1)
                        pool.wait_ge(*full(use).now(g, use))
                    else:
                        use = ("q", (h - 2) % REP0, 1)
                        pool.wait_ge(*(full(use).now if h != 2 else full(use).last)(g, use))
                pool.tensor_tensor(flat(hi), whole[:, :], zero[:, :].broadcast_to([P, D]), ALU.add).then_inc(hi_made.sem, 1)
                pool.wait_ge(*done(hi_made))
                pool.tensor_tensor(flat(lo), whole[:, :], flat(hi).bitcast(F32), ALU.subtract).then_inc(made.sem, 1)
                pool.wait_ge(*done(made))

            for n in range(AT_HOME, len(weights)):
                make(0, n, prologue=True)
            with pool.Fori(0, LAST) as g:
                for n in range(len(weights)):
                    make(g, n)
            for n in range(AT_HOME):
                make(LAST, n)

        @block.tensor
        def _(pe):
            full6.open(pe, len(AHEAD6))
            full7.open(pe, len(AHEAD7))
            for counter in (scored, turned, last_output):
                counter.open(pe)

            def wait_free(g, use, before_loop=False):
                uses = use6 if use in use6 else use7
                n = uses.index(use)
                counter, name = taken_out(uses[n - 1])
                if before_loop:
                    if use not in (AHEAD6[0], AHEAD7[0]):
                        pe.wait_ge(*counter.last(0, name))
                else:
                    pe.wait_ge(*(counter.now(g, name) if n else counter.last(g, name)))

            def project(g, use, w, slot, b, before_loop=False):
                wait_free(g, use, before_loop)
                for k in range(KT):
                    last = split_products(nc.tensor, bank(use)[:, :], [part[:, slot, k, :] for part in w],
                                          [part[:, k, half(b)] for part in mem.hT], k == 0, k == KT - 1)
                last.then_inc(full(use).sem, 1)

            def made_before(g, name, before_loop):
                pe.wait_ge(*(made.last(0, name) if before_loop else made.now(g, name)))

            def turn_v(g, b, before_loop=False):
                use = ("vt", b)
                pe.wait_ge(*(projected_out.last(0, ("v", b)) if before_loop else projected_out.now(g, ("v", b))))
                wait_free(g, use, before_loop)
                for t in range(TPH):
                    last = nc.tensor.transpose(bank(use)[:, tile(t)], vT[:, tile(b * TPH + t)], mem.ident[:, :])
                last.then_inc(full(use).sem, 1)

            made_before(0, ("k", 0), True)
            for b in halves:
                project(0, ("k", b), wkv, 0, b, True)
            made_before(0, ("v", 0), True)
            made_before(0, ("q", 0), True)
            for b in halves:
                project(0, ("q", 0, b), wq, 0, b, True)
            for b in halves:
                project(0, ("v", b), wkv, 1, b, True)
            for b in halves:
                turn_v(0, b, True)

            def turn(g, last_turn=False):
                def scores(u):
                    h, i = units[u]
                    if i % TPH == 0:
                        name = ("q", h, i // TPH)
                        pe.wait_ge(*(rope_lo.now(g, name) if h else rope_lo.last(g, name)))
                        if h == 0:
                            pe.wait_ge(*rope_lo.last(g, ("k", i // TPH)))
                    pe.wait_ge(*(exped.now(g, units[u - 2]) if u >= 2 else exped.last(g, units[u - 2])))
                    out = score[i % 2]
                    for c in range(i // TPH + 1):
                        keys = slice(c * HALF, min((c + 1) * HALF, (i + 1) * P))
                        diagonal = c == i // TPH
                        last = split_products(nc.tensor, out[:, keys], [part[:, h % 2, tile(i)] for part in qT],
                                              [part[:, keys] for part in kT], True, not diagonal)
                        if diagonal:
                            last = nc.tensor.matmul(out[:, tile(i)], mem.ident_bf[:, :], mem.causal[:, :],
                                                    start=False, stop=True)
                    last.then_inc(scored.sem, 1)

                def turn_probs(u):
                    h, i = units[u]
                    pe.wait_ge(*exped.now(g, (h, i)))
                    for c in range(i // TPH + 1):
                        n = pieces.index((h, i, c))
                        if n < 2:
                            pe.wait_ge(*output_added.last(g, (REP0 - 1, NT - 2 + n)))
                        else:
                            pe.wait_ge(*turned_out.now(g, pieces[n - 2]))
                        for j in range(c * TPH, min((c + 1) * TPH, i + 1)):
                            last = nc.tensor.transpose(turn_bank[n % 2][:, tile(j - c * TPH)], probs[:, i % 2, tile(j)],
                                                       mem.ident[:, :])
                        last.then_inc(turned.sem, 1)

                def values(h, b):
                    use = ("pv", h, b)
                    wait_free(g, use)
                    if h == 0:
                        pe.wait_ge(*v_done.last(g, b))
                    pe.wait_ge(*turned_out.now(g, (h, TPH * (b + 1) - 1, b)))
                    keys = TPH * (b + 1)
                    for j in range(keys):
                        first = max(0, j - TPH * b) * P
                        last = nc.tensor.matmul(bank(use)[:, first:HALF], v[:, j, :], probsT[b][:, j, first:HALF],
                                                start=(j == 0), stop=(j == keys - 1))
                    last.then_inc(full(use).sem, 1)

                def output(h, t):
                    if t % TPH == 0:
                        pe.wait_ge(*values_split.now(g, (h, t // TPH)))
                    if t == 0:
                        pe.wait_ge(*made.now(g, ("o", h)))
                    if h < REP0 - 1:
                        wait_free(g, ("o", h, t))
                        out, done = bank(("o", h, t)), full(("o", h, t))
                    else:
                        pe.wait_ge(*(output_added.now(g, (h, t - 2)) if t >= 2 else turned_out.now(g, pieces[t - 2])))
                        out, done = turn_bank[t % 2], last_output
                    split_products(nc.tensor, out[:, :], [part[:, h % 2, tile(t)] for part in ctxT],
                                   [part[:, h % 2, :] for part in wo], True, True).then_inc(done.sem, 1)

                scores(0)
                for u, (h, i) in enumerate(units):
                    if u < len(units) - 1:
                        scores(u + 1)
                    if h < REP0 - 1 and second_q(h, i):
                        project(g, ("q", h + 1, 1), wq, (h + 1) % 2, 1)
                    elif u == len(units) - 1 and not last_turn:
                        made_before(g, ("k", 0), False)
                        project(g, ("k", 0), wkv, 0, 0)
                    if h > 0:
                        output(h - 1, i)
                        if i == 0:
                            values(h - 1, 1)
                    if i == TPH:
                        values(h, 0)
                    if i == 0 and h == 0:
                        pe.wait_ge(*made.last(g, ("q", 1)))
                        project(g, ("q", 1, 0), wq, 1, 0)
                    turn_probs(u)
                    if i == 0 and 0 < h < REP0 - 1:
                        pe.wait_ge(*made.now(g, ("q", h + 1)))
                        project(g, ("q", h + 1, 0), wq, (h + 1) % 2, 0)
                o = REP0 - 1
                if last_turn:
                    values(o, 1)
                    for t in tiles:
                        output(o, t)
                    return
                project(g, ("k", 1), wkv, 0, 1)
                values(o, 1)
                made_before(g, ("q", 0), False)
                project(g, ("q", 0, 0), wq, 0, 0)
                output(o, 0)
                project(g, ("q", 0, 1), wq, 0, 1)
                output(o, 1)
                project(g, ("v", 0), wkv, 1, 0)
                output(o, 2)
                project(g, ("v", 1), wkv, 1, 1)
                output(o, 3)
                output(o, 4)
                turn_v(g, 0)
                output(o, 5)
                turn_v(g, 1)
                output(o, 6)
                output(o, 7)

            with pe.Fori(0, LAST) as g:
                turn(g)
            turn(LAST, last_turn=True)

        @block.vector
        def _(dve):
            for counter in (rope_mul, rope_sum, rope_hi, rope_lo):
                counter.open(dve, ROPED_AHEAD)
            for counter in (maxed, values_split, inverted, output_added):
                counter.open(dve)
            dve.wait_ge(rope_in, 16)

            def rope_steps(g, name, before_loop=False):
                n, b = roped_halves.index(name), name[-1]
                done = lambda counter: counter.last(0, name) if before_loop else counter.now(g, name)
                hi, lo = ([part[:, half(b)] for part in kT] if name[0] == "k" else
                          [part[:, name[1] % 2, half(b)] for part in qT])
                x, y = plain[:, n % 2, :], exchanged[:, n % 2, :]

                def multiply():
                    dve.wait_ge(*done(projected_out))
                    nc.vector.tensor_tensor(x, x, rope[:, 0, half(b)], ALU.mult)
                    nc.vector.tensor_tensor(y, y, rope[:, 1, half(b)], ALU.mult).then_inc(rope_mul.sem, 1)

                def add():
                    dve.wait_ge(*done(rope_mul))
                    if not before_loop:
                        dve.wait_ge(*(rope_lo.now if n else rope_lo.last)(g, roped_halves[n - 1]))
                    elif n > len(roped_halves) - ROPED_AHEAD:
                        dve.wait_ge(*rope_lo.last(0, roped_halves[n - 1]))
                    nc.vector.tensor_tensor(roped[:, :], x, y, ALU.add).then_inc(rope_sum.sem, 1)

                def high():
                    dve.wait_ge(*done(rope_sum))
                    nc.vector.tensor_copy(hi, roped[:, :]).then_inc(rope_hi.sem, 1)

                def low():
                    dve.wait_ge(*done(rope_hi))
                    nc.vector.tensor_tensor(lo, roped[:, :], hi.bitcast(F32), ALU.subtract).then_inc(rope_lo.sem, 1)

                return multiply, add, high, low

            def take_v(g, b, before_loop=False):
                use = ("vt", b)
                dve.wait_ge(*(full(use).last(0, use) if before_loop else full(use).now(g, use)))
                nc.vector.tensor_copy(v[:, b * TPH:(b + 1) * TPH, :],
                                      bank(use).rearrange("p (t d) -> p t d", t=TPH)).then_inc(v_done.sem, 1)

            for name in roped_halves[-ROPED_AHEAD:]:
                for step in rope_steps(0, name, True):
                    step()
            for b in halves:
                take_v(0, b, True)

            def turn(g, last_turn=False):
                def maximum(u):
                    h, i = units[u]
                    dve.wait_ge(*scored.now(g, (h, i)))
                    nc.vector.reduce_max(neg_max[:, h % 2, i:i + 1], score[i % 2][:, 0:(i + 1) * P], AX.X,
                                         negate=True).then_inc(maxed.sem, 1)

                def invert(h):
                    dve.wait_ge(*exped.now(g, (h, NT - 1)))
                    nc.vector.reciprocal(row_inv[:, h % 2, :], row_sum[:, h % 2, :]).then_inc(inverted.sem, 1)
                    dve.wait_ge(*inverted.now(g, h))

                def add_output(h, t):
                    use = ("o", h, t)
                    last_head = h == REP0 - 1
                    dve.wait_ge(*(last_output.now(g, t) if last_head else full(use).now(g, use)))
                    out = turn_bank[t % 2] if last_head else bank(use)
                    nc.vector.scalar_tensor_tensor(out=mem.x[:, t, :], in0=out[:, :],
                                                   scalar=row_inv[:, h % 2, t:t + 1], in1=mem.x[:, t, :],
                                                   op0=ALU.mult, op1=ALU.add).then_inc(output_added.sem, 1)

                def split_values(h, b):
                    dve.wait_ge(*ctx_hi.now(g, (h, b)))
                    nc.vector.tensor_tensor(ctxT[1][:, h % 2, half(b)], bank(("pv", h, b))[:, :],
                                            ctxT[0][:, h % 2, half(b)].bitcast(F32), ALU.subtract
                                            ).then_inc(values_split.sem, 1)

                maximum(0)
                for u, (h, i) in enumerate(units):
                    if u < len(units) - 1:
                        maximum(u + 1)
                    if i == 0 and h > 0:
                        invert(h - 1)
                    if h > 0:
                        add_output(h - 1, i)
                        if i == 0:
                            for step in rope_steps(g, ("q", h, 1)):
                                step()
                            split_values(h - 1, 1)
                    if h < REP0 - 1 and 2 <= i < NT - 2:
                        rope_steps(g, ("q", h + 1, 0))[i - 2]()
                    if i == TPH:
                        split_values(h, 0)
                o = REP0 - 1
                invert(o)
                if last_turn:
                    split_values(o, 1)
                    for t in tiles:
                        add_output(o, t)
                    return
                k0, k1, q0, q1 = (rope_steps(g, name) for name in roped_halves[-ROPED_AHEAD:])
                for step in k0 + k1:
                    step()
                split_values(o, 1)
                q0[0]()
                q0[1]()
                add_output(o, 0)
                q0[2]()
                q1[0]()
                q0[3]()
                q1[1]()
                add_output(o, 1)
                q1[2]()
                add_output(o, 2)
                q1[3]()
                add_output(o, 3)
                add_output(o, 4)
                take_v(g, 0)
                add_output(o, 5)
                take_v(g, 1)
                add_output(o, 6)
                add_output(o, 7)

            with dve.Fori(0, LAST) as g:
                turn(g)
            turn(LAST, last_turn=True)

        @block.scalar
        def _(act):
            for counter in (exped, turned_out, ctx_hi):
                counter.open(act)
            projected_out.open(act, ROPED_AHEAD + NHALF)
            shift_done.open(act, AHEAD)

            def shift(n):
                nc.scalar.activation(shifted[:, n % 2, :], raw[:, n % RING, :], ACT.Copy, bias=-ZERO_POINT
                                     ).then_inc(shift_done.sem, 1)

            def take_projected(g, name, before_loop=False):
                out, b = bank(name), name[-1]
                if before_loop:
                    act.wait_ge(*full(name).last(0, name))
                else:
                    act.wait_ge(*full(name).now(g, name))
                if name[0] == "v":
                    nc.scalar.copy(vT[:, half(b)], out[:, :]).then_inc(projected_out.sem, 1)
                    return
                n = roped_halves.index(name)
                if before_loop:
                    if n >= len(roped_halves) - ROPED_AHEAD + 2:
                        act.wait_ge(*rope_sum.last(0, roped_halves[n - 2]))
                else:
                    act.wait_ge(*(rope_sum.now(g, roped_halves[n - 2]) if n >= 2 else
                                  rope_sum.last(g, roped_halves[n - 2])))
                factor = SCALE0 if name[0] == "q" else 1.0
                nc.scalar.activation(plain[:, n % 2, :], out[:, :], ACT.Copy, scale=factor)
                nc.scalar.activation(exchanged[0:HH, n % 2, :], out[HH:HD0, :], ACT.Copy, scale=factor)
                nc.scalar.activation(exchanged[HH:HD0, n % 2, :], out[0:HH, :], ACT.Copy, scale=factor
                                     ).then_inc(projected_out.sem, 1)

            for n in range(AT_HOME, len(weights)):
                act.wait_ge(raw_in[n % RING], 32)
                if n >= AT_HOME + 2:
                    act.wait_ge(*scaled.last(0, weights[n - 2]))
                shift(n)
            for name in roped_halves[-ROPED_AHEAD:] + [("v", b) for b in halves]:
                take_projected(0, name, True)

            def turn(g, last_turn=False):
                def shift_next(n):
                    act.wait_ge(*loaded(g, n))
                    act.wait_ge(*steps_before(scaled, g, n, 2))
                    shift(n)

                def exponential(u):
                    h, i = units[u]
                    act.wait_ge(*maxed.now(g, (h, i)))
                    if i == 0:
                        act.wait_ge(*(inverted.now(g, h - 2) if h >= 2 else inverted.last(g, h - 2 + REP0)))
                    nc.scalar.activation(probs[:, i % 2, 0:(i + 1) * P], score[i % 2][:, 0:(i + 1) * P], ACT.Exp,
                                         bias=neg_max[:, h % 2, i:i + 1],
                                         accum_out=row_sum[:, h % 2, i:i + 1]).then_inc(exped.sem, 1)

                def take_turned(u):
                    h, i = units[u]
                    b = i // TPH
                    if i % TPH == 0:
                        use = ("pv", (h - 1) % REP0, b)
                        act.wait_ge(*(full(use).now if h else full(use).last)(g, use))
                    for c in range(b + 1):
                        n = pieces.index((h, i, c))
                        act.wait_ge(*turned.now(g, (h, i, c)))
                        keys = min(TPH, i + 1 - c * TPH)
                        nc.scalar.copy(probsT[b][:, c * TPH:c * TPH + keys, tile(i % TPH)],
                                       turn_bank[n % 2][:, 0:keys * P].rearrange("p (j q) -> p j q", j=keys)
                                       ).then_inc(turned_out.sem, 1)

                def high_values(h, b):
                    use = ("pv", h, b)
                    act.wait_ge(*full(use).now(g, use))
                    nc.scalar.copy(ctxT[0][:, h % 2, half(b)], bank(use)[:, :]).then_inc(ctx_hi.sem, 1)

                n = 0
                exponential(0)
                for u, (h, i) in enumerate(units):
                    if u < len(units) - 1:
                        exponential(u + 1)
                    if i == 0 and h > 0:
                        high_values(h - 1, 1)
                    if i == TPH:
                        high_values(h, 0)
                    if u == len(units) - 1 and not last_turn:
                        take_projected(g, ("k", 0))
                    elif h < REP0 - 1 and second_q(h, i):
                        take_projected(g, ("q", h + 1, 1))
                    if h == 0 and i == 0:
                        take_projected(g, ("q", 1, 0))
                    take_turned(u)
                    if 0 < h < REP0 - 1 and i == 0:
                        take_projected(g, ("q", h + 1, 0))
                    if i in (1, 2, 5) and n < (3, 5, 8, 10)[h] and n < (AT_HOME if last_turn else len(weights)):
                        shift_next(n)
                        n += 1
                if not last_turn:
                    take_projected(g, ("k", 1))
                high_values(REP0 - 1, 1)
                if not last_turn:
                    for name in (("q", 0, 0), ("q", 0, 1), ("v", 0), ("v", 1)):
                        take_projected(g, name)

            with act.Fori(0, LAST) as g:
                turn(g)
            turn(LAST, last_turn=True)


def layer0_ffn_phase(nc, mem, w):
    slots = range(2)
    kts = range(KT)
    with ExitStack() as ctx:
        sem = lambda name: mem.semaphores.enter_context(nc.semaphore("f0_" + name))
        turns = lambda name, names: Turns(sem(name), names)
        sb = lambda name, shape, dt=F32: ctx.enter_context(nc.sbuf_tensor("f0_" + name, shape, dt))
        pair = lambda name, shape: (sb(name + "_hi", shape, F32R), sb(name + "_lo", shape, F32R))
        raw = sb("raw", [P, 2, 3, D])
        raw_b = sb("raw_b", [P, 2, 2, RANK0])
        low_a = sb("low_a", [RANK0, 2, D])
        down_a = sb("down_a", [RANK0, 2, P])
        down_b, down_bT = sb("down_b", [P, KT, RANK0]), sb("down_bT", [RANK0, D])
        low_bT = sb("low_bT", [RANK0, 2, 2, P])
        wT = pair("wT", [P, 2, 2, KT, P])
        downT = pair("downT", [P, NF, D])
        down_full = sb("down_full", [P, D])
        hidden = sb("hidden", [P, NF, S])
        act_t = pair("act_t", [P, 2, NF, P])

        low_in, w_in = sem("low_in"), [sem(f"w_in{s}") for s in slots]
        bT_turned, wT_turned, projected = turns("bT_turned", slots), turns("wT_turned", [(s, m) for s in slots for m in (2, 0, 1)]), turns("projected", slots)
        down_bT_turned, down_bT_out = sem("down_bT_turned"), sem("down_bT_out")
        bT_out, w_hi, silu_done = turns("bT_out", slots), turns("w_hi", [(s, m) for s in slots for m in range(2)]), turns("silu_done", slots)
        w_split, down_gated = turns("w_split", [(s, m) for s in slots for m in (2, 0, 1)]), turns("down_gated", slots)
        down_hi, hidden_done = turns("down_hi", slots), turns("hidden_done", slots)
        cleared, act_hi, act_split, produced, added = sem("cleared"), sem("act_hi"), sem("act_split"), sem("produced"), sem("added")
        wT_bank, small_bank = mem.bank[0:3], mem.bank[3]
        out_pair = [mem.bank_pair4(0), mem.bank_pair4(1)]
        half = lambda b: slice(b * HALF, (b + 1) * HALF)
        LAST = NF - 1
        rows_of = lambda f: HID_LAST if isinstance(f, int) and f == LAST else P
        block = ctx.enter_context(nc.Block())

        def tiles_in_turn(g):
            return [(s, g * 2 + s) for s in slots] if not isinstance(g, int) or g < LAST // 2 else [(0, LAST)]

        @block.sync
        def _(sp):
            sp.dma_start(low_a[:, 0, :], w["gate_a"][:, :]).then_inc(low_in, 16)
            sp.dma_start(low_a[:, 1, :], w["up_a"][:, :]).then_inc(low_in, 16)
            sp.dma_start(down_b[:, :, :], w["down_b"].rearrange("(k p) r -> p k r", p=P)).then_inc(low_in, 16)

            def load(g):
                for s, f in tiles_in_turn(g):
                    r = rows_of(f)
                    rows = bass.ds(f * P, r)
                    sp.wait_ge(*wT_turned.last(g, (s, 1)))
                    sp.dma_start(raw[:r, s, 0, :], w["gate_w"][rows, :]).then_inc(w_in[s], 16)
                    sp.dma_start(raw[:r, s, 1, :], w["up_w"][rows, :]).then_inc(w_in[s], 16)
                    sp.dma_start(raw[:, s, 2, 0:KT * r].rearrange("p (k n) -> p k n", k=KT),
                                 w["down_w"][:, rows].rearrange("(k p) n -> p k n", p=P)).then_inc(w_in[s], 16)
                    sp.dma_start(raw_b[:r, s, 0, :], w["gate_b"][rows, :]).then_inc(w_in[s], 16)
                    sp.dma_start(raw_b[:r, s, 1, :], w["up_b"][rows, :]).then_inc(w_in[s], 16)
                    sp.dma_start(down_a[:, s, 0:r], w["down_a"][:, rows]).then_inc(w_in[s], 16)

            with sp.Fori(0, LAST // 2) as g:
                load(g)
            load(LAST // 2)

        @block.gpsimd
        def _(pool):
            pool.memset(hidden[:, LAST, :], 0.0).then_inc(cleared, 1)

        @block.tensor
        def _(pe):
            for counter in (bT_turned, wT_turned, projected):
                counter.open(pe)
            pe.wait_ge(low_in, 48)
            for k in kts:
                last = nc.tensor.transpose(small_bank[:RANK0, k * P:(k + 1) * P], down_b[:, k, :], mem.ident[:, :])
            last.then_inc(down_bT_turned, 1)
            pe.wait_ge(down_bT_out, 1)

            def prepare(g, s, f):
                r = rows_of(f)
                pe.wait_ge(w_in[s], g * 96 + 96)
                pe.wait_ge(*(bT_out.now(g, 0) if s else bT_out.last(g, 1)))
                for m in range(2):
                    last = nc.tensor.transpose(small_bank[:RANK0, m * P:m * P + r], raw_b[:r, s, m, :],
                                               mem.ident[:r, :r])
                last.then_inc(bT_turned.sem, 1)
                for m in (2, 0, 1):
                    pe.wait_ge(*(w_split.now(g, (0, m)) if s else w_split.last(g, (1, m))))
                    if m == 2:
                        for k in kts:
                            nc.tensor.matmul(wT_bank[2][:r, k * P:(k + 1) * P], raw[:, s, 2, k * r:(k + 1) * r],
                                             mem.ident[:, :], is_transpose=True, start=(k == 0), stop=False)
                        last = nc.tensor.matmul(wT_bank[2][:r, :], down_a[:, s, 0:r], down_bT[:, :],
                                                start=False, stop=True)
                    else:
                        if m == 0:
                            pe.wait_ge(*bT_out.now(g, s))
                        for k in kts:
                            nc.tensor.matmul(wT_bank[m][:, k * P:k * P + r], raw[:r, s, m, k * P:(k + 1) * P],
                                             mem.ident[:r, :r], is_transpose=True, start=(k == 0), stop=False)
                        for k in kts:
                            last = nc.tensor.matmul(wT_bank[m][:, k * P:k * P + r], low_a[:, m, k * P:(k + 1) * P],
                                                    low_bT[:, s, m, 0:r], start=False, stop=(k == KT - 1))
                    last.then_inc(wT_turned.sem, 1)

            def project(g, s, f):
                r = rows_of(f)
                pe.wait_ge(*w_split.now(g, (s, 1)))
                pe.wait_ge(*(hidden_done.now(g, 0) if s else hidden_done.last(g, 1)))
                for m in range(2):
                    for b in range(NHALF):
                        for k in kts:
                            last = split_products(nc.tensor, out_pair[m][:r, half(b)], [part[:, s, m, k, 0:r] for part in wT],
                                                  [part[:, k, half(b)] for part in mem.hT], k == 0, k == KT - 1)
                last.then_inc(projected.sem, 1)

            def turn(g):
                for s, f in tiles_in_turn(g):
                    prepare(g, s, f)
                    project(g, s, f)

            with pe.Fori(0, LAST // 2) as g:
                turn(g)
            turn(LAST // 2)
            for t in range(NT):
                pe.wait_ge(act_split, t + 1)
                if t >= 2:
                    pe.wait_ge(added, t - 1)
                for f in range(NF):
                    r = rows_of(f)
                    last = split_products(nc.tensor, mem.bank[t % 2][:, :], [part[:r, t % 2, f, :] for part in act_t],
                                          [part[:r, f, :] for part in downT], f == 0, f == NF - 1)
                last.then_inc(produced, 1)

        @block.scalar
        def _(act):
            for counter in (bT_out, w_hi, silu_done):
                counter.open(act)
            act.wait_ge(cleared, 1)
            act.wait_ge(down_bT_turned, 1)
            nc.scalar.copy(down_bT[:, :], small_bank[:RANK0, :]).then_inc(down_bT_out, 1)

            def turn(g):
                for s, f in tiles_in_turn(g):
                    r = rows_of(f)
                    act.wait_ge(*bT_turned.now(g, s))
                    nc.scalar.copy(low_bT[:, s, :, 0:r],
                                   small_bank[:RANK0, 0:2 * P].rearrange("r (m n) -> r m n", m=2)[:, :, 0:r]
                                   ).then_inc(bT_out.sem, 1)
                    for m in range(2):
                        act.wait_ge(*wT_turned.now(g, (s, m)))
                        nc.scalar.copy(wT[0][:, s, m, :, 0:r],
                                       wT_bank[m].rearrange("p (k n) -> p k n", k=KT)[:, :, 0:r]).then_inc(w_hi.sem, 1)
                    act.wait_ge(*projected.now(g, s))
                    nc.scalar.activation(hidden[:r, bass.ds(f, 1), :], out_pair[0][:r, :], ACT.Silu).then_inc(silu_done.sem, 1)

            with act.Fori(0, LAST // 2) as g:
                turn(g)
            turn(LAST // 2)

        @block.vector
        def _(dve):
            for counter in (w_split, down_gated, down_hi, hidden_done):
                counter.open(dve)
            dve.wait_ge(cleared, 1)

            def turn(g):
                for s, f in tiles_in_turn(g):
                    r = rows_of(f)
                    at = bass.ds(f, 1)
                    dve.wait_ge(*wT_turned.now(g, (s, 2)))
                    nc.vector.tensor_tensor(down_full[:r, :], wT_bank[2][:r, :], mem.gate[:r, 1, :],
                                            ALU.mult).then_inc(down_gated.sem, 1)
                    dve.wait_ge(*down_gated.now(g, s))
                    nc.vector.tensor_copy(downT[0][:r, at, :], down_full[:r, :]).then_inc(down_hi.sem, 1)
                    dve.wait_ge(*down_hi.now(g, s))
                    nc.vector.tensor_tensor(downT[1][:r, at, :], down_full[:r, :],
                                            downT[0][:r, at, :].bitcast(F32), ALU.subtract).then_inc(w_split.sem, 1)
                    for m in range(2):
                        dve.wait_ge(*w_hi.now(g, (s, m)))
                        nc.vector.tensor_tensor(wT[1][:, s, m, :, 0:r],
                                                wT_bank[m].rearrange("p (k n) -> p k n", k=KT)[:, :, 0:r],
                                                wT[0][:, s, m, :, 0:r].bitcast(F32), ALU.subtract
                                                ).then_inc(w_split.sem, 1)
                    dve.wait_ge(*silu_done.now(g, s))
                    nc.vector.tensor_tensor(hidden[:r, at, :], out_pair[1][:r, :], hidden[:r, at, :], ALU.mult
                                            ).then_inc(hidden_done.sem, 1)

            with dve.Fori(0, LAST // 2) as g:
                turn(g)
            turn(LAST // 2)
            dve.wait_ge(*hidden_done.now(LAST // 2, 0))

            def add(t):
                dve.wait_ge(produced, t + 1)
                nc.vector.tensor_tensor(mem.x[:, t, :], mem.bank[t % 2][:, :], mem.x[:, t, :], ALU.add).then_inc(added, 1)

            for t in range(NT):
                part = hidden[:, :, t * P:(t + 1) * P]
                nc.vector.tensor_copy(act_t[0][:, t % 2, :, :], part).then_inc(act_hi, 1)
                dve.wait_ge(act_hi, t + 1)
                nc.vector.tensor_tensor(act_t[1][:, t % 2, :, :], part, act_t[0][:, t % 2, :, :].bitcast(F32),
                                        ALU.subtract).then_inc(act_split, 1)
                if t:
                    add(t - 1)
            add(NT - 1)


def layer1_qkv_phase(nc, mem, k1, v1, rope_dram, w_dram, b_dram):
    NC = QKV1 // P
    NH, NP = NH1 + NKV1, HD1 // 2
    QW = NH1 * HD1
    with ExitStack() as ctx:
        sem = lambda name: mem.semaphores.enter_context(nc.semaphore("p1_" + name))
        sb = lambda name, shape, dt=F32: ctx.enter_context(nc.sbuf_tensor("p1_" + name, shape, dt))
        raw = sb("raw", [P, NC, D])
        bias = sb("bias", [P, QKV1])
        rope = sb("rope", [P, NT, 2, NP])
        wT = (sb("wT_hi", [P, KT, QKV1], F32R), sb("wT_lo", [P, KT, QKV1], F32R))
        qkv = sb("qkv", [P, NT, QKV1])
        part = [sb(f"part{n}", [P, 2, NH, NP]) for n in range(4)]
        roped = sb("roped", [P, 2, NH, HD1])
        q1 = [mem.hT[n].rearrange("p k s -> p (k s)").rearrange("p (t d) -> p t d", t=NT) for n in range(2)]
        w_in, small_in = sem("w_in"), sem("small_in")
        wT_turned, w_hi, w_split = sem("wT_turned"), sem("w_hi"), sem("w_split")
        projected, biased, rotated, summed, hi_done, split = (sem("projected"), sem("biased"), sem("rotated"),
                                                              sem("summed"), sem("hi_done"), sem("split"))
        block = ctx.enter_context(nc.Block())

        @block.sync
        def _(sp):
            sp.dma_start(raw[:, :, :], w_dram.rearrange("(c p) d -> p c d", p=P)).then_inc(w_in, 16)
            sp.dma_start(bias[:, :], b_dram.unsqueeze(0).broadcast_to([P, QKV1])).then_inc(small_in, 16)
            sp.dma_start(rope[:, :, :, :], rope_dram.rearrange("(t p) a f -> p t a f", p=P)).then_inc(small_in, 16)

        @block.tensor
        def _(pe):
            pe.wait_ge(w_in, 16)
            for k in range(KT):
                if k >= 2:
                    pe.wait_ge(w_split, k - 1)
                for c in range(NC):
                    last = nc.tensor.transpose(mem.bank_pair[k % 2][:, c * P:(c + 1) * P],
                                               raw[:, c, k * P:(k + 1) * P], mem.ident[:, :])
                last.then_inc(wT_turned, 1)
            pe.wait_ge(w_split, KT)
            for t in range(NT):
                if t >= 2:
                    pe.wait_ge(biased, t - 1)
                for cols in (slice(0, HALF), slice(HALF, QKV1)):
                    for k in range(KT):
                        last = split_products(nc.tensor, mem.bank_pair4(t % 2)[:, cols],
                                              [a[:, k, t * P:(t + 1) * P] for a in mem.hT],
                                              [a[:, k, cols] for a in wT], k == 0, k == KT - 1)
                last.then_inc(projected, 1)

        @block.scalar
        def _(act):
            for k in range(KT):
                act.wait_ge(wT_turned, k + 1)
                nc.scalar.copy(wT[0][:, k, :], mem.bank_pair[k % 2][:, 0:QKV1]).then_inc(w_hi, 1)

        @block.vector
        def _(dve):
            for k in range(KT):
                dve.wait_ge(w_hi, k + 1)
                nc.vector.tensor_tensor(wT[1][:, k, :], mem.bank_pair[k % 2][:, 0:QKV1],
                                        wT[0][:, k, :].bitcast(F32), ALU.subtract).then_inc(w_split, 1)
            dve.wait_ge(small_in, 32)
            for t in range(NT):
                dve.wait_ge(projected, t + 1)
                nc.vector.tensor_tensor(qkv[:, t, :], mem.bank_pair4(t % 2)[:, 0:QKV1], bias[:, :], ALU.add
                                        ).then_inc(biased, 1)
            dve.wait_ge(biased, NT)

            def rotate(t):
                x = qkv[:, t, 0:QK1].rearrange("p (h f two) -> p h f two", two=2, f=NP)
                turn = [rope[:, t, n, :].unsqueeze(1).broadcast_to([P, NH, NP]) for n in range(2)]
                for n, (a, b) in enumerate(((0, 0), (1, 1), (0, 1), (1, 0))):
                    last = nc.vector.tensor_tensor(part[n][:, t % 2, :, :], x[:, :, :, a], turn[b], ALU.mult)
                last.then_inc(rotated, 1)
                nc.vector.tensor_copy(v1[:, t, :], qkv[:, t, QK1:QKV1])

            def combine(t):
                dve.wait_ge(rotated, t + 1)
                r = roped[:, t % 2, :, :]
                nc.vector.tensor_tensor(r[:, :, 0:NP], part[0][:, t % 2], part[1][:, t % 2], ALU.subtract)
                nc.vector.tensor_tensor(r[:, :, NP:HD1], part[2][:, t % 2], part[3][:, t % 2], ALU.add).then_inc(summed, 1)

            def high(t):
                dve.wait_ge(summed, t + 1)
                r = roped[:, t % 2, :, :].rearrange("p h d -> p (h d)")
                nc.vector.tensor_scalar(q1[0][:, t, :], r[:, 0:QW], SCALE1, None, ALU.mult)
                nc.vector.tensor_copy(k1[0][:, t, :], r[:, QW:QK1]).then_inc(hi_done, 1)

            def low(t):
                dve.wait_ge(hi_done, t + 1)
                r = roped[:, t % 2, :, :].rearrange("p h d -> p (h d)")
                nc.vector.scalar_tensor_tensor(out=q1[1][:, t, :], in0=r[:, 0:QW], scalar=SCALE1,
                                               in1=q1[0][:, t, :].bitcast(F32), op0=ALU.mult, op1=ALU.subtract)
                nc.vector.tensor_tensor(k1[1][:, t, :], r[:, QW:QK1], k1[0][:, t, :].bitcast(F32),
                                        ALU.subtract).then_inc(split, 1)

            rotate(0)
            for t in range(NT):
                combine(t)
                if t < NT - 1:
                    rotate(t + 1)
                high(t)
                low(t)
                dve.wait_ge(split, t + 1)


def layer1_attention_phase(nc, mem, k1, v1, attended):
    heads, tiles, halves, pairs = range(REP1), range(NT), range(NHALF), range(REP1 // 2)
    STACK = 64
    PARTS = 3
    USED = PARTS * HD1
    MAX_HI, MAX_LO = USED, USED + 1
    VW = 32
    SLOTS = 3
    LAST = NKV1 - 1
    xs = [(b, j, h) for b in halves for j in range(TPH * (b + 1)) for h in heads]
    steps = [(b, j) for b in halves for j in range(TPH * (b + 1))]
    ys = [(h, i, c) for b in halves for h in heads for i in range(b * TPH, (b + 1) * TPH) for c in range(b + 1)]
    Y_HALF = [n for n, y in enumerate(ys) if y[1] < TPH][-1]
    at = {1: [("kA", 0)], 4: [("qA", 0, 0)], 6: [("qB", 1, 0)], 8: [("qB", 1, 1)], 10: [("qA", 0, 1)], 12: [("kA", 1)],
          15: [("qA", 1, 0)], 17: [("qA", 1, 1)], 20: [("ctx", 0)], 25: [("qB", 0, 0)], 27: [("qB", 0, 1)]}
    FIRST_Y = 7
    order, y = [], 0
    for n in range(len(xs)):
        order += at.get(n, []) + [("x", n)]
        while n >= FIRST_Y and y < min(len(ys), (n - FIRST_Y + 1) * 6 // 5):
            order.append(("y", y))
            y += 1
        if n % REP1 == 1 and n > REP1:
            order.append(("pv", n // REP1 - 1))
    order += [("pv", len(steps) - 1), ("ctx", 1)]
    assert y == len(ys)
    OWN = ("x", "pv", "ctx")
    is_own = lambda step: step[0] in OWN or step[:2] == ("qB", 1)
    staging = [step for step in order if step[0] in ("kA", "qA", "qB", "ctx")]
    order_first = [step for step in order if not is_own(step)]
    order_last = [step for step in order if is_own(step)]
    q1 = [mem.hT[n].rearrange("p k s -> p (k s)").rearrange("p (t d) -> p t d", t=NT) for n in range(2)]

    class Groups(Turns):

        def now(self, group, name):
            return self.sem, group[0] * self.n + (group[1] + 1) * self.n + self.names.index(name) + 1

        def last(self, group, name):
            return self.sem, group[0] * self.n + group[1] * self.n + self.names.index(name) + 1

    with ExitStack() as ctx:
        sem = lambda name: mem.semaphores.enter_context(nc.semaphore("a1_" + name))
        groups = lambda name, names: Groups(sem(name), names)
        sb = lambda name, shape, dt=F32: ctx.enter_context(nc.sbuf_tensor("a1_" + name, shape, dt))
        q_stack, k_stack = sb("q_stack", [P, NT, REP1, STACK]), sb("k_stack", [P, NT, 2, STACK])
        v, zero = sb("v", [P, NT, VW]), sb("zero", [P, 1])
        qA, qB = sb("qA", [P, len(pairs), S], F32R), sb("qB", [P, len(pairs), S], F32R)
        kA, kB = sb("kA", [P, 2, S], F32R), sb("kB", [P, 2, S], F32R)
        probsT = sb("probsT", [P, SLOTS, REP1, HALF])
        ctxT = sb("ctxT", [P, HALF])
        neg_max, row_inv = sb("neg_max", [P, NHALF, NT, REP1]), sb("row_inv", [P, TPH, REP1])
        cleared, filled = sem("cleared"), sem("filled")
        k_stacked, q_stacked = groups("k_stacked", ["k"]), groups("q_stacked", halves)
        kB_begun, kB_made, v_made = groups("kB_begun", halves), groups("kB_made", halves), groups("v_made", halves)
        kA_turned = groups("kA_turned", halves)
        qA_turned = groups("qA_turned", [(b, p) for b in halves for p in pairs])
        qB_turned = groups("qB_turned", [(b, p) for b in halves for p in pairs])
        x_scored, y_scored = groups("x_scored", range(len(xs))), groups("y_scored", range(len(ys)))
        valued, ctx_turned = groups("valued", steps), groups("ctx_turned", halves)
        qA_out = groups("qA_out", [(b, p) for b in halves for p in pairs])
        qB_out = groups("qB_out", [(b, p) for b in halves for p in pairs])
        exped, ctx_out = groups("exped", range(len(xs))), groups("ctx_out", halves)
        kA_out, maxed = groups("kA_out", halves), groups("maxed", range(len(ys)))
        combined, max_hi, max_placed = groups("combined", ["max"]), groups("max_hi", halves), groups("max_placed", halves)
        inverted, attended_done = groups("inverted", halves), groups("attended_done", halves)
        x_bank, y_bank = mem.bank[0:3], mem.bank[3:6]
        value_bank, stage_bank = mem.bank[6], mem.bank[7]
        staging_out = {"kA": kA_out, "qA": qA_out, "qB": qB_out, "ctx": attended_done}
        tile = lambda i: slice(i * P, (i + 1) * P)
        half = lambda b: slice(b * HALF, (b + 1) * HALF)
        in_half = lambda b: slice(b * TPH, (b + 1) * TPH)
        both = [slice(0, STACK), slice(STACK, 2 * STACK)]
        block = ctx.enter_context(nc.Block())

        @block.gpsimd
        def _(pool):
            clear = [v[:, :, :], q_stack[:, :, :, :], k_stack[:, :, :, :], kA[:, :, :].bitcast(F32),
                     kB[:, :, :].bitcast(F32), zero[:, :]]
            for buffer in clear:
                pool.memset(buffer, 0.0).then_inc(cleared, 1)
            for counter in (k_stacked, q_stacked, kB_begun, kB_made, v_made):
                counter.open(pool)
            pool.wait_ge(cleared, len(clear))
            pool.memset(v[:, :, HD1:HD1 + 1], 1.0).then_inc(filled, 1)
            for n in range(2):
                pool.wait_ge(filled, n + 1)
                pool.memset(kB[n * STACK + 32:(n + 1) * STACK, n, :].bitcast(F32), 1.0).then_inc(filled, 1)
            pool.wait_ge(filled, 3)

            def from_group(group, width):
                return bass.ds(group[0] * width + group[1] * width, width)

            def stack_k(group):
                pool.wait_ge(*kA_turned.last(group, NHALF - 1))
                for n, of in enumerate((0, 0, 1)):
                    source = k1[of][:, :, from_group(group, HD1)].bitcast(F32)
                    last = pool.tensor_tensor(k_stack[:, :, :, n * HD1:(n + 1) * HD1],
                                              source.unsqueeze(2).broadcast_to([P, NT, 2, HD1]),
                                              zero[:, :].unsqueeze(2).unsqueeze(3).broadcast_to([P, NT, 2, HD1]), ALU.add)
                last.then_inc(k_stacked.sem, 1)

            def stack_q(group, b):
                pool.wait_ge(*qB_turned.last(group, (b, pairs[-1])))
                for n, of in enumerate((0, 1, 0)):
                    source = q1[of][:, in_half(b), from_group(group, REP1 * HD1)].bitcast(F32)
                    last = pool.tensor_tensor(q_stack[:, in_half(b), :, n * HD1:(n + 1) * HD1],
                                              source.rearrange("p t (h d) -> p t h d", h=REP1),
                                              zero[:, :].unsqueeze(2).unsqueeze(3).broadcast_to([P, TPH, REP1, HD1]),
                                              ALU.add)
                last.then_inc(q_stacked.sem, 1)

            def copy_k(group, b):
                pool.wait_ge(*kA_out.now(group, b))
                pool.wait_ge(*x_scored.last(group, xs.index((1, TPH * (b + 1) - 1, REP1 - 1))))
                for n, counter in enumerate((kB_begun, kB_made)):
                    rows = slice(n * STACK, n * STACK + USED)
                    pool.tensor_tensor(kB[rows, n, half(b)], kA[rows, n, half(b)].bitcast(F32),
                                       zero[rows, :].broadcast_to([USED, HALF]), ALU.add).then_inc(counter.sem, 1)
                    pool.wait_ge(*counter.now(group, b))

            def make_v(group, b):
                pool.wait_ge(*valued.last(group, (1, TPH * (b + 1) - 1)))
                pool.tensor_tensor(v[:, in_half(b), 0:HD1], v1[:, in_half(b), from_group(group, HD1)],
                                   zero[:, :].unsqueeze(2).broadcast_to([P, TPH, HD1]), ALU.add).then_inc(v_made.sem, 1)

            def turn(g, ahead=2):
                own, following, second = (g, 0), (g, 1), (g, 2)
                copy_k(own, 1)
                make_v(own, 1)
                if ahead >= 1:
                    stack_q(following, 1)
                if ahead == 2:
                    stack_k(second)
                    stack_q(second, 0)
                if ahead >= 1:
                    copy_k(following, 0)
                    make_v(following, 0)

            stack_k((0, 0))
            stack_q((0, 0), 0)
            stack_q((0, 0), 1)
            stack_k((0, 1))
            stack_q((0, 1), 0)
            copy_k((0, 0), 0)
            make_v((0, 0), 0)
            with pool.Fori(0, LAST - 1) as g:
                turn(g)
            turn(LAST - 1, ahead=1)
            turn(LAST, ahead=0)

        @block.tensor
        def _(pe):
            for counter in (kA_turned, qA_turned, qB_turned, x_scored, y_scored, valued, ctx_turned):
                counter.open(pe)
            pe.wait_ge(filled, 3)

            def wait_stage_bank(own, following, step, of_order):
                uses = [s for s in staging if s in of_order]
                n = uses.index(step)
                if n:
                    before = uses[n - 1]
                    name = before[1] if before[0] in ("kA", "ctx") else before[1:]
                    pe.wait_ge(*staging_out[before[0]].now(own if is_own(before) else following, name))
                else:
                    pe.wait_ge(*attended_done.last(own, 1))

            def turn_k(group, b):
                if b == 0:
                    pe.wait_ge(*k_stacked.now(group, "k"))
                for t in range(TPH):
                    last = nc.tensor.transpose(stage_bank[:, tile(t)],
                                               k_stack[:, b * TPH + t, :, :].rearrange("p n r -> p (n r)"), mem.ident[:, :])
                last.then_inc(kA_turned.sem, 1)

            def turn_q(group, b, p, counter):
                for t in range(TPH):
                    stack = q_stack[:, b * TPH + t, 2 * p:2 * p + 2, :].rearrange("p n r -> p (n r)")
                    last = nc.tensor.transpose(stage_bank[:, tile(t)], stack, mem.ident[:, :])
                last.then_inc(counter.sem, 1)

            def score_x(group, n):
                b, j, h = xs[n]
                if (j, h) == (0, 0):
                    pe.wait_ge(*qB_out.now(group, (b, pairs[-1])))
                if h == 0 and j == TPH * b:
                    pe.wait_ge(*kB_made.now(group, b))
                pe.wait_ge(*(exped.now if n >= SLOTS else exped.last)(group, (n - SLOTS) % len(xs)))
                first = max(0, j - TPH * b) * P
                diagonal = j >= TPH * b
                out = x_bank[n % SLOTS]
                last = nc.tensor.matmul(out[:, first:HALF], kB[:, h % 2, tile(j)],
                                        qB[:, h // 2, b * HALF + first:(b + 1) * HALF], start=True, stop=not diagonal)
                if diagonal:
                    last = nc.tensor.matmul(out[:, first:first + P], mem.causal[:, :], mem.ident_bf[:, :],
                                            start=False, stop=True)
                last.then_inc(x_scored.sem, 1)

            def score_y(group, n):
                h, i, c = ys[n]
                b = i // TPH
                if i % TPH == 0 and c == 0 and h == 0:
                    pe.wait_ge(*kA_out.now(group, b))
                if i % TPH == 0 and c == 0 and h % 2 == 0:
                    pe.wait_ge(*qA_out.now(group, (b, h // 2)))
                pe.wait_ge(*(maxed.now if n >= SLOTS else maxed.last)(group, (n - SLOTS) % len(ys)))
                keys = min(HALF, (i + 1) * P - c * HALF)
                diagonal = c == b
                out = y_bank[n % SLOTS]
                last = nc.tensor.matmul(out[:, 0:keys], qA[:, h // 2, tile(i)],
                                        kA[:, h % 2, c * HALF:c * HALF + keys], start=True, stop=not diagonal)
                if diagonal:
                    last = nc.tensor.matmul(out[:, keys - P:keys], mem.ident_bf[:, :], mem.causal[:, :],
                                            start=False, stop=True)
                last.then_inc(y_scored.sem, 1)

            def values(group, s):
                b, j = steps[s]
                if j == 0:
                    pe.wait_ge(*(ctx_out.now(group, 0) if b else ctx_out.last(group, 1)))
                if j == TPH * b:
                    pe.wait_ge(*v_made.now(group, b))
                pe.wait_ge(*exped.now(group, xs.index((b, j, REP1 - 1))))
                first = max(0, j - TPH * b) * P
                for h in heads:
                    last = nc.tensor.matmul(value_bank[h * VW:(h + 1) * VW, first:HALF], v[:, j, :],
                                            probsT[:, s % SLOTS, h, first:HALF], start=(j == 0),
                                            stop=(j == TPH * (b + 1) - 1))
                last.then_inc(valued.sem, 1)

            def turn_values(group, b):
                pe.wait_ge(*ctx_out.now(group, b))
                for t in range(TPH):
                    last = nc.tensor.transpose(stage_bank[:, tile(t)], ctxT[:, tile(t)], mem.ident[:, :])
                last.then_inc(ctx_turned.sem, 1)

            def turn(own, following, of_order):
                for step in of_order:
                    kind, rest = step[0], step[1:]
                    if kind == "x":
                        score_x(own, *rest)
                    elif kind == "y":
                        score_y(following, *rest)
                    elif kind == "pv":
                        values(own, *rest)
                    else:
                        wait_stage_bank(own, following, step, of_order)
                        if kind == "kA":
                            turn_k(following, *rest)
                        elif kind == "qA":
                            if rest[1] == 0:
                                pe.wait_ge(*q_stacked.now(following, rest[0]))
                            turn_q(following, *rest, qA_turned)
                        elif kind == "qB":
                            group = own if is_own(step) else following
                            pe.wait_ge(*max_placed.now(group, rest[0]))
                            turn_q(group, *rest, qB_turned)
                        else:
                            turn_values(own, *rest)

            turn((0, -1), (0, 0), order_first)
            pe.wait_ge(*qB_out.now((0, 0), (0, pairs[-1])))
            with pe.Fori(0, LAST) as g:
                turn((g, 0), (g, 1), order)
            turn((LAST, 0), None, order_last)

        @block.vector
        def _(dve):
            for counter in (kA_out, maxed, combined, max_hi, max_placed, inverted, attended_done):
                counter.open(dve)
            dve.wait_ge(filled, 3)

            def take_k(group, b):
                dve.wait_ge(*kA_turned.now(group, b))
                dve.wait_ge(*kB_made.last(group, b))
                for n in range(2):
                    rows = slice(n * STACK, n * STACK + USED)
                    last = nc.vector.tensor_copy(kA[rows, n, half(b)], stage_bank[rows, :])
                last.then_inc(kA_out.sem, 1)

            def maximum(group, n):
                h, i, c = ys[n]
                dve.wait_ge(*y_scored.now(group, n))
                keys = min(HALF, (i + 1) * P - c * HALF)
                nc.vector.reduce_max(neg_max[:, c, i, h:h + 1], y_bank[n % SLOTS][:, 0:keys], AX.X,
                                     negate=True).then_inc(maxed.sem, 1)

            def place_maxima(group, b):
                t = in_half(b)
                dve.wait_ge(*maxed.now(group, len(ys) - 1 if b else Y_HALF))
                if b:
                    nc.vector.tensor_tensor(neg_max[:, 0, t, :], neg_max[:, 0, t, :], neg_max[:, 1, t, :],
                                            ALU.min).then_inc(combined.sem, 1)
                    dve.wait_ge(*combined.now(group, "max"))
                nc.vector.tensor_copy(q_stack[:, t, :, MAX_HI].bitcast(F32R), neg_max[:, 0, t, :]).then_inc(max_hi.sem, 1)
                dve.wait_ge(*max_hi.now(group, b))
                nc.vector.tensor_tensor(q_stack[:, t, :, MAX_LO], neg_max[:, 0, t, :], q_stack[:, t, :, MAX_HI],
                                        ALU.subtract).then_inc(max_placed.sem, 1)

            def normalize(group, b):
                dve.wait_ge(*ctx_turned.now(group, b))
                out = stage_bank.rearrange("p (t h w) -> p t h w", t=TPH, h=REP1)
                nc.vector.reciprocal(row_inv[:, :, :], out[:, :, :, HD1]).then_inc(inverted.sem, 1)
                dve.wait_ge(*inverted.now(group, b))
                nc.vector.tensor_tensor(
                    attended[:, in_half(b), bass.ds(group[0] * (REP1 * HD1), REP1 * HD1)]
                    .rearrange("p t (h d) -> p t h d", h=REP1), out[:, :, :, 0:HD1],
                    row_inv[:, :, :].unsqueeze(3).broadcast_to([P, TPH, REP1, HD1]), ALU.mult
                    ).then_inc(attended_done.sem, 1)

            def turn(own, following, of_order):
                for step in of_order:
                    kind, rest = step[0], step[1:]
                    if kind == "kA":
                        take_k(following, *rest)
                    elif kind == "y":
                        maximum(following, *rest)
                        if rest[0] == Y_HALF:
                            place_maxima(following, 0)
                        elif rest[0] == len(ys) - 1:
                            place_maxima(following, 1)
                    elif kind == "ctx":
                        normalize(own, *rest)

            turn((0, -1), (0, 0), order_first)
            with dve.Fori(0, LAST) as g:
                turn((g, 0), (g, 1), order)
            turn((LAST, 0), None, order_last)

        @block.scalar
        def _(act):
            for counter in (qA_out, qB_out, exped, ctx_out):
                counter.open(act)

            def take_q(group, b, p, turned, out, counter):
                act.wait_ge(*turned.now(group, (b, p)))
                nc.scalar.copy(out[:, p, half(b)], stage_bank[:, :]).then_inc(counter.sem, 1)

            def exponential(group, n):
                b, j, h = xs[n]
                s = steps.index((b, j))
                if h == 0:
                    act.wait_ge(*(valued.now if s >= SLOTS else valued.last)(group, steps[(s - SLOTS) % len(steps)]))
                act.wait_ge(*x_scored.now(group, n))
                first = max(0, j - TPH * b) * P
                nc.scalar.activation(probsT[:, s % SLOTS, h, first:HALF], x_bank[n % SLOTS][:, first:HALF], ACT.Exp
                                     ).then_inc(exped.sem, 1)

            def take_values(group, b):
                act.wait_ge(*valued.now(group, (b, TPH * (b + 1) - 1)))
                act.wait_ge(*(ctx_turned.now(group, 0) if b else ctx_turned.last(group, 1)))
                nc.scalar.copy(ctxT[:, :], value_bank[:, :]).then_inc(ctx_out.sem, 1)

            def turn(own, following, of_order):
                for step in of_order:
                    kind, rest = step[0], step[1:]
                    if kind == "qA":
                        act.wait_ge(*y_scored.last(following, len(ys) - 1 if rest[0] else Y_HALF))
                        take_q(following, *rest, qA_turned, qA, qA_out)
                    elif kind == "qB":
                        take_q(own if is_own(step) else following, *rest, qB_turned, qB, qB_out)
                    elif kind == "x":
                        exponential(own, *rest)
                    elif kind == "pv" and steps[rest[0]][1] == TPH * (steps[rest[0]][0] + 1) - 1:
                        take_values(own, steps[rest[0]][0])

            turn((0, -1), (0, 0), order_first)
            with act.Fori(0, LAST) as g:
                turn((g, 0), (g, 1), order)
            turn((LAST, 0), None, order_last)


def layer1_output_phase(nc, mem, attended, w_dram, b_dram):
    with ExitStack() as ctx:
        sem = lambda name: mem.semaphores.enter_context(nc.semaphore("o1_" + name))
        sb = lambda name, shape, dt=F32: ctx.enter_context(nc.sbuf_tensor("o1_" + name, shape, dt))
        raw, bias = sb("raw", [P, KT, D]), sb("bias", [P, D])
        gated = sb("gated", [P, KT, D])
        wT = (sb("wT_hi", [P, KT, D], F32R), sb("wT_lo", [P, KT, D], F32R))
        aT = mem.hT
        w_in, b_in = sem("w_in"), sem("b_in")
        w_turned, w_gated, w_hi, w_split = sem("w_turned"), sem("w_gated"), sem("w_hi"), sem("w_split")
        a_turned, a_hi, a_split = sem("a_turned"), sem("a_hi"), sem("a_split")
        bias_gated, biased, produced, added = sem("bias_gated"), sem("biased"), sem("produced"), sem("added")
        pieces = [(half, k) for half in range(NHALF) for k in range(KT)]
        block = ctx.enter_context(nc.Block())

        @block.sync
        def _(sp):
            sp.dma_start(raw[:, :, :], w_dram.rearrange("(c p) d -> p c d", p=P)).then_inc(w_in, 16)
            sp.dma_start(bias[:, :], b_dram.unsqueeze(0).broadcast_to([P, D])).then_inc(b_in, 16)

        @block.gpsimd
        def _(pool):
            pool.wait_ge(b_in, 16)
            pool.tensor_tensor(bias[:, :], bias[:, :], mem.gate[:, 2, :], ALU.mult).then_inc(bias_gated, 1)
            pool.wait_ge(bias_gated, 1)
            for t in range(NT):
                last = pool.tensor_tensor(mem.x[:, t, :], mem.x[:, t, :], bias[:, :], ALU.add).then_inc(biased, 1)

        @block.tensor
        def _(pe):
            for i, (half, k) in enumerate(pieces):
                if i >= 2:
                    pe.wait_ge(a_split, i - 1)
                for t in range(TPH):
                    last = nc.tensor.transpose(mem.bank[i % 2][:, t * P:(t + 1) * P],
                                               attended[:, half * TPH + t, k * P:(k + 1) * P], mem.ident[:, :])
                last.then_inc(a_turned, 1)
            pe.wait_ge(w_in, 16)
            for k in range(KT):
                if k >= 2:
                    pe.wait_ge(w_gated, k - 1)
                for c in range(KT):
                    last = nc.tensor.transpose(mem.bank[2 + k % 2][:, c * P:(c + 1) * P], raw[:, c, k * P:(k + 1) * P],
                                               mem.ident[:, :])
                last.then_inc(w_turned, 1)
            pe.wait_ge(w_split, KT)
            for t in range(NT):
                if t >= 2:
                    pe.wait_ge(added, t - 1)
                for k in range(KT):
                    last = split_products(nc.tensor, mem.bank[4 + t % 2][:, :], [a[:, k, t * P:(t + 1) * P] for a in aT],
                                          [a[:, k, :] for a in wT], k == 0, k == KT - 1)
                last.then_inc(produced, 1)

        @block.scalar
        def _(act):
            for i, (half, k) in enumerate(pieces):
                act.wait_ge(a_turned, i + 1)
                nc.scalar.copy(aT[0][:, k, half * HALF:(half + 1) * HALF], mem.bank[i % 2][:, :]).then_inc(a_hi, 1)
            for k in range(KT):
                act.wait_ge(w_gated, k + 1)
                nc.scalar.copy(wT[0][:, k, :], gated[:, k, :]).then_inc(w_hi, 1)

        @block.vector
        def _(dve):
            for i, (half, k) in enumerate(pieces):
                cols = slice(half * HALF, (half + 1) * HALF)
                dve.wait_ge(a_hi, i + 1)
                nc.vector.tensor_tensor(aT[1][:, k, cols], mem.bank[i % 2][:, :], aT[0][:, k, cols].bitcast(F32),
                                        ALU.subtract).then_inc(a_split, 1)
            for k in range(KT):
                dve.wait_ge(w_turned, k + 1)
                nc.vector.tensor_tensor(gated[:, k, :], mem.bank[2 + k % 2][:, :], mem.gate[:, 2, :], ALU.mult
                                        ).then_inc(w_gated, 1)
            for k in range(KT):
                dve.wait_ge(w_hi, k + 1)
                nc.vector.tensor_tensor(wT[1][:, k, :], gated[:, k, :], wT[0][:, k, :].bitcast(F32), ALU.subtract
                                        ).then_inc(w_split, 1)
            for t in range(NT):
                dve.wait_ge(produced, t + 1)
                dve.wait_ge(biased, t + 1)
                nc.vector.tensor_tensor(mem.x[:, t, :], mem.bank[4 + t % 2][:, :], mem.x[:, t, :], ALU.add
                                        ).then_inc(added, 1)


def layer1_experts_phase(nc, mem, x_out, w):
    RT = (ER + P - 1) // P
    R_OF = [P, ER - P]
    LW = NE + ER
    with ExitStack() as ctx:
        sem = lambda name: mem.semaphores.enter_context(nc.semaphore("e1_" + name))
        sb = lambda name, shape, dt=F32: ctx.enter_context(nc.sbuf_tensor("e1_" + name, shape, dt))
        pair = lambda name, shape: (sb(name + "_hi", shape, F32R), sb(name + "_lo", shape, F32R))
        raw, raw_a, raw_g = sb("raw", [P, KT, D]), sb("raw_a", [P, RT, D]), sb("raw_g", [NE, D])
        raw_b = sb("raw_b", [P, KT, NE, RANK1])
        gated = sb("gated", [P, 2, D])
        wT, aT = pair("wT", [P, KT, D]), pair("aT", [P, KT, LW])
        bT = pair("bT", [P, RT, D])
        number = sb("number", [P, NE], I32)
        numberf = sb("numberf", [P, NE])
        low_all = sb("low_all", [P, NT, LW])
        top, index, indexf = sb("top", [P, NT, 8]), sb("index", [P, NT, 8], U32), sb("indexf", [P, NT, 2])
        gap, exped, prob = sb("gap", [P, NT]), sb("exped", [P, NT]), sb("prob", [P, NT, 2])
        chosen, mix = sb("chosen", [P, 2, NE]), sb("mix", [P, NE])
        scaled = sb("scaled", [P, 2, ER])
        sT = pair("sT", [P, 2, RT, P])
        w_in, a_in, b_in = sem("w_in"), sem("a_in"), sem("b_in")
        w_turned, w_gated, w_hi, w_split = sem("w_turned"), sem("w_gated"), sem("w_hi"), sem("w_split")
        a_turned, a_hi, a_split = sem("a_turned"), sem("a_hi"), sem("a_split")
        counted, numbered = sem("counted"), sem("numbered")
        logits_done, logits_out, topped, indexed = sem("logits_done"), sem("logits_out"), sem("topped"), sem("indexed")
        step, gapped, exp_done = sem("step"), sem("gapped"), sem("exp_done")
        scaled_done, s_turned, s_hi, s_split = sem("scaled_done"), sem("s_turned"), sem("s_hi"), sem("s_split")
        produced, added, stored = sem("produced"), sem("added"), sem("stored")
        mats = [("w", k) for k in range(KT)] + [("b", r) for r in range(RT)]
        block = ctx.enter_context(nc.Block())

        @block.sync
        def _(sp):
            sp.dma_start(raw_g[:, :], w["gate"][:, :]).then_inc(a_in, 16)
            a = w["a"].rearrange("e r d -> (e r) d")
            sp.dma_start(raw_a[:, 0, :], a[0:P, :]).then_inc(a_in, 16)
            sp.dma_start(raw_a[:R_OF[1], 1, :], a[P:ER, :]).then_inc(a_in, 16)
            sp.dma_start(raw[:, :, :], w["base"].rearrange("(c p) d -> p c d", p=P)).then_inc(w_in, 16)
            for c in range(KT):
                sp.dma_start(raw_b[:, c, :, :], w["b"][:, c * P:(c + 1) * P, :].rearrange("e p r -> p e r")
                             ).then_inc(b_in, 16)
            for t in range(NT):
                sp.wait_ge(added, t + 1)
                sp.dma_start(x_out[0, t * P:(t + 1) * P, :], mem.x[:, t, :]).then_inc(stored, 16)
            sp.wait_ge(stored, 16 * NT)

        @block.gpsimd
        def _(pool):
            pool.iota(number[:, :], [[1, NE]], base=0, channel_multiplier=0).then_inc(counted, 1)

        @block.tensor
        def _(pe):
            pe.wait_ge(a_in, 48)
            for k in range(KT):
                if k >= 2:
                    pe.wait_ge(a_split, k - 1)
                out = mem.bank[k % 2]
                cols = slice(k * P, (k + 1) * P)
                nc.tensor.transpose(out[:, 0:NE], raw_g[:, cols], mem.ident[:NE, :NE])
                nc.tensor.transpose(out[:, NE:NE + P], raw_a[:, 0, cols], mem.ident[:, :])
                nc.tensor.transpose(out[:, NE + P:LW], raw_a[:R_OF[1], 1, cols], mem.ident[:R_OF[1], :R_OF[1]]
                                    ).then_inc(a_turned, 1)
            pe.wait_ge(w_in, 16)
            for n, (m, k) in enumerate(mats):
                if m == "b" and k == 0:
                    pe.wait_ge(b_in, 16 * KT)
                if n >= 2:
                    pe.wait_ge(w_gated, n - 1)
                out = mem.bank[2 + n % 2]
                for c in range(KT):
                    if m == "w":
                        last = nc.tensor.transpose(out[:, c * P:(c + 1) * P], raw[:, c, k * P:(k + 1) * P], mem.ident[:, :])
                    else:
                        rows = raw_b[:, c, :, :].rearrange("p e r -> p (e r)")[:, k * P:k * P + R_OF[k]]
                        last = nc.tensor.transpose(out[:R_OF[k], c * P:(c + 1) * P], rows, mem.ident[:, :])
                last.then_inc(w_turned, 1)
            pe.wait_ge(a_split, KT)

            def low(t):
                if t >= 2:
                    pe.wait_ge(logits_out, t - 1)
                for k in range(KT):
                    last = split_products(nc.tensor, mem.bank[t % 2][:, 0:LW], [a[:, k, t * P:(t + 1) * P] for a in mem.hT],
                                          [a[:, k, :] for a in aT], k == 0, k == KT - 1)
                last.then_inc(logits_done, 1)

            for t in range(NT):
                low(t)
            pe.wait_ge(w_split, len(mats))
            for t in range(NT):
                out = mem.bank[6 + t % 2]
                if t >= 2:
                    pe.wait_ge(added, t - 1)
                for k in range(KT):
                    split_products(nc.tensor, out[:, :], [a[:, k, t * P:(t + 1) * P] for a in mem.hT],
                                   [a[:, k, :] for a in wT], k == 0, False)
                pe.wait_ge(scaled_done, t + 1)
                if t >= 2:
                    pe.wait_ge(s_split, t - 1)
                for r in range(RT):
                    last = nc.tensor.transpose(mem.bank[4 + t % 2][:R_OF[r], r * P:(r + 1) * P],
                                               scaled[:, t % 2, r * P:r * P + R_OF[r]], mem.ident[:, :])
                last.then_inc(s_turned, 1)
                pe.wait_ge(s_split, t + 1)
                for r in range(RT):
                    n = R_OF[r]
                    last = split_products(nc.tensor, out[:, :], [a[:n, t % 2, r, :] for a in sT],
                                          [a[:n, r, :] for a in bT], False, r == RT - 1)
                last.then_inc(produced, 1)

        @block.scalar
        def _(act):
            for k in range(KT):
                act.wait_ge(a_turned, k + 1)
                nc.scalar.copy(aT[0][:, k, :], mem.bank[k % 2][:, 0:LW]).then_inc(a_hi, 1)
            for n, (m, k) in enumerate(mats):
                act.wait_ge(w_gated, n + 1)
                rows = P if m == "w" else R_OF[k]
                nc.scalar.copy((wT if m == "w" else bT)[0][:rows, k, :], gated[:rows, n % 2, :]).then_inc(w_hi, 1)
            act.wait_ge(gapped, 1)
            nc.scalar.activation(exped[:, :], gap[:, :], ACT.Exp).then_inc(exp_done, 1)
            for t in range(NT):
                act.wait_ge(s_turned, t + 1)
                for r in range(RT):
                    last = nc.scalar.copy(sT[0][:R_OF[r], t % 2, r, :], mem.bank[4 + t % 2][:R_OF[r], r * P:(r + 1) * P])
                last.then_inc(s_hi, 1)

        @block.vector
        def _(dve):
            steps = [0]

            def link(instruction):
                steps[0] += 1
                instruction.then_inc(step, 1)
                dve.wait_ge(step, steps[0])

            for k in range(KT):
                dve.wait_ge(a_hi, k + 1)
                nc.vector.tensor_tensor(aT[1][:, k, :], mem.bank[k % 2][:, 0:LW], aT[0][:, k, :].bitcast(F32),
                                        ALU.subtract).then_inc(a_split, 1)
            for n, (m, k) in enumerate(mats):
                rows = P if m == "w" else R_OF[k]
                dve.wait_ge(w_turned, n + 1)
                nc.vector.tensor_tensor(gated[:rows, n % 2, :], mem.bank[2 + n % 2][:rows, :], mem.gate[:rows, 3, :],
                                        ALU.mult).then_inc(w_gated, 1)
                out = (wT if m == "w" else bT)
                dve.wait_ge(w_hi, n + 1)
                nc.vector.tensor_tensor(out[1][:rows, k, :], gated[:rows, n % 2, :], out[0][:rows, k, :].bitcast(F32),
                                        ALU.subtract).then_inc(w_split, 1)
                dve.wait_ge(w_split, n + 1)
            dve.wait_ge(counted, 1)
            link(nc.vector.tensor_copy(numberf[:, :], number[:, :]))
            for t in range(NT):
                dve.wait_ge(logits_done, t + 1)
                nc.vector.tensor_copy(low_all[:, t, :], mem.bank[t % 2][:, 0:LW]).then_inc(logits_out, 1)
                dve.wait_ge(logits_out, t + 1)
                nc.vector.max(top[:, t, :], low_all[:, t, 0:NE]).then_inc(topped, 1)
                dve.wait_ge(topped, t + 1)
                nc.vector.max_index(index[:, t, :], top[:, t, :], low_all[:, t, 0:NE]).then_inc(indexed, 1)
            dve.wait_ge(indexed, NT)
            link(nc.vector.tensor_copy(indexf[:, :, :], index[:, :, 0:2]))
            nc.vector.tensor_tensor(gap[:, :], top[:, :, 1], top[:, :, 0], ALU.subtract).then_inc(gapped, 1)
            dve.wait_ge(exp_done, 1)
            link(nc.vector.tensor_scalar(gap[:, :], exped[:, :], 1.0, None, ALU.add))
            link(nc.vector.reciprocal(prob[:, :, 0], gap[:, :]))
            link(nc.vector.tensor_scalar(prob[:, :, 0], prob[:, :, 0], LORA_SCALE, None, ALU.mult))
            link(nc.vector.tensor_tensor(prob[:, :, 1], prob[:, :, 0], exped[:, :], ALU.mult))
            for t in range(NT):
                for n in range(2):
                    last = nc.vector.tensor_scalar(chosen[:, n, :], numberf[:, :], indexf[:, t, n:n + 1],
                                                   prob[:, t, n:n + 1], ALU.is_equal, ALU.mult)
                link(last)
                link(nc.vector.tensor_tensor(mix[:, :], chosen[:, 0, :], chosen[:, 1, :], ALU.add))
                if t >= 2:
                    dve.wait_ge(s_turned, t - 1)
                nc.vector.tensor_tensor(scaled[:, t % 2, :].rearrange("p (e r) -> p e r", e=NE),
                                        low_all[:, t, NE:LW].rearrange("p (e r) -> p e r", e=NE),
                                        mix[:, :].unsqueeze(2).broadcast_to([P, NE, RANK1]), ALU.mult
                                        ).then_inc(scaled_done, 1)
                dve.wait_ge(scaled_done, t + 1)
                dve.wait_ge(s_hi, t + 1)
                for r in range(RT):
                    n = R_OF[r]
                    last = nc.vector.tensor_tensor(sT[1][:n, t % 2, r, :], mem.bank[4 + t % 2][:n, r * P:(r + 1) * P],
                                                   sT[0][:n, t % 2, r, :].bitcast(F32), ALU.subtract)
                last.then_inc(s_split, 1)
                dve.wait_ge(produced, t + 1)
                nc.vector.tensor_tensor(mem.x[:, t, :], mem.bank[6 + t % 2][:, :], mem.x[:, t, :], ALU.add
                                        ).then_inc(added, 1)


def program(nc, ins, out, rope0, rope1):
    with ExitStack() as ctx:
        sb = lambda name, shape, dt=F32: ctx.enter_context(nc.sbuf_tensor(name, shape, dt))
        mem = Memory()
        mem.semaphores = ctx
        mem.ident, mem.ident_bf = sb("ident", [P, P]), sb("ident_bf", [P, P], BF16)
        mem.causal, mem.ones = sb("causal", [P, P], BF16), sb("ones", [P, P])
        mem.x = sb("x", [P, NT, D])
        mem.hT = (sb("hT_hi", [P, KT, S], F32R), sb("hT_lo", [P, KT, S], F32R))
        mem.gate, mem.column = sb("gate", [P, 4, D]), sb("column", [P, 8, KT])
        psum = ctx.enter_context(nc.psum_tensor("psum", [P, 8, HALF], F32))
        mem.bank = [psum[:, b, :] for b in range(8)]
        mem.bank_pair = [psum[:, 2 * s:2 * s + 2, :].rearrange("p b n -> p (b n)") for s in range(2)]
        mem.bank_pair4 = lambda m: psum[:, 4 + 2 * m:6 + 2 * m, :].rearrange("p b n -> p (b n)")
        mem.layernorm_counts = layernorm_counts(nc, mem)
        constants_phase(nc, mem)
        modulation_phase(nc, mem, ins["L0_attn_hidden_states"], (ins["L0_c"], ins["L1_c"]),
                         (ins["L0_wmod"], ins["L1_wmod"]))
        layernorm_phase(nc, mem, 0, mem.column[:, 1, :], mem.column[:, 0, :])
        layer0_attention_phase(nc, mem, rope0, {w: ins["L0_attn_qw_" + w] for w in "qkvo"},
                               {w: ins["L0_attn_scales_" + w] for w in "qkvo"})
        layernorm_phase(nc, mem, 1, mem.column[:, 3, :], mem.column[:, 2, :])
        layer0_ffn_phase(nc, mem, {n: ins["L0_ffn_" + n] for n in
                                   ("gate_w", "up_w", "down_w", "gate_a", "gate_b", "up_a", "up_b", "down_a", "down_b")})
        layernorm_phase(nc, mem, 2, mem.column[:, 5, :], mem.column[:, 4, :])
        with ExitStack() as attention:
            sb1 = lambda name, shape, dt=F32: attention.enter_context(nc.sbuf_tensor(name, shape, dt))
            k1 = (sb1("k1_hi", [P, NT, NKV1 * HD1], F32R), sb1("k1_lo", [P, NT, NKV1 * HD1], F32R))
            v1, attended = sb1("v1", [P, NT, NKV1 * HD1]), sb1("attended", [P, NT, D])
            layer1_qkv_phase(nc, mem, k1, v1, rope1, ins["L1_attn_w_qkv"], ins["L1_attn_b_qkv"])
            layer1_attention_phase(nc, mem, k1, v1, attended)
            layer1_output_phase(nc, mem, attended, ins["L1_attn_w_o"], ins["L1_attn_b_o"])
        layernorm_phase(nc, mem, 3, mem.column[:, 7, :], mem.column[:, 6, :])
        layer1_experts_phase(nc, mem, out, {"base": ins["L1_ffn_base_W"], "gate": ins["L1_ffn_gate_W"],
                                            "a": ins["L1_ffn_lora_A"], "b": ins["L1_ffn_lora_B"]})


_INS = [
    "L0_attn_hidden_states", "L0_attn_scales_q", "L0_attn_scales_k", "L0_attn_scales_v", "L0_attn_scales_o",
    "L0_attn_qw_q", "L0_attn_qw_k", "L0_attn_qw_v", "L0_attn_qw_o", "L0_ffn_gate_w", "L0_ffn_up_w", "L0_ffn_down_w",
    "L0_ffn_gate_a", "L0_ffn_gate_b", "L0_ffn_up_a", "L0_ffn_up_b", "L0_ffn_down_a", "L0_ffn_down_b", "L0_c", "L0_wmod",
    "L1_attn_w_qkv", "L1_attn_b_qkv", "L1_attn_w_o", "L1_attn_b_o", "L1_ffn_base_W", "L1_ffn_gate_W", "L1_ffn_lora_A",
    "L1_ffn_lora_B", "L1_c", "L1_wmod",
]


def _rope_tables():
    import numpy as np

    def angles(width):
        inverse = np.float32(1) / np.float32(10000) ** (np.arange(0, width, 2, dtype=np.float32) / np.float32(width))
        return np.arange(S, dtype=np.float32)[:, None] * inverse[None, :]

    a0, a1 = angles(HD0), angles(HD1)
    cos0, sin0 = np.cos(a0).T, np.sin(a0).T
    return (np.stack([np.concatenate([cos0, cos0]), np.concatenate([-sin0, sin0])]).astype(np.float32),
            np.stack([np.cos(a1), np.sin(a1)], axis=1).astype(np.float32))


def kernel(**inputs):
    import numpy as np
    import concourse.bacc as bacc
    from concourse.bass_utils import run_bass_kernel_spmd

    nc = bacc.Bacc("TRN2", target_bir_lowering=False, num_devices=1)
    rope0, rope1 = _rope_tables()
    arrays = {f"in_{name}": np.ascontiguousarray(inputs[name]) for name in _INS}
    arrays["rope0"], arrays["rope1"] = rope0, rope1
    aps = {name: nc.dram_tensor(name, a.shape, mybir.dt.from_np(a.dtype), kind="ExternalInput").ap()
           for name, a in arrays.items()}
    out = nc.dram_tensor("out", (1, S, D), F32, kind="ExternalOutput").ap()
    program(nc, {name: aps[f"in_{name}"] for name in _INS}, out, aps["rope0"], aps["rope1"])
    result = run_bass_kernel_spmd(nc, [arrays], core_ids=[0])
    return result.results[0]["out"]
```
